# Optimizing a Trainium2 kernel written in Bass

```python
import numpy as np
import jax
import jax.numpy as jnp

def _softmax(x, axis=-1):
    return jax.nn.softmax(x, axis=axis)

def _gelu(x):
    return jax.nn.gelu(x, approximate=True)

def _silu(x):
    return jax.nn.silu(x)

def _sigmoid(x):
    return jax.nn.sigmoid(x)

def _layernorm(x, axis=-1, eps=1e-05):
    m = jnp.mean(x, axis=axis, keepdims=True)
    v = jnp.var(x, axis=axis, keepdims=True)
    return (x - m) / jnp.sqrt(v + eps)

def _scatter_add(tgt, idx, src, axis=0):
    return tgt.at[idx].add(src)

def _segment_sum(src, seg, n):
    return jax.ops.segment_sum(src, seg, n)
kernel_name = 'mk_gnn_resnorm_d4_gnn_r8_02e40a'

def setup_inputs(seed: int=0):
    np.random.seed(seed)
    _w = jnp.asarray

    def _rec_inputs():
        import jax
        import jax.numpy as jnp
        _gk = jax.random.key(seed)
        x = -0.0009044 + 1 * jax.random.normal(jax.random.fold_in(_gk, 1), (6250, 160), jnp.float32)
        _s = jax.random.randint(jax.random.fold_in(_gk, 2), (100000,), 0, 6250, jnp.int32)
        _d = jax.random.randint(jax.random.fold_in(_gk, 3), (100000,), 0, 6250, jnp.int32)
        _loop = jnp.arange(6250, dtype=jnp.int32)
        src = jnp.concatenate([_s, _d, _loop])
        dst = jnp.concatenate([_d, _s, _loop])
        _o = jnp.argsort(dst, stable=True)
        src = src[_o]
        dst = dst[_o]
        edge_attr_16 = jax.random.uniform(jax.random.fold_in(_gk, 11), (206250, 16), jnp.float32, 0.0, 1)
        edge_attr_3 = 0.00047201 + 1.00023 * jax.random.normal(jax.random.fold_in(_gk, 12), (206250, 3), jnp.float32)
        edge_attr_4 = 0.000898722 + 1.00012 * jax.random.normal(jax.random.fold_in(_gk, 13), (206250, 4), jnp.float32)
        edge_attr_64 = 0.000279952 + 1.00013 * jax.random.normal(jax.random.fold_in(_gk, 14), (206250, 64), jnp.float32)
        node_vec1 = -0.00915711 + 0.999674 * jax.random.normal(jax.random.fold_in(_gk, 16), (6250, 1), jnp.float32)
        return (x, src, dst, edge_attr_16, edge_attr_3, edge_attr_4, edge_attr_64, node_vec1)
    x, src, dst, edge_attr_16, edge_attr_3, edge_attr_4, edge_attr_64, node_vec1 = _rec_inputs()

    def _L0_gnn_setup():
        import jax, jax.numpy as jnp
        import numpy as np
        N_NODES = 1250
        N_EDGES = 40000
        MUL0, MUL1 = (64, 32)
        EDGE_DIM = 64
        W_NUMEL = 224
        DENOM = 32.0
        SQRT3 = 3.0 ** 0.5
        INV_SQRT3 = 1.0 / SQRT3
        INV_SQRT2 = 2.0 ** (-0.5)

        def _forward(node_feature, edge_attr, edge_feature, W_skip0, W_skip1, W_nl0, W_nl1, W_fc1, W_fc2, W_out_s, W_out_v, edge_index):
            N = node_feature.shape[0]
            E = edge_attr.shape[0]
            s = node_feature[:, :MUL0]
            v = node_feature[:, MUL0:].reshape(N, MUL1, 3)
            skip_s = s @ W_skip0
            skip_v = jnp.einsum('nmi,mk->nki', v, W_skip1)
            s = s @ W_nl0
            v = jnp.einsum('nmi,mk->nki', v, W_nl1)
            rhat = edge_attr / jnp.linalg.norm(edge_attr, axis=-1, keepdims=True)
            sh1 = SQRT3 * rhat
            w = jax.nn.relu(edge_feature @ W_fc1) @ W_fc2
            w0, w1, w2, w3, w4 = jnp.split(w, [64, 128, 160, 192], axis=-1)
            src, dst = (edge_index[0], edge_index[1])
            xs = s[dst]
            xv = v[dst]
            out0a = w0 * xs
            out0b = w3 * (jnp.einsum('emi,ei->em', xv, sh1) * INV_SQRT3)
            out1a = (w1 * xs)[:, :, None] * sh1[:, None, :]
            out1b = w2[:, :, None] * xv
            out1c = w4[:, :, None] * (jnp.cross(xv, sh1[:, None, :]) * INV_SQRT2)
            tp = jnp.concatenate([out0a, out0b, out1a.reshape(E, -1), out1b.reshape(E, -1), out1c.reshape(E, -1)], axis=-1)
            agg = jax.ops.segment_sum(tp, src, num_segments=N) / DENOM
            agg_s = agg[:, :96]
            agg_v = agg[:, 96:].reshape(N, 128, 3)
            out_s = agg_s @ W_out_s + skip_s
            out_v = jnp.einsum('nmi,mk->nki', agg_v, W_out_v) + skip_v
            fs = jax.nn.silu(out_s[:, :MUL0])
            gate = jax.nn.sigmoid(out_s[:, MUL0:MUL0 + 32])
            gv = gate[:, :, None] * out_v
            return jnp.concatenate([fs, gv.reshape(N, -1)], axis=-1)
        key = jax.random.key(seed)
        ks = jax.random.split(key, 12)

        def lin(k, fi, fo):
            return jax.random.normal(k, (fi, fo), jnp.float32) / np.float32(np.sqrt(fi))
        return {'node_feature': jax.random.normal(ks[0], (N_NODES, MUL0 + 3 * MUL1), jnp.float32), 'edge_attr': jax.random.normal(ks[1], (N_EDGES, 3), jnp.float32), 'edge_feature': jax.random.normal(ks[2], (N_EDGES, EDGE_DIM), jnp.float32), 'W_skip0': lin(ks[3], MUL0, 96), 'W_skip1': lin(ks[4], MUL1, 32), 'W_nl0': lin(ks[5], MUL0, MUL0), 'W_nl1': lin(ks[6], MUL1, MUL1), 'W_fc1': lin(ks[7], EDGE_DIM, 64), 'W_fc2': lin(ks[8], 64, W_NUMEL), 'W_out_s': lin(ks[9], 96, 96), 'W_out_v': lin(ks[10], 128, 32), 'edge_index': jax.random.randint(ks[11], (2, N_EDGES), 0, N_NODES)}
    _L0_gnn_all = _L0_gnn_setup()
    _L0_gnn_in = {k: v for k, v in _L0_gnn_all.items() if k in ('W_skip0', 'W_skip1', 'W_nl0', 'W_nl1', 'W_fc1', 'W_fc2', 'W_out_s', 'W_out_v')}
    del _L0_gnn_all

    def _L1_gnn_setup():
        import jax, jax.numpy as jnp
        import numpy as np
        N, E = (2500, 40000)
        CS, CV = (64, 32)
        AS_, AV, H = (16, 8, 4)
        NB = 16
        SQRT3 = 1.7320508075688772
        SQRT2 = 1.4142135623730951
        EPS = 1e-05

        def _cg_tp(s, v, y0, y1, w_ss, w_sv, w_vs, w_vv0, w_vv1):
            out_s = jnp.concatenate([w_ss * s * y0[:, None], w_vv0 * (jnp.einsum('eci,ei->ec', v, y1) / SQRT3)], axis=-1)
            out_v = jnp.concatenate([(w_sv * s)[:, :, None] * y1[:, None, :], (w_vs * jnp.ones_like(v[..., 0]))[..., None] * v * y0[:, None, None], (w_vv1 * jnp.ones_like(v[..., 0]))[..., None] * (jnp.cross(v, y1[:, None, :]) / SQRT2)], axis=1)
            return (out_s, out_v)

        def _equiv_layernorm(s, v, gamma_s, beta_s, gamma_v):
            mu = jnp.mean(s, axis=-1, keepdims=True)
            var = jnp.var(s, axis=-1, keepdims=True)
            s_n = (s - mu) * jax.lax.rsqrt(var + EPS) * gamma_s + beta_s
            rms = jnp.sqrt(jnp.mean(jnp.sum(v * v, axis=-1), axis=-1, keepdims=True) + EPS)
            v_n = v / rms[..., None] * gamma_v[None, :, None]
            return (s_n, v_n)
        key = jax.random.key(seed)
        ks = jax.random.split(key, 26)

        def rn(k, shape, fan):
            return jax.random.normal(k, shape, jnp.float32) / np.sqrt(fan)
        D1S, D1V = (CS + CV, CS + 2 * CV)
        WN = 2 * CS + 3 * CV
        inp = {'node': jax.random.normal(ks[0], (N, CS + 3 * CV), jnp.float32), 'edge_index': jax.random.randint(ks[1], (2, E), 0, N, jnp.int64 if jax.config.jax_enable_x64 else jnp.int32), 'rbf': jax.random.uniform(ks[2], (E, NB), jnp.float32), 'rsh': jax.random.normal(ks[3], (E, 4), jnp.float32), 'gamma_s': jnp.ones((CS,), jnp.float32), 'beta_s': jnp.zeros((CS,), jnp.float32), 'gamma_v': jnp.ones((CV,), jnp.float32), 'Ws_src': rn(ks[4], (CS, CS), CS), 'Wv_src': rn(ks[5], (CV, CV), CV), 'Ws_dst': rn(ks[6], (CS, CS), CS), 'Wv_dst': rn(ks[7], (CV, CV), CV), 'W_rbf': rn(ks[8], (NB, WN), NB), 'W_alpha': rn(ks[9], (D1S, H * AS_), D1S), 'alpha_dot': rn(ks[10], (1, H, AS_), AS_), 'Ws_val': rn(ks[11], (D1S, CS), D1S), 'Wv_val': rn(ks[12], (D1V, CV), D1V), 'Wg': rn(ks[13], (CS, CV), CS), 'w2_ss': rn(ks[14], (CS,), 1), 'w2_sv': rn(ks[15], (CS,), 1), 'w2_vs': rn(ks[16], (CV,), 1), 'w2_vv0': rn(ks[17], (CV,), 1), 'w2_vv1': rn(ks[18], (CV,), 1), 'Ws_vlin': rn(ks[19], (D1S, H * AS_), D1S), 'Wv_vlin': rn(ks[20], (D1V, H * AV), D1V), 'Wps': rn(ks[21], (H * AS_, CS), H * AS_), 'Wpv': rn(ks[22], (H * AV, CV), H * AV)}
        return inp
    _L1_gnn_all = _L1_gnn_setup()
    _L1_gnn_in = {k: v for k, v in _L1_gnn_all.items() if k in ('gamma_s', 'beta_s', 'gamma_v', 'Ws_src', 'Wv_src', 'Ws_dst', 'Wv_dst', 'W_rbf', 'W_alpha', 'alpha_dot', 'Ws_val', 'Wv_val', 'Wg', 'w2_ss', 'w2_sv', 'w2_vs', 'w2_vv0', 'w2_vv1', 'Ws_vlin', 'Wv_vlin', 'Wps', 'Wpv')}
    del _L1_gnn_all

    def _L2_gnn_setup():
        import jax, jax.numpy as jnp
        import numpy as np
        MUL0, MUL1 = (64, 32)
        INV_SQRT3 = 1.0 / np.sqrt(3.0)

        def _split(x):
            return (x[:, :MUL0], x[:, MUL0:].reshape(x.shape[0], MUL1, 3))

        def _merge(o0, o1):
            return jnp.concatenate([o0, o1.reshape(o1.shape[0], -1)], axis=-1)

        def _tp(x0, x1, y0, y1, w000, w011, w101, w110):
            fan0 = x0.shape[1] * y0.shape[1] + x1.shape[1] * y1.shape[1]
            fan1 = x0.shape[1] * y1.shape[1] + x1.shape[1] * y0.shape[1]
            out0 = (jnp.einsum('eu,ev,uvw->ew', x0, y0, w000) + INV_SQRT3 * jnp.einsum('euk,evk,uvw->ew', x1, y1, w110)) / np.sqrt(fan0)
            out1 = (jnp.einsum('eu,evk,uvw->ewk', x0, y1, w011) + jnp.einsum('euk,ev,uvw->ewk', x1, y0, w101)) / np.sqrt(fan1)
            return (out0, out1)

        def _lin(x0, x1, w0, w1):
            return (x0 @ w0 / np.sqrt(x0.shape[1]), jnp.einsum('euk,uv->evk', x1, w1) / np.sqrt(x1.shape[1]))
        key = jax.random.key(seed)
        ks = jax.random.split(key, 20)
        N, E = (6250, 62500)
        inp = {'node_features': jax.random.normal(ks[0], (N, MUL0 + 3 * MUL1), dtype=jnp.float32), 'edge_index': jax.random.randint(ks[1], (2, E), 0, N, dtype=jnp.int64), 'edge_attr_tensor': jax.random.normal(ks[2], (E, 4), dtype=jnp.float32), 'node_attr_scalar_raw': jax.random.normal(ks[3], (N, 1), dtype=jnp.float32), 'wm000': jax.random.normal(ks[4], (MUL0, 1, MUL0), dtype=jnp.float32), 'wm011': jax.random.normal(ks[5], (MUL0, 1, MUL1), dtype=jnp.float32), 'wm101': jax.random.normal(ks[6], (MUL1, 1, MUL1), dtype=jnp.float32), 'wm110': jax.random.normal(ks[7], (MUL1, 1, MUL0), dtype=jnp.float32), 'lm0': jax.random.normal(ks[8], (MUL0, MUL0), dtype=jnp.float32), 'lm1': jax.random.normal(ks[9], (MUL1, MUL1), dtype=jnp.float32), 'wu000': jax.random.normal(ks[10], (MUL0, MUL0, MUL0), dtype=jnp.float32), 'wu011': jax.random.normal(ks[11], (MUL0, MUL1, MUL1), dtype=jnp.float32), 'wu101': jax.random.normal(ks[12], (MUL1, MUL0, MUL1), dtype=jnp.float32), 'wu110': jax.random.normal(ks[13], (MUL1, MUL1, MUL0), dtype=jnp.float32), 'lu0': jax.random.normal(ks[14], (MUL0, MUL0), dtype=jnp.float32), 'lu1': jax.random.normal(ks[15], (MUL1, MUL1), dtype=jnp.float32)}
        return inp
    _L2_gnn_all = _L2_gnn_setup()
    _L2_gnn_in = {k: v for k, v in _L2_gnn_all.items() if k in ('wm000', 'wm011', 'wm101', 'wm110', 'lm0', 'lm1', 'wu000', 'wu011', 'wu101', 'wu110', 'lu0', 'lu1')}
    del _L2_gnn_all

    def _L3_gnn_setup():
        import jax, jax.numpy as jnp
        import numpy as np
        N = 2500
        E = 80000
        INV_SQRT3 = 0.5773502691896258
        INV8 = 0.125
        INV_SQRT32 = 0.17677669529663687
        INV64 = 0.015625
        INV32 = 0.03125
        INV_SQRT2048 = 0.022097086912079608
        key = jax.random.key(seed)
        ks = jax.random.split(key, 16)
        f32 = jnp.float32
        return {'node_features': jax.random.normal(ks[0], (N, 160), f32), 'edge_index': jax.random.randint(ks[1], (2, E), 0, N), 'edge_attr_tensor': jax.random.normal(ks[2], (E, 4), f32), 'node_attr_scalar_raw': jax.random.normal(ks[3], (N, 1), f32), 'Wm_ss': jax.random.normal(ks[4], (64, 64), f32), 'Wm_vv': jax.random.normal(ks[5], (32, 64), f32), 'Wm_sv': jax.random.normal(ks[6], (64, 32), f32), 'Wm_vs': jax.random.normal(ks[7], (32, 32), f32), 'Lm_s': jax.random.normal(ks[8], (64, 64), f32), 'Lm_v': jax.random.normal(ks[9], (32, 32), f32), 'Wu_ss': jax.random.normal(ks[10], (64, 64, 64), f32), 'Wu_vv': jax.random.normal(ks[11], (32, 32, 64), f32), 'Wu_sv': jax.random.normal(ks[12], (64, 32, 32), f32), 'Wu_vs': jax.random.normal(ks[13], (32, 64, 32), f32), 'Lu_s': jax.random.normal(ks[14], (64, 64), f32), 'Lu_v': jax.random.normal(ks[15], (32, 32), f32)}
    _L3_gnn_all = _L3_gnn_setup()
    _L3_gnn_in = {k: v for k, v in _L3_gnn_all.items() if k in ('Wm_ss', 'Wm_vv', 'Wm_sv', 'Wm_vs', 'Lm_s', 'Lm_v', 'Wu_ss', 'Wu_vv', 'Wu_sv', 'Wu_vs', 'Lu_s', 'Lu_v')}
    del _L3_gnn_all
    return {'x': x, 'src': src, 'dst': dst, 'edge_attr_16': edge_attr_16, 'edge_attr_3': edge_attr_3, 'edge_attr_4': edge_attr_4, 'edge_attr_64': edge_attr_64, 'node_vec1': node_vec1, 'L0_gnn_W_skip0': _L0_gnn_in['W_skip0'], 'L0_gnn_W_skip1': _L0_gnn_in['W_skip1'], 'L0_gnn_W_nl0': _L0_gnn_in['W_nl0'], 'L0_gnn_W_nl1': _L0_gnn_in['W_nl1'], 'L0_gnn_W_fc1': _L0_gnn_in['W_fc1'], 'L0_gnn_W_fc2': _L0_gnn_in['W_fc2'], 'L0_gnn_W_out_s': _L0_gnn_in['W_out_s'], 'L0_gnn_W_out_v': _L0_gnn_in['W_out_v'], 'L1_gnn_gamma_s': _L1_gnn_in['gamma_s'], 'L1_gnn_beta_s': _L1_gnn_in['beta_s'], 'L1_gnn_gamma_v': _L1_gnn_in['gamma_v'], 'L1_gnn_Ws_src': _L1_gnn_in['Ws_src'], 'L1_gnn_Wv_src': _L1_gnn_in['Wv_src'], 'L1_gnn_Ws_dst': _L1_gnn_in['Ws_dst'], 'L1_gnn_Wv_dst': _L1_gnn_in['Wv_dst'], 'L1_gnn_W_rbf': _L1_gnn_in['W_rbf'], 'L1_gnn_W_alpha': _L1_gnn_in['W_alpha'], 'L1_gnn_alpha_dot': _L1_gnn_in['alpha_dot'], 'L1_gnn_Ws_val': _L1_gnn_in['Ws_val'], 'L1_gnn_Wv_val': _L1_gnn_in['Wv_val'], 'L1_gnn_Wg': _L1_gnn_in['Wg'], 'L1_gnn_w2_ss': _L1_gnn_in['w2_ss'], 'L1_gnn_w2_sv': _L1_gnn_in['w2_sv'], 'L1_gnn_w2_vs': _L1_gnn_in['w2_vs'], 'L1_gnn_w2_vv0': _L1_gnn_in['w2_vv0'], 'L1_gnn_w2_vv1': _L1_gnn_in['w2_vv1'], 'L1_gnn_Ws_vlin': _L1_gnn_in['Ws_vlin'], 'L1_gnn_Wv_vlin': _L1_gnn_in['Wv_vlin'], 'L1_gnn_Wps': _L1_gnn_in['Wps'], 'L1_gnn_Wpv': _L1_gnn_in['Wpv'], 'L2_gnn_wm000': _L2_gnn_in['wm000'], 'L2_gnn_wm011': _L2_gnn_in['wm011'], 'L2_gnn_wm101': _L2_gnn_in['wm101'], 'L2_gnn_wm110': _L2_gnn_in['wm110'], 'L2_gnn_lm0': _L2_gnn_in['lm0'], 'L2_gnn_lm1': _L2_gnn_in['lm1'], 'L2_gnn_wu000': _L2_gnn_in['wu000'], 'L2_gnn_wu011': _L2_gnn_in['wu011'], 'L2_gnn_wu101': _L2_gnn_in['wu101'], 'L2_gnn_wu110': _L2_gnn_in['wu110'], 'L2_gnn_lu0': _L2_gnn_in['lu0'], 'L2_gnn_lu1': _L2_gnn_in['lu1'], 'L3_gnn_Wm_ss': _L3_gnn_in['Wm_ss'], 'L3_gnn_Wm_vv': _L3_gnn_in['Wm_vv'], 'L3_gnn_Wm_sv': _L3_gnn_in['Wm_sv'], 'L3_gnn_Wm_vs': _L3_gnn_in['Wm_vs'], 'L3_gnn_Lm_s': _L3_gnn_in['Lm_s'], 'L3_gnn_Lm_v': _L3_gnn_in['Lm_v'], 'L3_gnn_Wu_ss': _L3_gnn_in['Wu_ss'], 'L3_gnn_Wu_vv': _L3_gnn_in['Wu_vv'], 'L3_gnn_Wu_sv': _L3_gnn_in['Wu_sv'], 'L3_gnn_Wu_vs': _L3_gnn_in['Wu_vs'], 'L3_gnn_Lu_s': _L3_gnn_in['Lu_s'], 'L3_gnn_Lu_v': _L3_gnn_in['Lu_v']}

def reference(x, src, dst, edge_attr_16, edge_attr_3, edge_attr_4, edge_attr_64, node_vec1, L0_gnn_W_skip0, L0_gnn_W_skip1, L0_gnn_W_nl0, L0_gnn_W_nl1, L0_gnn_W_fc1, L0_gnn_W_fc2, L0_gnn_W_out_s, L0_gnn_W_out_v, L1_gnn_gamma_s, L1_gnn_beta_s, L1_gnn_gamma_v, L1_gnn_Ws_src, L1_gnn_Wv_src, L1_gnn_Ws_dst, L1_gnn_Wv_dst, L1_gnn_W_rbf, L1_gnn_W_alpha, L1_gnn_alpha_dot, L1_gnn_Ws_val, L1_gnn_Wv_val, L1_gnn_Wg, L1_gnn_w2_ss, L1_gnn_w2_sv, L1_gnn_w2_vs, L1_gnn_w2_vv0, L1_gnn_w2_vv1, L1_gnn_Ws_vlin, L1_gnn_Wv_vlin, L1_gnn_Wps, L1_gnn_Wpv, L2_gnn_wm000, L2_gnn_wm011, L2_gnn_wm101, L2_gnn_wm110, L2_gnn_lm0, L2_gnn_lm1, L2_gnn_wu000, L2_gnn_wu011, L2_gnn_wu101, L2_gnn_wu110, L2_gnn_lu0, L2_gnn_lu1, L3_gnn_Wm_ss, L3_gnn_Wm_vv, L3_gnn_Wm_sv, L3_gnn_Wm_vs, L3_gnn_Lm_s, L3_gnn_Lm_v, L3_gnn_Wu_ss, L3_gnn_Wu_vv, L3_gnn_Wu_sv, L3_gnn_Wu_vs, L3_gnn_Lu_s, L3_gnn_Lu_v):
    import jax
    import jax.numpy as jnp

    def _L0_gnn_ref(node_feature, edge_attr, edge_feature, W_skip0, W_skip1, W_nl0, W_nl1, W_fc1, W_fc2, W_out_s, W_out_v, edge_index):
        import jax, jax.numpy as jnp
        import numpy as np
        N_NODES = 1250
        N_EDGES = 40000
        MUL0, MUL1 = (64, 32)
        EDGE_DIM = 64
        W_NUMEL = 224
        DENOM = 32.0
        SQRT3 = 3.0 ** 0.5
        INV_SQRT3 = 1.0 / SQRT3
        INV_SQRT2 = 2.0 ** (-0.5)

        def _forward(node_feature, edge_attr, edge_feature, W_skip0, W_skip1, W_nl0, W_nl1, W_fc1, W_fc2, W_out_s, W_out_v, edge_index):
            N = node_feature.shape[0]
            E = edge_attr.shape[0]
            s = node_feature[:, :MUL0]
            v = node_feature[:, MUL0:].reshape(N, MUL1, 3)
            skip_s = s @ W_skip0
            skip_v = jnp.einsum('nmi,mk->nki', v, W_skip1)
            s = s @ W_nl0
            v = jnp.einsum('nmi,mk->nki', v, W_nl1)
            rhat = edge_attr / jnp.linalg.norm(edge_attr, axis=-1, keepdims=True)
            sh1 = SQRT3 * rhat
            w = jax.nn.relu(edge_feature @ W_fc1) @ W_fc2
            w0, w1, w2, w3, w4 = jnp.split(w, [64, 128, 160, 192], axis=-1)
            src, dst = (edge_index[0], edge_index[1])
            xs = s[dst]
            xv = v[dst]
            out0a = w0 * xs
            out0b = w3 * (jnp.einsum('emi,ei->em', xv, sh1) * INV_SQRT3)
            out1a = (w1 * xs)[:, :, None] * sh1[:, None, :]
            out1b = w2[:, :, None] * xv
            out1c = w4[:, :, None] * (jnp.cross(xv, sh1[:, None, :]) * INV_SQRT2)
            tp = jnp.concatenate([out0a, out0b, out1a.reshape(E, -1), out1b.reshape(E, -1), out1c.reshape(E, -1)], axis=-1)
            agg = jax.ops.segment_sum(tp, src, num_segments=N) / DENOM
            agg_s = agg[:, :96]
            agg_v = agg[:, 96:].reshape(N, 128, 3)
            out_s = agg_s @ W_out_s + skip_s
            out_v = jnp.einsum('nmi,mk->nki', agg_v, W_out_v) + skip_v
            fs = jax.nn.silu(out_s[:, :MUL0])
            gate = jax.nn.sigmoid(out_s[:, MUL0:MUL0 + 32])
            gv = gate[:, :, None] * out_v
            return jnp.concatenate([fs, gv.reshape(N, -1)], axis=-1)
        return _forward(node_feature, edge_attr, edge_feature, W_skip0, W_skip1, W_nl0, W_nl1, W_fc1, W_fc2, W_out_s, W_out_v, edge_index)

    def _L1_gnn_ref(node, rbf, rsh, gamma_s, beta_s, gamma_v, Ws_src, Wv_src, Ws_dst, Wv_dst, W_rbf, W_alpha, alpha_dot, Ws_val, Wv_val, Wg, w2_ss, w2_sv, w2_vs, w2_vv0, w2_vv1, Ws_vlin, Wv_vlin, Wps, Wpv, edge_index):
        import jax, jax.numpy as jnp
        import numpy as np
        N, E = (2500, 40000)
        CS, CV = (64, 32)
        AS_, AV, H = (16, 8, 4)
        NB = 16
        SQRT3 = 1.7320508075688772
        SQRT2 = 1.4142135623730951
        EPS = 1e-05

        def _cg_tp(s, v, y0, y1, w_ss, w_sv, w_vs, w_vv0, w_vv1):
            out_s = jnp.concatenate([w_ss * s * y0[:, None], w_vv0 * (jnp.einsum('eci,ei->ec', v, y1) / SQRT3)], axis=-1)
            out_v = jnp.concatenate([(w_sv * s)[:, :, None] * y1[:, None, :], (w_vs * jnp.ones_like(v[..., 0]))[..., None] * v * y0[:, None, None], (w_vv1 * jnp.ones_like(v[..., 0]))[..., None] * (jnp.cross(v, y1[:, None, :]) / SQRT2)], axis=1)
            return (out_s, out_v)

        def _equiv_layernorm(s, v, gamma_s, beta_s, gamma_v):
            mu = jnp.mean(s, axis=-1, keepdims=True)
            var = jnp.var(s, axis=-1, keepdims=True)
            s_n = (s - mu) * jax.lax.rsqrt(var + EPS) * gamma_s + beta_s
            rms = jnp.sqrt(jnp.mean(jnp.sum(v * v, axis=-1), axis=-1, keepdims=True) + EPS)
            v_n = v / rms[..., None] * gamma_v[None, :, None]
            return (s_n, v_n)
        n = node.shape[0]
        e = rsh.shape[0]
        s = node[:, :CS]
        v = node[:, CS:].reshape(n, CV, 3)
        s_n, v_n = _equiv_layernorm(s, v, gamma_s, beta_s, gamma_v)
        src, dst = (edge_index[0], edge_index[1])
        msg_s = (s_n @ Ws_src)[src] + (s_n @ Ws_dst)[dst]
        msg_v = jnp.einsum('ncx,cd->ndx', v_n, Wv_src)[src] + jnp.einsum('ncx,cd->ndx', v_n, Wv_dst)[dst]
        y0, y1 = (rsh[:, 0], rsh[:, 1:4])
        w1 = rbf @ W_rbf
        m1_s, m1_v = _cg_tp(msg_s, msg_v, y0, y1, w1[:, :CS], w1[:, CS:2 * CS], w1[:, 2 * CS:2 * CS + CV], w1[:, 2 * CS + CV:2 * CS + 2 * CV], w1[:, 2 * CS + 2 * CV:])
        a = (m1_s @ W_alpha).reshape(e, H, AS_)
        a = jnp.where(a > 0, a, 0.2 * a)
        a = jnp.sum(a * alpha_dot, axis=-1, keepdims=True)
        amax = jax.ops.segment_max(a, dst, num_segments=n)
        amax = jnp.where(jnp.isfinite(amax), amax, 0.0)
        ex = jnp.exp(a - amax[dst])
        den = jax.ops.segment_sum(ex, dst, num_segments=n)
        alpha = ex / (den[dst] + 1e-16)
        val_s = m1_s @ Ws_val
        val_v = jnp.einsum('ecx,cd->edx', m1_v, Wv_val)
        val_v = val_v * jax.nn.sigmoid(val_s @ Wg)[..., None]
        val_s = jax.nn.sigmoid(val_s)
        m2_s, m2_v = _cg_tp(val_s, val_v, y0, y1, w2_ss, w2_sv, w2_vs, w2_vv0, w2_vv1)
        hs = (m2_s @ Ws_vlin).reshape(e, H, AS_)
        hv = jnp.einsum('ecx,cd->edx', m2_v, Wv_vlin).reshape(e, H, AV, 3)
        h = jnp.concatenate([hs, hv.reshape(e, H, AV * 3)], axis=-1)
        agg = jax.ops.segment_sum(alpha * h, dst, num_segments=n)
        agg_s = agg[:, :, :AS_].reshape(n, H * AS_)
        agg_v = agg[:, :, AS_:].reshape(n, H * AV, 3)
        out = node + jnp.concatenate([agg_s @ Wps, jnp.einsum('ncx,cd->ndx', agg_v, Wpv).reshape(n, CV * 3)], axis=-1)
        return out

    def _L2_gnn_ref(node_features, edge_index, edge_attr_tensor, node_attr_scalar_raw, wm000, wm011, wm101, wm110, lm0, lm1, wu000, wu011, wu101, wu110, lu0, lu1):
        import jax, jax.numpy as jnp
        import numpy as np
        MUL0, MUL1 = (64, 32)
        INV_SQRT3 = 1.0 / np.sqrt(3.0)

        def _split(x):
            return (x[:, :MUL0], x[:, MUL0:].reshape(x.shape[0], MUL1, 3))

        def _merge(o0, o1):
            return jnp.concatenate([o0, o1.reshape(o1.shape[0], -1)], axis=-1)

        def _tp(x0, x1, y0, y1, w000, w011, w101, w110):
            fan0 = x0.shape[1] * y0.shape[1] + x1.shape[1] * y1.shape[1]
            fan1 = x0.shape[1] * y1.shape[1] + x1.shape[1] * y0.shape[1]
            out0 = (jnp.einsum('eu,ev,uvw->ew', x0, y0, w000) + INV_SQRT3 * jnp.einsum('euk,evk,uvw->ew', x1, y1, w110)) / np.sqrt(fan0)
            out1 = (jnp.einsum('eu,evk,uvw->ewk', x0, y1, w011) + jnp.einsum('euk,ev,uvw->ewk', x1, y0, w101)) / np.sqrt(fan1)
            return (out0, out1)

        def _lin(x0, x1, w0, w1):
            return (x0 @ w0 / np.sqrt(x0.shape[1]), jnp.einsum('euk,uv->evk', x1, w1) / np.sqrt(x1.shape[1]))
        N = node_features.shape[0]
        row, col = (edge_index[0], edge_index[1])
        r_vec = edge_attr_tensor[:, :3]
        dist = edge_attr_tensor[:, 3:4]
        e0 = dist
        e1 = r_vec[:, None, :]
        xj0, xj1 = _split(node_features[col])
        m0, m1 = _tp(xj0, xj1, e0, e1, wm000, wm011, wm101, wm110)
        d0, d1 = _lin(xj0, xj1, lm0, lm1)
        msgs = _merge(m0 + d0, m1 + d1)
        agg = jax.ops.segment_sum(msgs, row, num_segments=N)
        a0, a1 = _split(agg)
        x0, x1 = _split(node_features)
        u0, u1 = _tp(x0, x1, a0, a1, wu000, wu011, wu101, wu110)
        ud0, ud1 = _lin(x0, x1, lu0, lu1)
        return node_features + _merge(u0 + ud0, u1 + ud1)

    def _L3_gnn_ref(node_features, edge_index, edge_attr_tensor, node_attr_scalar_raw, Wm_ss, Wm_vv, Wm_sv, Wm_vs, Lm_s, Lm_v, Wu_ss, Wu_vv, Wu_sv, Wu_vs, Lu_s, Lu_v):
        import jax, jax.numpy as jnp
        import numpy as np
        N = 2500
        E = 80000
        INV_SQRT3 = 0.5773502691896258
        INV8 = 0.125
        INV_SQRT32 = 0.17677669529663687
        INV64 = 0.015625
        INV32 = 0.03125
        INV_SQRT2048 = 0.022097086912079608
        n = node_features.shape[0]
        e = edge_attr_tensor.shape[0]
        row, col = (edge_index[0], edge_index[1])
        r_vec = edge_attr_tensor[:, :3]
        dist = edge_attr_tensor[:, 3:4]
        xj = node_features[col]
        s = xj[:, :64]
        v = xj[:, 64:].reshape(e, 32, 3)
        m0 = s @ Wm_ss * dist * INV8 + jnp.einsum('eui,ei->eu', v, r_vec) @ Wm_vv * (INV_SQRT3 * INV_SQRT32)
        m1 = (s @ Wm_sv)[:, :, None] * r_vec[:, None, :] * INV8 + jnp.einsum('eui,uw->ewi', v, Wm_vs) * dist[:, :, None] * INV_SQRT32
        m0 = m0 + s @ Lm_s * INV8
        m1 = m1 + jnp.einsum('eui,uw->ewi', v, Lm_v) * INV_SQRT32
        msg = jnp.concatenate([m0, m1.reshape(e, 96)], axis=-1)
        agg = jax.ops.segment_sum(msg, row, num_segments=n)
        a0 = agg[:, :64]
        a1 = agg[:, 64:].reshape(n, 32, 3)
        xs = node_features[:, :64]
        xv = node_features[:, 64:].reshape(n, 32, 3)
        u0 = jnp.einsum('nu,nv,uvw->nw', xs, a0, Wu_ss) * INV64 + jnp.einsum('nui,nvi,uvw->nw', xv, a1, Wu_vv) * (INV_SQRT3 * INV32)
        u1 = jnp.einsum('nu,nvi,uvw->nwi', xs, a1, Wu_sv) * INV_SQRT2048 + jnp.einsum('nui,nv,uvw->nwi', xv, a0, Wu_vs) * INV_SQRT2048
        u0 = u0 + xs @ Lu_s * INV8
        u1 = u1 + jnp.einsum('nui,uw->nwi', xv, Lu_v) * INV_SQRT32
        upd = jnp.concatenate([u0, u1.reshape(n, 96)], axis=-1)
        return node_features + upd
    edge_index = jnp.stack([src, dst])
    x = _layernorm(x + _L0_gnn_ref(x, edge_attr_3, edge_attr_64, L0_gnn_W_skip0, L0_gnn_W_skip1, L0_gnn_W_nl0, L0_gnn_W_nl1, L0_gnn_W_fc1, L0_gnn_W_fc2, L0_gnn_W_out_s, L0_gnn_W_out_v, edge_index), axis=-1)
    x = _layernorm(x + _L1_gnn_ref(x, edge_attr_16, edge_attr_4, L1_gnn_gamma_s, L1_gnn_beta_s, L1_gnn_gamma_v, L1_gnn_Ws_src, L1_gnn_Wv_src, L1_gnn_Ws_dst, L1_gnn_Wv_dst, L1_gnn_W_rbf, L1_gnn_W_alpha, L1_gnn_alpha_dot, L1_gnn_Ws_val, L1_gnn_Wv_val, L1_gnn_Wg, L1_gnn_w2_ss, L1_gnn_w2_sv, L1_gnn_w2_vs, L1_gnn_w2_vv0, L1_gnn_w2_vv1, L1_gnn_Ws_vlin, L1_gnn_Wv_vlin, L1_gnn_Wps, L1_gnn_Wpv, edge_index), axis=-1)
    x = _layernorm(x + _L2_gnn_ref(x, edge_index, edge_attr_4, node_vec1, L2_gnn_wm000, L2_gnn_wm011, L2_gnn_wm101, L2_gnn_wm110, L2_gnn_lm0, L2_gnn_lm1, L2_gnn_wu000, L2_gnn_wu011, L2_gnn_wu101, L2_gnn_wu110, L2_gnn_lu0, L2_gnn_lu1), axis=-1)
    x = _layernorm(x + _L3_gnn_ref(x, edge_index, edge_attr_4, node_vec1, L3_gnn_Wm_ss, L3_gnn_Wm_vv, L3_gnn_Wm_sv, L3_gnn_Wm_vs, L3_gnn_Lm_s, L3_gnn_Lm_v, L3_gnn_Wu_ss, L3_gnn_Wu_vv, L3_gnn_Wu_sv, L3_gnn_Wu_vs, L3_gnn_Lu_s, L3_gnn_Lu_v), axis=-1)
    return x

_drawn_inputs = setup_inputs


def setup_inputs(seed=0):
    import zlib

    import numpy as np

    out = dict(_drawn_inputs(seed))
    spreads = {'L1_gnn_gamma_s': (1.0, 0.2), 'L1_gnn_beta_s': (0.0, 0.1), 'L1_gnn_gamma_v': (1.0, 0.2)}
    factors = {}
    for name, (base, spread) in spreads.items():
        noise = np.random.default_rng([zlib.crc32(name.encode()), seed]).standard_normal(out[name].shape)
        drawn = base * np.exp(spread * noise) if base else spread * noise
        out[name] = jnp.asarray(drawn.astype(out[name].dtype))
    for name, factor in factors.items():
        out[name] = (out[name] * factor).astype(out[name].dtype)
    return out
```

```python
from contextlib import ExitStack

import concourse.bass as bass
from concourse import mybir

F32 = mybir.dt.float32
I32 = mybir.dt.int32
ALU = mybir.AluOpType
ACT = mybir.ActivationFunctionType
AX = mybir.AxisListType

P = 128
N, E = 6250, 206250
NB = 2 * -(-N // (2 * P))
NP = NB * P
NT = -(-E // P)
EP = NT * P
U = 4
TURNS = NT // U
assert TURNS * U == NT
CS, CV = 64, 32
D = CS + 3 * CV
ACC_ROWS = NP + P
ADD_TABLES = 2
SM_TABLES = U
AGG0 = 480
CAT = 2 * D + 3 * CS + CV
HD = 41
SMW = 4 + 4 * HD
COMB = D + SMW
LOW = -1.0e30
EPS = 1e-5
S3 = 3.0 ** 0.5
S2 = 2.0 ** 0.5


class Tile:

    def __init__(self, i, j, unroll, number, off=0, held=None):
        self.i, self.j, self.unroll, self.number, self.off, self.held = i, j, unroll, number, off, held

    def back(self, k):
        off, j = divmod(self.j - k, self.unroll)
        return Tile(self.i, j, self.unroll, self.number, self.off + off, self.held)

    def value(self, a, c):
        if self.held is not None:
            return self.held[(a, c)]
        return self.i * a + c

    def first_turns(self):
        return isinstance(self.i, int)

    def exists(self):
        return not self.first_turns() or 0 <= self.unroll * (self.i + self.off) + self.j < self.number

    def t(self):
        return self.count(0)

    def count(self, more=0, each=1):
        return self.value(each * self.unroll, each * (self.unroll * self.off + self.j) + more)

    def dma(self, before=0):
        return self.value(16, 16 * (self.off + 1 - before))

    def reuses(self, slots):
        return not self.first_turns() or self.unroll * (self.i + self.off) + self.j >= slots


def run_steps(eng, step, lag, unroll, number, held=()):
    turns = number // unroll
    assert turns * unroll == number and lag <= unroll
    for j in range(unroll):
        step(Tile(0, j, unroll, number))
    with eng.Fori(1, turns) as i:
        registers = {(a, c): eng.snap(eng.to_reg(i * a + c)) for a, c in held} or None
        for j in range(unroll):
            step(Tile(i, j, unroll, number, 0, registers))
    for j in range(lag):
        step(Tile(turns, j, unroll, number))


def edge_steps(eng, step, lag, held=()):
    run_steps(eng, step, lag, U, NT, held)


def node_steps(eng, step):
    run_steps(eng, step, 0, 2, NB)


def bcast(ap, shape):
    return ap.to_broadcast(list(shape))


class Phase:

    def __init__(self, nc, name):
        self.nc, self.name, self.ctx, self.sems = nc, name, ExitStack(), []

    def __enter__(self):
        self.ctx.__enter__()
        return self

    def __exit__(self, *args):
        if args[0] is None:
            sems = self.sems
            with self.nc.Block() as block:
                @block.gpsimd
                def _(pool):
                    for s in sems:
                        pool.sem_clear(s)
        return self.ctx.__exit__(*args)

    def sb(self, name, shape, dtype=F32):
        return self.ctx.enter_context(self.nc.sbuf_tensor(f"{self.name}_{name}", shape, dtype))

    def ps(self, name, shape=(P, 512)):
        return self.ctx.enter_context(self.nc.psum_tensor(f"{self.name}_{name}", list(shape), F32))

    def sem(self, name):
        s = self.ctx.enter_context(self.nc.semaphore(f"{self.name}_{name}"))
        self.sems.append(s)
        return s

    def sems_of(self, name, n):
        return [self.sem(f"{name}{k}") for k in range(n)]


def prepare(nc, g, A, tables):
    with Phase(nc, "prep") as ph:
        rows = [ph.sb(f"row_i{k}", [P, NT], I32) for k in range(2)]
        rows_f = [ph.sb(f"row_f{k}", [P, NT]) for k in range(2)]
        square = ph.sb("square", [P, NT, 3])
        norm = ph.sb("norm", [P, NT])
        waste_i = ph.sb("waste_i", [P, 1], I32)
        ones = ph.sb("ones", [P, P])
        zeros = ph.sb("zeros", [P, AGG0])
        loaded, made, unit, stored, consts = (ph.sem(n) for n in ("loaded", "cast", "unit", "stored", "consts"))
        rooted, zeroed, cleared = (ph.sem(n) for n in ("rooted", "zeroed", "cleared"))
        with nc.Block() as block:
            @block.sync
            def _(sp):
                for dst, src in ((g.key_i[0], A["src_col"]), (g.key_i[1], A["dst_col"]),
                                 (rows[0], A["src_row"]), (rows[1], A["dst_row"])):
                    sp.dma_start(dst[:, :], src).then_inc(loaded, 16)
                sp.dma_start(g.attr3[:, :, :], A["attr3"]).then_inc(loaded, 16)
                sp.dma_start(g.attr4[:, :, :], A["attr4"]).then_inc(loaded, 16)
                sp.wait_ge(zeroed, 1)
                for table in tables:
                    width = table.shape[1]
                    sp.dma_start(table.rearrange("(b p) w -> p b w", p=P),
                                 bcast(zeros[:, 0:width].unsqueeze(1), (P, ACC_ROWS // P, width))).then_inc(cleared, 16)
                sp.wait_ge(cleared, 16 * len(tables))
                for k in range(2):
                    sp.wait_ge(made, k + 1)
                    sp.dma_start(g.key_rows[k].rearrange("(p t) -> p t", p=P), rows_f[k][:, :]).then_inc(stored, 16)
                sp.wait_ge(stored, 32)

            @block.gpsimd
            def _(pool):
                pool.memset(ones[:, :], 1.0).then_inc(consts, 1)
                pool.iota(waste_i[:, :], pattern=[[0, 1]], base=NP, channel_multiplier=1).then_inc(consts, 1)
                pool.wait_ge(consts, 1)
                pool.affine_select(out=g.ident[:, :], in_=ones[:, :], compare_op=ALU.is_equal, fill=0.0, base=0,
                                   pattern=[[-1, P]], channel_multiplier=1).then_inc(consts, 1)
                pool.affine_select(out=g.before[:, :], in_=ones[:, :], compare_op=ALU.is_gt, fill=0.0, base=0,
                                   pattern=[[-1, P]], channel_multiplier=1).then_inc(consts, 1)

            @block.vector
            def _(dve):
                dve.memset(zeros[:, :], 0.0).then_inc(zeroed, 1)
                dve.wait_ge(loaded, 96)
                for k in range(2):
                    dve.tensor_copy(rows_f[k][:, :], rows[k][:, :]).then_inc(made, 1)
                for k in range(2):
                    dve.tensor_copy(g.key_f[k][:, :], g.key_i[k][:, :])
                dve.wait_ge(consts, 2)
                dve.tensor_copy(g.waste[:, :], waste_i[:, :])
                dve.tensor_tensor(square[:, :, :], g.attr3[:, :, :], g.attr3[:, :, :], ALU.mult).then_inc(unit, 1)
                dve.wait_ge(unit, 1)
                dve.tensor_reduce(norm[:, :], square[:, :, :], AX.X, ALU.add).then_inc(unit, 1)
                dve.wait_ge(rooted, 1)
                dve.reciprocal(norm[:, :], norm[:, :]).then_inc(unit, 1)
                dve.wait_ge(unit, 3)
                dve.scalar_tensor_tensor(out=g.attr3[:, :, :], in0=g.attr3[:, :, :], scalar=S3,
                                         in1=bcast(norm[:, :].unsqueeze(2), (P, NT, 3)),
                                         op0=ALU.mult, op1=ALU.mult).then_inc(unit, 1)
                dve.wait_ge(unit, 4)

            @block.scalar
            def _(act):
                act.wait_ge(unit, 2)
                act.activation(norm[:, :], norm[:, :], ACT.Sqrt).then_inc(rooted, 1)

    with Phase(nc, "firsts") as ph:
        W = 2
        keys = [[ph.sb(f"keys{k}{q}", [P, W * P]) for q in range(2)] for k in range(2)]
        earlier = [ph.sb(f"earlier{k}", [P, NT]) for k in range(2)]
        hit = [ph.sb(f"hit{q}", [P, 2 * W * P]) for q in range(2)]
        work = [ph.sb(f"work{k}", [P, NT]) for k in range(2)]
        landed = [ph.sems_of(f"landed{k}", 2) for k in range(2)]
        counted, final = ph.sem("counted"), ph.sem("final")
        with nc.Block() as block:
            @block.sync
            def _(sp):
                def load(s):
                    if s.reuses(2):
                        sp.wait_ge(counted, s.count(-1))
                    for k in range(2):
                        src = g.key_rows[k][bass.ds(s.t() * (W * P), W * P)].partition_broadcast(P)
                        sp.dma_start(keys[k][s.j][:, :], src).then_inc(landed[k][s.j], 16)
                run_steps(sp, load, 0, 2, NT // W)

            @block.vector
            def _(dve):
                def count(s):
                    if s.reuses(2):
                        dve.wait_ge(counted, s.count(-1))
                    for k in range(2):
                        dve.wait_ge(landed[k][s.j], s.dma())
                        for w in range(W):
                            t = s.t() * W + w
                            place = (W * k + w) * P
                            ins = dve.scalar_tensor_tensor(
                                out=hit[s.j][:, place:place + P], in0=keys[k][s.j][:, w * P:(w + 1) * P],
                                scalar=g.key_f[k][:, bass.ds(t, 1)], in1=g.before[:, :],
                                op0=ALU.is_equal, op1=ALU.mult, accum_out=earlier[k][:, bass.ds(t, 1)])
                    ins.then_inc(counted, 1)
                run_steps(dve, count, 0, 2, NT // W)
                dve.wait_ge(counted, NT // W)
                n = 0

                def then(ins):
                    nonlocal n
                    n += 1
                    ins.then_inc(final, 1)
                    dve.wait_ge(final, n)
                for k in range(2):
                    then(dve.tensor_scalar(earlier[k][:, :], earlier[k][:, :], 1.0, None, ALU.min))
                    then(dve.tensor_scalar(work[k][:, :], g.key_f[k][:, :], -1.0, g.waste[:, 0:1], ALU.mult, ALU.add))
                    then(dve.tensor_tensor(work[k][:, :], work[k][:, :], earlier[k][:, :], ALU.mult))
                    then(dve.tensor_tensor(g.put_i[k][:, :], work[k][:, :], g.key_f[k][:, :], ALU.add))



def edge_layer0(nc, g, A, table, accs):
    with Phase(nc, "e0") as ph:
        W1, W2 = ph.sb("W1", [64, P]), ph.sb("W2", [64, 224])
        feat = [ph.sb(f"feat{k}", [64, P]) for k in range(U)]
        keys = [ph.sb(f"keys{k}", [P, P]) for k in range(U)]
        take = [ph.sb(f"take{k}", [P, 1], I32) for k in range(U)]
        put = [ph.sb(f"put{k}", [P, 1], I32) for k in range(U)]
        row = [ph.sb(f"row{k}", [P, D]) for k in range(U)]
        hid = [ph.sb(f"hid{k}", [64, P]) for k in range(2)]
        same = [ph.sb(f"same{k}", [P, P]) for k in range(2)]
        QW = 1024
        q = [ph.sb(f"q{k}", [P, QW]) for k in range(2)]
        part = ph.sb("part", [P, 3 * CV])
        total = [ph.sb(f"total{k}", [P, AGG0]) for k in range(U)]
        ps_h, ps_w, ps_o = ([ph.ps(f"{n}{k}") for k in range(2)] for n in ("ps_h", "ps_w", "ps_o"))
        wl = ph.sem("weights")
        keys_in, feat_in = ph.sems_of("keys_in", U), ph.sems_of("feat_in", U)
        row_in, added = g.pool_dmas["e0"]
        (take_set, put_set, same_set, prods, dot0, dot1, halves, feats, hid_ps, hid_set, w_ps, sv_set,
         sums_ps, total_set) = (ph.sem(n) for n in (
             "take_set", "put_set", "same_set", "prods", "dot0", "dot1", "halves", "feats", "hid_ps",
             "hid_set", "w_ps", "sv_set", "sums_ps", "total_set"))
        SV, CR, DOT, S0, V2, T1 = 0, 192, 288, 320, 384, 672

        with nc.Block() as block:
            @block.sync
            def _(sp):
                sp.dma_start(W1[:, :], A["w0_fc1"]).then_inc(wl, 16)
                sp.dma_start(W2[:, :], A["w0_fc2"]).then_inc(wl, 16)

                def step(t):
                    if not t.exists():
                        return
                    if t.reuses(U):
                        sp.wait_ge(same_set, t.count(1 - U))
                    sp.dma_start(keys[t.j][:, :], g.key_rows[0][bass.ds(t.t() * P, P)].partition_broadcast(P)).then_inc(keys_in[t.j], 16)
                    if t.reuses(U):
                        sp.wait_ge(hid_ps, t.count(1 - U))
                    sp.dma_start(feat[t.j][:, :], A["attr64_T"][:, bass.ds(t.t() * P, P)]).then_inc(feat_in[t.j], 16)
                edge_steps(sp, step, 0)

            @block.gpsimd
            def _(pool):
                def step(s):
                    if s.exists():
                        t = s
                        pool.wait_ge(wl, 32)
                        pool.wait_ge(take_set, t.count(1))
                        if t.reuses(U):
                            pool.wait_ge(prods, t.count(1 - U))
                        pool.indirect_dma_start(out=row[t.j][:, :], out_offset=None, in_=table,
                                                in_offset=bass.IndirectOffsetOnAxis(ap=take[t.j][:, :], axis=0)).then_inc(row_in[t.j], 16)
                    t = s.back(3)
                    if t.exists():
                        pool.wait_ge(wl, 32)
                        pool.wait_ge(total_set, t.count(1))
                        pool.wait_ge(put_set, t.count(1))
                        if t.reuses(ADD_TABLES):
                            pool.wait_ge(added[(t.j - ADD_TABLES) % U], t.back(ADD_TABLES).dma())
                        pool.indirect_dma_start(out=accs[t.j % ADD_TABLES], out_offset=bass.IndirectOffsetOnAxis(ap=put[t.j][:, :], axis=0),
                                                in_=total[t.j][:, :], in_offset=None, compute_op=ALU.add).then_inc(added[t.j], 16)
                edge_steps(pool, step, 3, [(U, c) for c in range(-6, 5)] + [(16, 16 * c) for c in (-1, 0, 1)])
                for k in range(U):
                    pool.wait_ge(added[k], 16 * TURNS)

            @block.tensor
            def _(pe):
                pe.wait_ge(wl, 32)

                def step(s):
                    t = s.back(1)
                    if t.exists():
                        b = t.j % 2
                        pe.wait_ge(feat_in[t.j], t.dma())
                        if t.reuses(2):
                            pe.wait_ge(hid_set, t.count(-1))
                        pe.matmul(ps_h[b][:, 0:P], W1[:, :], feat[t.j][:, :], start=True, stop=True).then_inc(hid_ps, 1)
                        pe.wait_ge(hid_set, t.count(1))
                        if t.reuses(2):
                            pe.wait_ge(prods, t.count(-1))
                        pe.matmul(ps_w[b][:, 0:224], hid[b][:, :], W2[:, :], start=True, stop=True).then_inc(w_ps, 1)
                    t = s.back(2)
                    if t.exists():
                        b = t.j % 2
                        pe.wait_ge(feats, t.count(1))
                        pe.wait_ge(sv_set, t.count(1))
                        if t.reuses(2):
                            pe.wait_ge(total_set, t.count(-1))
                        pe.matmul(ps_o[b][:, 0:AGG0], same[b][:, :], q[b][:, 0:AGG0], start=True, stop=True).then_inc(sums_ps, 1)
                edge_steps(pe, step, 2)

            @block.scalar
            def _(act):
                def step(s):
                    t = s.back(1)
                    if t.exists():
                        b = t.j % 2
                        act.wait_ge(hid_ps, t.count(1))
                        if t.reuses(2):
                            act.wait_ge(w_ps, t.count(-1))
                        act.activation(hid[b][:, :], ps_h[b][0:64, 0:P], ACT.Relu).then_inc(hid_set, 1)
                    t = s.back(2)
                    if t.exists():
                        b = t.j % 2
                        act.wait_ge(prods, t.count(1))
                        if t.reuses(2):
                            act.wait_ge(sums_ps, t.count(-1))
                        for c in range(3):
                            ins = act.activation(q[b][:, SV + CS * c:SV + CS * (c + 1)], q[b][:, T1:T1 + CS], ACT.Copy,
                                                 scale=g.attr3[:, bass.ds(t.t(), 1), c])
                        ins.then_inc(sv_set, 1)
                        act.wait_ge(sums_ps, t.count(1))
                        if t.reuses(U):
                            act.wait_ge(added[t.j], t.dma(1))
                        act.activation(total[t.j][:, :], ps_o[b][:, 0:AGG0], ACT.Copy).then_inc(total_set, 1)
                edge_steps(act, step, 2)

            @block.vector
            def _(dve):
                def step(s):
                    if s.exists():
                        t = s
                        if t.reuses(U):
                            dve.wait_ge(row_in[t.j], t.dma(1))
                        dve.tensor_copy(take[t.j][:, :], g.key_i[1][:, bass.ds(t.t(), 1)]).then_inc(take_set, 1)
                    t = s.back(2)
                    if not t.exists():
                        return
                    b = t.j % 2
                    qb, w = q[b], ps_w[b]
                    sh = [g.attr3[:, bass.ds(t.t(), 1), c] for c in range(3)]
                    if t.reuses(U):
                        dve.wait_ge(added[t.j], t.dma(1))
                    dve.tensor_copy(put[t.j][:, :], g.put_i[0][:, bass.ds(t.t(), 1)]).then_inc(put_set, 1)
                    dve.wait_ge(row_in[t.j], t.dma())
                    dve.wait_ge(w_ps, t.count(1))
                    if t.reuses(2):
                        dve.wait_ge(sums_ps, t.count(-1))
                        dve.wait_ge(sv_set, t.count(-1))
                    dve.tensor_tensor(qb[:, S0:S0 + 2 * (T1 - S0)].rearrange("p (a c) -> p a c", a=2)[:, :, 0:CS],
                                      w[:, 0:2 * CS].rearrange("p (a c) -> p a c", a=2),
                                      bcast(row[t.j][:, 0:CS].unsqueeze(1), (P, 2, CS)), ALU.mult)
                    dve.tensor_tensor(qb[:, V2:V2 + 9 * CV].rearrange("p (g c m) -> p g c m", g=3, c=3),
                                      bcast(w[:, 2 * CS:2 * CS + 3 * CV].rearrange("p (g m) -> p g m", g=3).unsqueeze(2), (P, 3, 3, CV)),
                                      bcast(row[t.j][:, CS:D].rearrange("p (c m) -> p c m", c=3).unsqueeze(1), (P, 3, 3, CV)),
                                      ALU.mult).then_inc(prods, 1)
                    dve.wait_ge(keys_in[t.j], t.dma())
                    dve.tensor_scalar(same[b][:, :], keys[t.j][:, :], g.key_f[0][:, bass.ds(t.t(), 1)], None, ALU.is_equal).then_inc(same_set, 1)
                    q3 = [qb[:, V2 + (3 + c) * CV:V2 + (4 + c) * CV] for c in range(3)]
                    q4 = [qb[:, V2 + (6 + c) * CV:V2 + (7 + c) * CV] for c in range(3)]
                    dot = qb[:, DOT:DOT + CV]
                    dve.wait_ge(prods, t.count(1))
                    dve.tensor_scalar(dot, q3[0], sh[0], None, ALU.mult).then_inc(dot0, 1)
                    for c in range(3):
                        ins = dve.tensor_scalar(part[:, c * CV:(c + 1) * CV], q4[(c + 2) % 3], sh[(c + 1) % 3], None, ALU.mult)
                    ins.then_inc(halves, 1)
                    dve.wait_ge(dot0, t.count(1))
                    dve.scalar_tensor_tensor(out=dot, in0=q3[1], scalar=sh[1], in1=dot, op0=ALU.mult, op1=ALU.add).then_inc(dot1, 1)
                    dve.wait_ge(halves, t.count(1))
                    for c in range(3):
                        dve.scalar_tensor_tensor(out=qb[:, CR + c * CV:CR + (c + 1) * CV], in0=q4[(c + 1) % 3], scalar=sh[(c + 2) % 3],
                                                 in1=part[:, c * CV:(c + 1) * CV], op0=ALU.mult, op1=ALU.subtract)
                    dve.wait_ge(dot1, t.count(1))
                    dve.scalar_tensor_tensor(out=dot, in0=q3[2], scalar=sh[2], in1=dot, op0=ALU.mult, op1=ALU.add).then_inc(feats, 1)
                edge_steps(dve, step, 2)


class Linked:

    def __init__(self, eng, sem, each):
        self.eng, self.sem, self.each, self.k = eng, sem, each, 0

    def start(self, item):
        self.item, self.k = item, 0

    def link(self, ins):
        self.k += 1
        ins.then_inc(self.sem, 1)
        self.eng.wait_ge(self.sem, self.item.count(self.k, self.each))

    def end(self):
        assert self.k == self.each, self.k


def layernorm(dve, chain, y, stats, out, squares, roots, item, nth, each):
    chain.link(dve.bn_stats(stats[:, 0:6], y))
    dve.memset(stats[:, 22:23], 0.0)
    chain.link(dve.bn_aggr(stats[:, 6:8], stats[:, 0:6]))
    dve.tensor_scalar(stats[:, 8:9], stats[:, 7:8], EPS, None, ALU.add).then_inc(squares, 1)
    dve.wait_ge(roots, item.count(nth, each))
    chain.link(dve.reciprocal(stats[:, 8:9], stats[:, 8:9]))
    return dve.tensor_scalar(out, y, stats[:, 6:7], stats[:, 8:9], ALU.subtract, ALU.mult)


def root(act, at, squares, roots, item, nth, each):
    act.wait_ge(squares, item.count(nth, each))
    act.activation(at, at, ACT.Sqrt).then_inc(roots, 1)


def load_matrix(eng, dst, src, sem):
    eng.dma_start(dst[:, :, :], src.rearrange("(k p) n -> p k n", p=P)).then_inc(sem, 16)


def first_table(nc, g, A, x, table):
    with Phase(nc, "n0") as ph:
        W = ph.sb("W", [P, 2, D])
        row = [ph.sb(f"row{k}", [P, 2 * P]) for k in range(2)]
        rowT = [ph.sb(f"rowT{k}", [P, 2 * P]) for k in range(2)]
        out = [ph.sb(f"out{k}", [P, D]) for k in range(2)]
        ps_t, ps_o = [ph.ps(f"ps_t{k}") for k in range(2)], [ph.ps(f"ps_o{k}") for k in range(2)]
        wl, blank, turned, turned_sb, ps_set, out_set = (ph.sem(n) for n in (
            "weights", "blank", "turned", "turned_sb", "ps_set", "out_set"))
        row_in, stored = ph.sems_of("row_in", 2), ph.sems_of("stored", 2)
        with nc.Block() as block:
            @block.sync
            def _(sp):
                load_matrix(sp, W, A["w0_nl"], wl)

                def step(b):
                    if b.reuses(2):
                        sp.wait_ge(turned, b.count(-1))
                    sp.dma_start(row[b.j][:, 0:D], x[bass.ds(b.t() * P, P), :]).then_inc(row_in[b.j], 16)
                    p = b.back(1)
                    if p.exists():
                        sp.wait_ge(out_set, p.count(1))
                        sp.dma_start(table[bass.ds(p.t() * P, P), :], out[p.j][:, :]).then_inc(stored[p.j], 16)
                run_steps(sp, step, 0, 2, NB)
                last = Tile(NB // 2 - 1, 1, 2, NB)
                sp.wait_ge(out_set, last.count(1))
                sp.dma_start(table[(NB - 1) * P:NB * P, :], out[1][:, :]).then_inc(stored[1], 16)
                for k in range(2):
                    sp.wait_ge(stored[k], 16 * (NB // 2))

            @block.tensor
            def _(pe):
                pe.wait_ge(wl, 16)
                pe.wait_ge(blank, 1)

                def step(b):
                    pe.wait_ge(row_in[b.j], b.dma())
                    if b.reuses(2):
                        pe.wait_ge(turned_sb, b.count(-1))
                    pe.transpose(ps_t[b.j][:, 0:P], row[b.j][:, 0:P], g.ident[:, :])
                    pe.transpose(ps_t[b.j][:, P:2 * P], row[b.j][:, P:2 * P], g.ident[:, :]).then_inc(turned, 1)
                    pe.wait_ge(turned_sb, b.count(1))
                    if b.reuses(2):
                        pe.wait_ge(out_set, b.count(-1))
                    for c in range(2):
                        ins = pe.matmul(ps_o[b.j][:, 0:D], rowT[b.j][:, c * P:(c + 1) * P], W[:, c, :], start=c == 0, stop=c == 1)
                    ins.then_inc(ps_set, 1)
                node_steps(pe, step)

            @block.scalar
            def _(act):
                def step(b):
                    act.wait_ge(turned, b.count(1))
                    if b.reuses(2):
                        act.wait_ge(ps_set, b.count(-1))
                    act.activation(rowT[b.j][:, :], ps_t[b.j][:, 0:2 * P], ACT.Copy).then_inc(turned_sb, 1)
                node_steps(act, step)

            @block.vector
            def _(dve):
                dve.memset(row[0][:, D:2 * P], 0.0)
                dve.memset(row[1][:, D:2 * P], 0.0).then_inc(blank, 1)

                def step(b):
                    dve.wait_ge(ps_set, b.count(1))
                    if b.reuses(2):
                        dve.wait_ge(stored[b.j], b.dma(1))
                    dve.tensor_copy(out[b.j][:, :], ps_o[b.j][:, 0:D]).then_inc(out_set, 1)
                node_steps(dve, step)


def nodes_after_0(nc, g, A, x, accs, x_out, src_table, combs):
    with Phase(nc, "n1") as ph:
        WA, WX, WT = ph.sb("WA", [P, 4, 192]), ph.sb("WX", [P, 2, 192]), ph.sb("WT", [P, 2, 2 * D])
        gam, bet = ph.sb("gam", [P, D]), ph.sb("bet", [P, CS])
        two = range(2)
        acc = [[ph.sb(f"acc{k}{a}", [P, AGG0]) for a in range(ADD_TABLES)] for k in two]
        row = [ph.sb(f"row{k}", [P, 2 * P]) for k in two]
        agg = [ph.sb(f"agg{k}", [P, 4 * P]) for k in two]
        aggT = [ph.sb(f"aggT{k}", [P, 4 * P]) for k in two]
        rowT = [ph.sb(f"rowT{k}", [P, 2 * P]) for k in two]
        sig = [ph.sb(f"sig{k}", [P, 96]) for k in two]
        y = [ph.sb(f"y{k}", [P, D]) for k in two]
        new = [ph.sb(f"new{k}", [P, D]) for k in two]
        nrm = [ph.sb(f"nrm{k}", [P, 2 * P]) for k in two]
        nrmT = [ph.sb(f"nrmT{k}", [P, 2 * P]) for k in two]
        stats = [ph.sb(f"stats{k}", [P, 24]) for k in two]
        ts = [ph.sb(f"ts{k}", [P, D]) for k in two]
        comb = [ph.sb(f"comb{k}", [P, COMB]) for k in two]
        sq = ph.sb("sq", [P, 3 * CV])
        ps_a, ps_x, ps_o, ps_n, ps_c = (ph.ps(n) for n in ("ps_a", "ps_x", "ps_o", "ps_n", "ps_c"))
        names = ("weights", "scaled", "blank", "agg_set", "agg_t", "aggT_set", "rowT_set", "o_set", "sig_set",
                 "chain", "new_set", "nrm_set", "nrm_t", "nrmT_set", "c_set", "out_set", "upd_set", "squares", "roots")
        (wl, scaled, blank, agg_set, agg_t, aggT_set, rowT_set, o_set, sig_set, chained, new_set, nrm_set,
         nrm_t, nrmT_set, c_set, out_set, upd_set, squares, roots) = (ph.sem(n) for n in names)
        row_in, acc_in, stored = ph.sems_of("row_in", 2), ph.sems_of("acc_in", 2), ph.sems_of("stored", 2)
        PUTS = 2 + SM_TABLES
        with nc.Block() as block:
            @block.sync
            def _(sp):
                load_matrix(sp, WA, A["w0_agg"], wl)
                load_matrix(sp, WX, A["w0_skip"], wl)
                load_matrix(sp, WT, A["w1_tab"], wl)
                sp.dma_start(gam[:, :], A["gamma1"].partition_broadcast(P)).then_inc(wl, 16)
                sp.dma_start(bet[:, :], A["beta1"].partition_broadcast(P)).then_inc(wl, 16)

                def store(p):
                    where = bass.ds(p.t() * P, P)
                    sp.wait_ge(new_set, p.count(1))
                    sp.dma_start(x_out[where, :], new[p.j][:, :]).then_inc(stored[p.j], 16)
                    sp.wait_ge(out_set, p.count(1))
                    sp.dma_start(src_table[where, :], ts[p.j][:, :]).then_inc(stored[p.j], 16)
                    for k in range(SM_TABLES):
                        sp.dma_start(combs[k][where, :], comb[p.j][:, :]).then_inc(stored[p.j], 16)

                def step(b):
                    where = bass.ds(b.t() * P, P)
                    if b.reuses(2):
                        sp.wait_ge(agg_set, b.count(-1))
                    for a in range(ADD_TABLES):
                        sp.dma_start(acc[b.j][a][:, :], accs[a][where, :]).then_inc(acc_in[b.j], 16)
                    if b.reuses(2):
                        sp.wait_ge(upd_set, b.count(-1))
                    sp.dma_start(row[b.j][:, 0:D], x[where, :]).then_inc(row_in[b.j], 16)
                    p = b.back(1)
                    if p.exists():
                        store(p)
                node_steps(sp, step)
                store(Tile(NB // 2 - 1, 1, 2, NB))
                for k in two:
                    sp.wait_ge(stored[k], 16 * PUTS * (NB // 2))

            @block.tensor
            def _(pe):
                pe.wait_ge(scaled, 1)
                pe.wait_ge(blank, 1)

                def step(b):
                    pe.wait_ge(agg_set, b.count(1))
                    pe.wait_ge(row_in[b.j], b.dma())
                    if b.reuses(2):
                        pe.wait_ge(rowT_set, b.count(0))
                    for c in range(4):
                        pe.transpose(ps_a[:, c * P:(c + 1) * P], agg[b.j][:, c * P:(c + 1) * P], g.ident[:, :])
                    for c in range(2):
                        ins = pe.transpose(ps_x[:, c * P:(c + 1) * P], row[b.j][:, c * P:(c + 1) * P], g.ident[:, :])
                    ins.then_inc(agg_t, 1)
                    pe.wait_ge(rowT_set, b.count(1))
                    if b.reuses(2):
                        pe.wait_ge(upd_set, b.count(0))
                    for c in range(4):
                        pe.matmul(ps_o[:, 0:192], aggT[b.j][:, c * P:(c + 1) * P], WA[:, c, :], start=c == 0, stop=False)
                    for c in range(2):
                        ins = pe.matmul(ps_o[:, 0:192], rowT[b.j][:, c * P:(c + 1) * P], WX[:, c, :], start=False, stop=c == 1)
                    ins.then_inc(o_set, 1)
                    pe.wait_ge(nrm_set, b.count(1))
                    if b.reuses(2):
                        pe.wait_ge(nrmT_set, b.count(0))
                    for c in range(2):
                        ins = pe.transpose(ps_n[:, c * P:(c + 1) * P], nrm[b.j][:, c * P:(c + 1) * P], g.ident[:, :])
                    ins.then_inc(nrm_t, 1)
                    pe.wait_ge(nrmT_set, b.count(1))
                    if b.reuses(2):
                        pe.wait_ge(out_set, b.count(0))
                    for c in range(2):
                        ins = pe.matmul(ps_c[:, 0:2 * D], nrmT[b.j][:, c * P:(c + 1) * P], WT[:, c, :], start=c == 0, stop=c == 1)
                    ins.then_inc(c_set, 1)
                node_steps(pe, step)

            @block.scalar
            def _(act):
                act.wait_ge(wl, 16 * 5)
                act.mul(WA[:, :, :], WA[:, :, :], 1.0 / 32.0).then_inc(scaled, 1)
                act.wait_ge(scaled, 1)
                act.mul(WA[64:128, 1, :], WA[64:128, 1, :], 1.0 / S2)
                act.mul(WA[0:32, 2, :], WA[0:32, 2, :], 1.0 / S2)
                act.mul(WA[32:64, 2, :], WA[32:64, 2, :], 1.0 / S3).then_inc(scaled, 1)

                def step(b):
                    act.wait_ge(agg_t, b.count(1))
                    if b.reuses(2):
                        act.wait_ge(o_set, b.count(-1))
                    act.activation(aggT[b.j][:, :], ps_a[:, :], ACT.Copy)
                    act.activation(rowT[b.j][:, :], ps_x[:, 0:2 * P], ACT.Copy).then_inc(rowT_set, 1)
                    act.wait_ge(o_set, b.count(1))
                    if b.reuses(2):
                        act.wait_ge(upd_set, b.count(-1))
                    act.activation(sig[b.j][:, :], ps_o[:, 0:96], ACT.Sigmoid).then_inc(sig_set, 1)
                    root(act, stats[b.j][:, 8:9], squares, roots, b, 1, 2)
                    root(act, stats[b.j][:, 18:20], squares, roots, b, 2, 2)
                    act.wait_ge(nrm_t, b.count(1))
                    if b.reuses(2):
                        act.wait_ge(c_set, b.count(-1))
                    act.activation(nrmT[b.j][:, :], ps_n[:, 0:2 * P], ACT.Copy).then_inc(nrmT_set, 1)
                    act.wait_ge(c_set, b.count(1))
                    if b.reuses(2):
                        act.wait_ge(stored[b.j], b.value(16 * PUTS, 16 * PUTS * b.off))
                    act.activation(ts[b.j][:, :], ps_c[:, 0:D], ACT.Copy)
                    act.activation(comb[b.j][:, 0:D], ps_c[:, D:2 * D], ACT.Copy).then_inc(out_set, 1)
                node_steps(act, step)

            @block.vector
            def _(dve):
                for k in two:
                    dve.memset(row[k][:, D:2 * P], 0.0)
                    dve.memset(nrm[k][:, D:2 * P], 0.0)
                    dve.memset(agg[k][:, AGG0:4 * P], 0.0)
                    dve.memset(comb[k][:, D:D + 4], LOW)
                    ins = dve.memset(comb[k][:, D + 4:COMB], 0.0)
                ins.then_inc(blank, 1)
                chain = Linked(dve, chained, 11)

                def step(b):
                    chain.start(b)
                    s, link = stats[b.j], chain.link
                    dve.wait_ge(acc_in[b.j], b.value(32, 32 * (b.off + 1)))
                    if b.reuses(2):
                        dve.wait_ge(agg_t, b.count(-1))
                    dve.tensor_tensor(agg[b.j][:, 0:AGG0], acc[b.j][0][:, :], acc[b.j][1][:, :], ALU.add).then_inc(agg_set, 1)
                    dve.wait_ge(sig_set, b.count(1))
                    yb = y[b.j]
                    dve.tensor_tensor(yb[:, 0:CS], ps_o[:, 0:CS], sig[b.j][:, 0:CS], ALU.mult)
                    link(dve.tensor_tensor(yb[:, CS:D].rearrange("p (c m) -> p c m", c=3),
                                           ps_o[:, 96:192].rearrange("p (c m) -> p c m", c=3),
                                           bcast(sig[b.j][:, CS:96].unsqueeze(1), (P, 3, CV)), ALU.mult))
                    dve.tensor_tensor(yb[:, :], yb[:, :], row[b.j][:, 0:D], ALU.add).then_inc(upd_set, 1)
                    dve.wait_ge(upd_set, b.count(1))
                    if b.reuses(2):
                        dve.wait_ge(stored[b.j], b.value(16 * PUTS, 16 * PUTS * b.off))
                    layernorm(dve, chain, yb[:, :], s, new[b.j][:, :], squares, roots, b, 1, 2).then_inc(new_set, 1)
                    dve.wait_ge(new_set, b.count(1))
                    nb, nv = new[b.j], nrm[b.j]
                    link(dve.bn_stats(s[:, 9:15], nb[:, 0:CS]))
                    link(dve.tensor_tensor(sq[:, :], nb[:, CS:D], nb[:, CS:D], ALU.mult))
                    dve.memset(s[:, 22:23], 0.0)
                    link(dve.bn_aggr(s[:, 15:17], s[:, 9:15]))
                    link(dve.tensor_reduce(s[:, 17:18], sq[:, :], AX.X, ALU.add))
                    dve.tensor_scalar(s[:, 18:19], s[:, 16:17], EPS, None, ALU.add)
                    dve.tensor_scalar(s[:, 19:20], s[:, 17:18], 1.0 / CV, EPS, ALU.mult, ALU.add).then_inc(squares, 1)
                    dve.wait_ge(roots, b.count(2, 2))
                    link(dve.reciprocal(s[:, 18:20], s[:, 18:20]))
                    if b.reuses(2):
                        dve.wait_ge(nrm_t, b.count(-1))
                    dve.tensor_scalar(nv[:, 0:CS], nb[:, 0:CS], s[:, 15:16], s[:, 18:19], ALU.subtract, ALU.mult)
                    link(dve.tensor_scalar(nv[:, CS:D], nb[:, CS:D], s[:, 19:20], None, ALU.mult))
                    link(dve.tensor_tensor(nv[:, 0:D], nv[:, 0:D], gam[:, :], ALU.mult))
                    dve.tensor_tensor(nv[:, 0:CS], nv[:, 0:CS], bet[:, :], ALU.add).then_inc(nrm_set, 1)
                    chain.end()
                node_steps(dve, step)


def edge_layer1(nc, g, A, src_table, combs):
    with Phase(nc, "e1") as ph:
        two = range(2)

        def pair(name, shape):
            return [ph.sb(f"{name}{k}", shape) for k in two]
        WR, WG = ph.sb("WR", [16, 224]), ph.sb("WG", [64, CV])
        WS1, WV1, WS2, WV2 = ph.sb("WS1", [P, 160]), ph.sb("WV1", [P, CV]), ph.sb("WS2", [P, CS]), ph.sb("WV2", [P, CV])
        WvT, w2, adot = ph.sb("WvT", [64, P]), ph.sb("w2", [P, 2]), ph.sb("adot", [P, CS])
        rbf = [ph.sb(f"rbf{k}", [16, P]) for k in range(U)]
        keys = [ph.sb(f"keys{k}", [P, P]) for k in range(U)]
        takes = [[ph.sb(f"take{k}{q}", [P, 1], I32) for k in range(U)] for q in two]
        put = [ph.sb(f"put{k}", [P, 1], I32) for k in range(U)]
        yt = [ph.sb(f"yt{k}", [P, 4]) for k in range(U)]
        srow = [ph.sb(f"srow{k}", [P, D]) for k in range(U)]
        crow = [ph.sb(f"crow{k}", [P, COMB]) for k in range(U)]
        mv, qs, qv = pair("mv", [P, D]), pair("qs", [P, 2 * CS]), pair("qv", [P, 9 * CV])
        m1, m2, m1T, m2T = (pair(n, [P, 4 * P]) for n in ("m1", "m2", "m1T", "m2T"))
        half1, half2 = ph.sb("half1", [P, 3 * CV]), ph.sb("half2", [P, 3 * CV])
        th, sg, vv = pair("th", [P, 96]), pair("sg", [P, 96]), pair("vv", [P, 3 * CV])
        ra, lr, lw = pair("ra", [P, CS]), pair("lr", [P, CS]), pair("lw", [P, CS])
        lg, mx, dif, ex = pair("lg", [P, 4]), pair("mx", [P, 8]), pair("dif", [P, 8]), pair("ex", [P, 8])
        same, apart, hw = pair("same", [P, P]), pair("apart", [P, P]), pair("hw", [P, 4 * HD])
        ps_w = [ph.ps(f"ps_w{k}") for k in two]
        ps_m1, ps_m2, ps_a, ps_h, ps_x, ps_g = (ph.ps(n) for n in ("ps_m1", "ps_m2", "ps_a", "ps_h", "ps_x", "ps_g"))
        wl, made, wready, blank = (ph.sem(n) for n in ("weights", "made", "wready", "blank"))
        keys_in, rbf_in = ph.sems_of("keys_in", U), ph.sems_of("rbf_in", U)
        srow_in, crow_in, written = g.pool_dmas["e1"]
        (take_set, put_set, w_ps, mv_set, prods, sv1_set, dot1a, dot1b, feats1, m1_t, m1T_set, a_ps, th_set, ra_set, sg_set,
         vv_set, lr_set, sv2_set, dot2a, dot2b, feats2, m2_t, m2T_set, h_ps, masks, lw_set, lg_set, x_ps, mx_set, mn_set,
         dif_set, ex_set, kept, hw_set, scaled, g_ps, row_set) = (ph.sem(n) for n in (
             "take_set", "put_set", "w_ps", "mv_set", "prods", "sv1_set", "dot1a", "dot1b", "feats1", "m1_t", "m1T_set",
             "a_ps", "th_set", "ra_set", "sg_set", "vv_set", "lr_set", "sv2_set", "dot2a", "dot2b", "feats2", "m2_t",
             "m2T_set", "h_ps", "masks", "lw_set", "lg_set", "x_ps", "mx_set", "mn_set", "dif_set", "ex_set", "kept",
             "hw_set", "scaled", "g_ps", "row_set"))
        Y0, Y1 = 0, 1

        def y(t, c):
            return yt[t.j][:, c:c + 1]

        with nc.Block() as block:
            @block.sync
            def _(sp):
                for dst, src in ((WR, "w1_rbf"), (WG, "w1_g"), (WS2, "w1_s2"), (WV1, "w1_v1"), (WV2, "w1_v2"), (WvT, "w1_valT"), (w2, "w1_w2")):
                    sp.dma_start(dst[:, :], A[src]).then_inc(wl, 16)
                sp.dma_start(WS1[:, 0:128], A["w1_s1"]).then_inc(wl, 16)
                sp.dma_start(adot[:, :], A["w1_adot"].partition_broadcast(P)).then_inc(wl, 16)

                def step(t):
                    if t.reuses(U):
                        sp.wait_ge(masks, t.count(1 - U))
                    sp.dma_start(keys[t.j][:, :], g.key_rows[1][bass.ds(t.t() * P, P)].partition_broadcast(P)).then_inc(keys_in[t.j], 16)
                    if t.reuses(U):
                        sp.wait_ge(w_ps, t.count(1 - U))
                    sp.dma_start(rbf[t.j][:, :], A["attr16_T"][:, bass.ds(t.t() * P, P)]).then_inc(rbf_in[t.j], 16)
                edge_steps(sp, step, 0)

            @block.gpsimd
            def _(pool):
                def step(s):
                    t = s
                    if t.exists():
                        pool.wait_ge(wl, 16 * 9)
                        pool.wait_ge(take_set, t.count(1))
                        if t.reuses(U):
                            pool.wait_ge(mv_set, t.count(1 - U))
                        pool.indirect_dma_start(out=srow[t.j][:, :], out_offset=None, in_=src_table,
                                                in_offset=bass.IndirectOffsetOnAxis(ap=takes[0][t.j][:, :], axis=0)).then_inc(srow_in[t.j], 16)
                        pool.wait_ge(wl, 16 * 9)
                        if t.reuses(U):
                            pool.wait_ge(written[t.j], t.dma(1))
                        pool.indirect_dma_start(out=crow[t.j][:, :], out_offset=None, in_=combs[t.j][0:NP, :],
                                                in_offset=bass.IndirectOffsetOnAxis(ap=takes[1][t.j][:, :], axis=0)).then_inc(crow_in[t.j], 16)
                    t = s.back(3)
                    if t.exists():
                        pool.wait_ge(wl, 16 * 9)
                        pool.wait_ge(put_set, t.count(1))
                        pool.wait_ge(row_set, t.count(1))
                        pool.indirect_dma_start(out=combs[t.j], out_offset=bass.IndirectOffsetOnAxis(ap=put[t.j][:, :], axis=0),
                                                in_=crow[t.j][:, :], in_offset=None).then_inc(written[t.j], 16)
                edge_steps(pool, step, 3, [(U, c) for c in range(-3, 5)] + [(16, 16 * c) for c in (0, 1)])
                for k in range(U):
                    pool.wait_ge(written[k], 16 * (NT // U))

            @block.tensor
            def _(pe):
                pe.wait_ge(wl, 16 * 9)
                pe.matmul(ps_g[:, 0:CV], WvT[:, :], WG[:, :], start=True, stop=True).then_inc(made, 1)
                pe.wait_ge(wready, 1)
                pe.wait_ge(blank, 1)

                def turn(t, m, ps, ready, half, free, out):
                    pe.wait_ge(ready, t.count(1))
                    pe.wait_ge(half, t.count(1))
                    if t.reuses(1):
                        pe.wait_ge(free, t.count(0))
                    for c in range(4):
                        ins = pe.transpose(ps[:, c * P:(c + 1) * P], m[t.j % 2][:, c * P:(c + 1) * P], g.ident[:, :])
                    ins.then_inc(out, 1)

                def step(s):
                    a, b = s.back(1), s.back(2)
                    if a.exists():
                        k = a.j % 2
                        pe.wait_ge(rbf_in[a.j], a.dma())
                        if a.reuses(2):
                            pe.wait_ge(prods, a.count(-1))
                        pe.matmul(ps_w[k][:, 0:224], rbf[a.j][:, :], WR[:, :], start=True, stop=True).then_inc(w_ps, 1)
                    if b.exists():
                        turn(b, m2, ps_m2, feats2, sv2_set, m2T_set, m2_t)
                        k = b.j % 2
                        pe.wait_ge(lg_set, b.count(1))
                        if b.reuses(1):
                            pe.wait_ge(mx_set, b.count(0))
                        pe.matmul(ps_x[:, :].rearrange("p (h e) -> p h e", h=4), g.ident[:, :],
                                  bcast(apart[k][:, :].unsqueeze(1), (P, 4, P)), start=True, stop=False)
                        for h in range(4):
                            ins = pe.matmul(ps_x[:, h * P:(h + 1) * P], bcast(lg[k][:, h:h + 1], (P, P)), g.ident[:, :],
                                            start=False, stop=h == 3)
                        ins.then_inc(x_ps, 1)
                        pe.wait_ge(m2T_set, b.count(1))
                        if b.reuses(1):
                            pe.wait_ge(hw_set, b.count(0))
                        pe.matmul(ps_h[:, 0:CS], m2T[k][:, 0:P], WS2[:, :], start=True, stop=True)
                        for c in range(3):
                            ins = pe.matmul(ps_h[:, CS + c * CV:CS + (c + 1) * CV], m2T[k][:, (c + 1) * P:(c + 2) * P], WV2[:, :],
                                            start=True, stop=True)
                        ins.then_inc(h_ps, 1)
                    if a.exists():
                        k = a.j % 2
                        turn(a, m1, ps_m1, feats1, sv1_set, m1T_set, m1_t)
                        pe.wait_ge(m1T_set, a.count(1))
                        if a.reuses(1):
                            pe.wait_ge(lr_set, a.count(0))
                        pe.matmul(ps_a[:, 0:160], m1T[k][:, 0:P], WS1[:, :], start=True, stop=True)
                        for c in range(3):
                            ins = pe.matmul(ps_a[:, 160 + c * CV:160 + (c + 1) * CV], m1T[k][:, (c + 1) * P:(c + 2) * P], WV1[:, :],
                                            start=True, stop=True)
                        ins.then_inc(a_ps, 1)
                    if b.exists():
                        k = b.j % 2
                        pe.wait_ge(hw_set, b.count(1))
                        if b.reuses(1):
                            pe.wait_ge(row_set, b.count(0))
                        pe.matmul(ps_g[:, 0:4 * HD], same[k][:, :], hw[k][:, :], start=True, stop=True).then_inc(g_ps, 1)
                edge_steps(pe, step, 2)

            @block.scalar
            def _(act):
                def products(t, m, p0, pv, qvs, out):
                    act.activation(m[:, 0:CS], p0, ACT.Copy, scale=y(t, Y0))
                    for c in range(3):
                        act.activation(m[:, (c + 1) * P:(c + 1) * P + CS], pv, ACT.Copy, scale=y(t, Y1 + c))
                    act.activation(m[:, P:4 * P].rearrange("p (c m) -> p c m", c=3)[:, :, CS:CS + CV],
                                   qvs.rearrange("p (c m) -> p c m", c=3), ACT.Copy, scale=y(t, Y0)).then_inc(out, 1)

                def step(s):
                    a, b = s.back(1), s.back(2)
                    if b.exists():
                        k = b.j % 2
                        act.wait_ge(a_ps, b.count(1))
                        if b.reuses(2):
                            act.wait_ge(lr_set, b.count(-1))
                        act.activation(th[k][:, :], ps_a[:, CS:160], ACT.Tanh, scale=0.5).then_inc(th_set, 1)
                        act.activation(ra[k][:, :], ps_a[:, 0:CS], ACT.Relu, scale=0.8).then_inc(ra_set, 1)
                        act.wait_ge(sg_set, b.count(1))
                        act.wait_ge(vv_set, b.count(1))
                        if b.reuses(2):
                            act.wait_ge(m2_t, b.count(-1))
                        products(b, m2[k], sg[k][:, 0:CS], sg[k][:, 0:CS], vv[k][:, :], sv2_set)
                    if a.exists():
                        k = a.j % 2
                        act.wait_ge(prods, a.count(1))
                        if a.reuses(2):
                            act.wait_ge(m1_t, a.count(-1))
                        products(a, m1[k], qs[k][:, 0:CS], qs[k][:, CS:2 * CS], qv[k][:, 0:3 * CV], sv1_set)
                    if b.exists():
                        k = b.j % 2
                        act.wait_ge(m2_t, b.count(1))
                        if b.reuses(2):
                            act.wait_ge(h_ps, b.count(-1))
                        act.activation(m2T[k][:, :], ps_m2[:, :], ACT.Copy).then_inc(m2T_set, 1)
                    if a.exists():
                        k = a.j % 2
                        act.wait_ge(m1_t, a.count(1))
                        if a.reuses(2):
                            act.wait_ge(a_ps, a.count(-1))
                        act.activation(m1T[k][:, :], ps_m1[:, :], ACT.Copy).then_inc(m1T_set, 1)
                    if b.exists():
                        k = b.j % 2
                        act.wait_ge(dif_set, b.count(1))
                        if b.reuses(2):
                            act.wait_ge(scaled, b.count(-1))
                        act.activation(ex[k][:, :], dif[k][:, :], ACT.Exp).then_inc(ex_set, 1)
                edge_steps(act, step, 2)

            @block.vector
            def _(dve):
                for k in two:
                    dve.memset(m1[k][:, 96:P], 0.0)
                    ins = dve.memset(m2[k][:, 96:P], 0.0)
                ins.then_inc(blank, 1)
                dve.wait_ge(wl, 16 * 9)
                dve.wait_ge(made, 1)
                dve.tensor_copy(WS1[:, 128:160], ps_g[:, 0:CV])
                dve.tensor_scalar(WV1[96:128, :], WV1[96:128, :], 1.0 / S2, None, ALU.mult)
                dve.tensor_scalar(WS2[:, :], WS2[:, :], w2[:, 0:1], None, ALU.mult)
                dve.tensor_scalar(WV2[:, :], WV2[:, :], w2[:, 1:2], None, ALU.mult).then_inc(blank, 1)
                dve.wait_ge(blank, 2)
                dve.tensor_scalar(WS1[64:96, :], WS1[64:96, :], 1.0 / S3, None, ALU.mult)
                dve.tensor_scalar(WS2[64:96, :], WS2[64:96, :], 1.0 / S3, None, ALU.mult)
                dve.tensor_scalar(WV2[96:128, :], WV2[96:128, :], 1.0 / S2, None, ALU.mult).then_inc(wready, 1)

                def products(t, m, half, dot_of, cross_of, first, second, last):
                    dot = m[:, CS:CS + CV]
                    d = [dot_of[:, c * CV:(c + 1) * CV] for c in range(3)]
                    v = [cross_of[:, c * CV:(c + 1) * CV] for c in range(3)]
                    dve.tensor_scalar(dot, d[0], y(t, Y1), None, ALU.mult)
                    for c in range(3):
                        ins = dve.tensor_scalar(half[:, c * CV:(c + 1) * CV], v[(c + 2) % 3], y(t, Y1 + (c + 1) % 3), None, ALU.mult)
                    ins.then_inc(first, 1)
                    dve.wait_ge(first, t.count(1))
                    dve.scalar_tensor_tensor(out=dot, in0=d[1], scalar=y(t, Y1 + 1), in1=dot, op0=ALU.mult, op1=ALU.add).then_inc(second, 1)
                    for c in range(3):
                        at = (c + 1) * P + CS + CV
                        dve.scalar_tensor_tensor(out=m[:, at:at + CV], in0=v[(c + 1) % 3], scalar=y(t, Y1 + (c + 2) % 3),
                                                 in1=half[:, c * CV:(c + 1) * CV], op0=ALU.mult, op1=ALU.subtract)
                    dve.wait_ge(second, t.count(1))
                    dve.scalar_tensor_tensor(out=dot, in0=d[2], scalar=y(t, Y1 + 2), in1=dot, op0=ALU.mult, op1=ALU.add).then_inc(last, 1)

                def step(s):
                    a, b = s.back(1), s.back(2)
                    if s.exists():
                        t = s
                        if t.reuses(U):
                            dve.wait_ge(srow_in[t.j], t.dma(1))
                            dve.wait_ge(crow_in[t.j], t.dma(1))
                        dve.tensor_copy(takes[0][t.j][:, :], g.key_i[0][:, bass.ds(t.t(), 1)])
                        dve.tensor_copy(takes[1][t.j][:, :], g.key_i[1][:, bass.ds(t.t(), 1)]).then_inc(take_set, 1)
                    if a.exists():
                        k = a.j % 2
                        if a.reuses(U):
                            dve.wait_ge(written[a.j], a.dma(1))
                            dve.wait_ge(sv2_set, a.count(1 - U))
                        dve.tensor_copy(yt[a.j][:, :], g.attr4[:, bass.ds(a.t(), 1), :].rearrange("p t c -> p (t c)"))
                        dve.tensor_copy(put[a.j][:, :], g.put_i[1][:, bass.ds(a.t(), 1)]).then_inc(put_set, 1)
                        dve.wait_ge(srow_in[a.j], a.dma())
                        dve.wait_ge(crow_in[a.j], a.dma())
                        dve.tensor_tensor(mv[k][:, :], srow[a.j][:, :], crow[a.j][:, 0:D], ALU.add).then_inc(mv_set, 1)
                    if b.exists():
                        k = b.j % 2
                        dve.wait_ge(th_set, b.count(1))
                        if b.reuses(2):
                            dve.wait_ge(sv2_set, b.count(-1))
                        dve.tensor_scalar(sg[k][:, :], th[k][:, :], 0.5, 0.5, ALU.mult, ALU.add).then_inc(sg_set, 1)
                        dve.wait_ge(ra_set, b.count(1))
                        dve.scalar_tensor_tensor(out=lr[k][:, :], in0=ps_a[:, 0:CS], scalar=0.2, in1=ra[k][:, :], op0=ALU.mult, op1=ALU.add)
                        dve.wait_ge(sg_set, b.count(1))
                        dve.tensor_tensor(vv[k][:, :].rearrange("p (c m) -> p c m", c=3), ps_a[:, 160:256].rearrange("p (c m) -> p c m", c=3),
                                          bcast(sg[k][:, CS:96].unsqueeze(1), (P, 3, CV)), ALU.mult).then_inc(vv_set, 1)
                        dve.wait_ge(vv_set, b.count(1))
                        dve.tensor_tensor(lw[k][:, :], lr[k][:, :], adot[:, :], ALU.mult).then_inc(lr_set, 1)
                    if a.exists():
                        k = a.j % 2
                        dve.wait_ge(w_ps, a.count(1))
                        dve.wait_ge(mv_set, a.count(1))
                        if a.reuses(2):
                            dve.wait_ge(sv1_set, a.count(-1))
                        dve.tensor_tensor(qs[k][:, :].rearrange("p (g m) -> p g m", g=2), ps_w[k][:, 0:2 * CS].rearrange("p (g m) -> p g m", g=2),
                                          bcast(mv[k][:, 0:CS].unsqueeze(1), (P, 2, CS)), ALU.mult)
                        dve.tensor_tensor(qv[k][:, :].rearrange("p (g c m) -> p g c m", g=3, c=3),
                                          bcast(ps_w[k][:, 2 * CS:224].rearrange("p (g m) -> p g m", g=3).unsqueeze(2), (P, 3, 3, CV)),
                                          bcast(mv[k][:, CS:D].rearrange("p (c m) -> p c m", c=3).unsqueeze(1), (P, 3, 3, CV)),
                                          ALU.mult).then_inc(prods, 1)
                    if b.exists():
                        k = b.j % 2
                        if b.reuses(2):
                            dve.wait_ge(m2_t, b.count(-1))
                        products(b, m2[k], half2, vv[k], vv[k], dot2a, dot2b, feats2)
                        dve.wait_ge(keys_in[b.j], b.dma())
                        key = g.key_f[1][:, bass.ds(b.t(), 1)]
                        dve.tensor_scalar(same[k][:, :], keys[b.j][:, :], key, None, ALU.is_equal)
                        dve.tensor_scalar(apart[k][:, :], keys[b.j][:, :], key, LOW, ALU.not_equal, ALU.mult).then_inc(masks, 1)
                        dve.wait_ge(lr_set, b.count(1))
                        dve.tensor_reduce(lg[k][:, :], lw[k][:, :].rearrange("p (h m) -> p h m", h=4), AX.X, ALU.add).then_inc(lg_set, 1)
                    if a.exists():
                        k = a.j % 2
                        dve.wait_ge(prods, a.count(1))
                        if a.reuses(2):
                            dve.wait_ge(m1_t, a.count(-1))
                        products(a, m1[k], half1, qv[k][:, 3 * CV:6 * CV], qv[k][:, 6 * CV:9 * CV], dot1a, dot1b, feats1)
                    if b.exists():
                        k = b.j % 2
                        row = crow[b.j]
                        dve.wait_ge(x_ps, b.count(1))
                        dve.tensor_reduce(mx[k][:, 0:4], ps_x[:, :].rearrange("p (h e) -> p h e", h=4), AX.X, ALU.max).then_inc(mx_set, 1)
                        dve.wait_ge(mx_set, b.count(1))
                        dve.tensor_tensor(mx[k][:, 4:8], row[:, D:D + 4], mx[k][:, 0:4], ALU.max).then_inc(mn_set, 1)
                        dve.wait_ge(mn_set, b.count(1))
                        if b.reuses(2):
                            dve.wait_ge(ex_set, b.count(-1))
                        dve.tensor_tensor(dif[k][:, 0:4], lg[k][:, :], mx[k][:, 4:8], ALU.subtract)
                        dve.tensor_tensor(dif[k][:, 4:8], row[:, D:D + 4], mx[k][:, 4:8], ALU.subtract).then_inc(dif_set, 1)
                        dve.wait_ge(dif_set, b.count(1))
                        dve.tensor_copy(row[:, D:D + 4], mx[k][:, 4:8]).then_inc(kept, 1)
                        dve.wait_ge(ex_set, b.count(1))
                        dve.wait_ge(h_ps, b.count(1))
                        if b.reuses(2):
                            dve.wait_ge(g_ps, b.count(-1))
                        heads = hw[k][:, :].rearrange("p (h m) -> p h m", h=4)
                        e4 = ex[k][:, 0:4]
                        dve.tensor_tensor(heads[:, :, 1:17], ps_h[:, 0:CS].rearrange("p (h m) -> p h m", h=4),
                                          bcast(e4.unsqueeze(2), (P, 4, 16)), ALU.mult)
                        for c in range(3):
                            dve.tensor_tensor(heads[:, :, 17 + 8 * c:25 + 8 * c],
                                              ps_h[:, CS + c * CV:CS + (c + 1) * CV].rearrange("p (h m) -> p h m", h=4),
                                              bcast(e4.unsqueeze(2), (P, 4, 8)), ALU.mult)
                        dve.tensor_copy(heads[:, :, 0:1], e4.unsqueeze(2)).then_inc(hw_set, 1)
                        acc = row[:, D + 4:COMB]
                        dve.tensor_tensor(acc.rearrange("p (h m) -> p h m", h=4), acc.rearrange("p (h m) -> p h m", h=4),
                                          bcast(ex[k][:, 4:8].unsqueeze(2), (P, 4, HD)), ALU.mult).then_inc(scaled, 1)
                        dve.wait_ge(g_ps, b.count(1))
                        dve.wait_ge(scaled, b.count(1))
                        dve.tensor_tensor(acc, acc, ps_g[:, 0:4 * HD], ALU.add).then_inc(row_set, 1)
                edge_steps(dve, step, 2)


def nodes_after_1(nc, g, A, x, combs, x_out, table, scales):
    with Phase(nc, "n2") as ph:
        two = range(2)

        def pair(name, shape):
            return [ph.sb(f"{name}{k}", shape) for k in two]
        WP, WT = ph.sb("WP", [P, 2, D]), ph.sb("WT", [P, 2, CAT])
        runs, row, agg, aggT, new, newT = pair("runs", [P, SM_TABLES, SMW]), pair("row", [P, D]), pair("agg", [P, 2 * P]), pair("aggT", [P, 2 * P]), pair("new", [P, 2 * P]), pair("newT", [P, 2 * P])
        mx, wt, tot, y, stats, tab = pair("mx", [P, 4]), pair("wt", [P, SM_TABLES, 4]), pair("tot", [P, 4 * HD]), pair("y", [P, D]), pair("stats", [P, 24]), pair("tab", [P, CAT])
        ps_a, ps_o, ps_n, ps_c, ps_d = (ph.ps(n) for n in ("ps_a", "ps_o", "ps_n", "ps_c", "ps_d"))
        (wl, ready, blank, dif_set, wt_set, agg_set, agg_t, aggT_set, o_set, upd_set, squares, roots, new_set, new_t, newT_set,
         c_set, tab_set, chained) = (ph.sem(n) for n in (
             "weights", "ready", "blank", "dif_set", "wt_set", "agg_set", "agg_t", "aggT_set", "o_set", "upd_set", "squares",
             "roots", "new_set", "new_t", "newT_set", "c_set", "tab_set", "chained"))
        row_in, runs_in, stored = (ph.sems_of(n, 2) for n in ("row_in", "runs_in", "stored"))
        with nc.Block() as block:
            @block.sync
            def _(sp):
                load_matrix(sp, WP, A["w1_out"], wl)
                load_matrix(sp, WT, A["w2_tab"], wl)

                def store(p):
                    where = bass.ds(p.t() * P, P)
                    sp.wait_ge(new_set, p.count(1))
                    sp.dma_start(x_out[where, :], new[p.j][:, 0:D]).then_inc(stored[p.j], 16)
                    sp.wait_ge(tab_set, p.count(1))
                    sp.dma_start(table[where, :], tab[p.j][:, :]).then_inc(stored[p.j], 16)

                def step(b):
                    where = bass.ds(b.t() * P, P)
                    if b.reuses(2):
                        sp.wait_ge(agg_set, b.count(-1))
                    for k in range(SM_TABLES):
                        sp.dma_start(runs[b.j][:, k, :], combs[k][where, D:COMB]).then_inc(runs_in[b.j], 16)
                    if b.reuses(2):
                        sp.wait_ge(upd_set, b.count(-1))
                    sp.dma_start(row[b.j][:, :], x[where, :]).then_inc(row_in[b.j], 16)
                    p = b.back(1)
                    if p.exists():
                        store(p)
                node_steps(sp, step)
                store(Tile(NB // 2 - 1, 1, 2, NB))
                for k in two:
                    sp.wait_ge(stored[k], 32 * (NB // 2))

            @block.tensor
            def _(pe):
                pe.wait_ge(ready, 1)
                pe.wait_ge(blank, 1)

                def step(b):
                    pe.wait_ge(agg_set, b.count(1))
                    if b.reuses(1):
                        pe.wait_ge(aggT_set, b.count(0))
                    for c in range(2):
                        ins = pe.transpose(ps_a[:, c * P:(c + 1) * P], agg[b.j][:, c * P:(c + 1) * P], g.ident[:, :])
                    ins.then_inc(agg_t, 1)
                    pe.wait_ge(aggT_set, b.count(1))
                    if b.reuses(1):
                        pe.wait_ge(upd_set, b.count(0))
                    for c in range(2):
                        ins = pe.matmul(ps_o[:, 0:D], aggT[b.j][:, c * P:(c + 1) * P], WP[:, c, :], start=c == 0, stop=c == 1)
                    ins.then_inc(o_set, 1)
                    message_rows(pe, g, b, new[b.j], newT[b.j], WT, ps_n, ps_c, ps_d, new_set, new_t, newT_set, c_set, tab_set)
                node_steps(pe, step)

            @block.scalar
            def _(act):
                act.wait_ge(wl, 32)
                scale_columns(act, WT, scales, ready)

                def step(b):
                    act.wait_ge(dif_set, b.count(1))
                    if b.reuses(2):
                        act.wait_ge(agg_set, b.count(-1))
                    act.activation(wt[b.j][:, :, :], wt[b.j][:, :, :], ACT.Exp).then_inc(wt_set, 1)
                    act.wait_ge(agg_t, b.count(1))
                    if b.reuses(2):
                        act.wait_ge(o_set, b.count(-1))
                    act.activation(aggT[b.j][:, :], ps_a[:, 0:2 * P], ACT.Copy).then_inc(aggT_set, 1)
                    root(act, stats[b.j][:, 8:9], squares, roots, b, 1, 1)
                    message_copies(act, b, newT[b.j], tab[b.j], ps_n, ps_c, ps_d, new_t, newT_set, c_set, tab_set, stored[b.j], 2)
                node_steps(act, step)

            @block.vector
            def _(dve):
                for k in two:
                    dve.memset(agg[k][:, D:2 * P], 0.0)
                    ins = dve.memset(new[k][:, D:2 * P], 0.0)
                ins.then_inc(blank, 1)
                chain = Linked(dve, chained, 9)

                def step(b):
                    chain.start(b)
                    link, r, k = chain.link, runs[b.j], b.j
                    dve.wait_ge(runs_in[k], b.value(16 * SM_TABLES, 16 * SM_TABLES * (b.off + 1)))
                    link(dve.tensor_reduce(mx[k][:, :], r[:, :, 0:4].rearrange("p k h -> p h k"), AX.X, ALU.max))
                    dve.tensor_tensor(wt[k][:, :, :], r[:, :, 0:4], bcast(mx[k][:, :].unsqueeze(1), (P, SM_TABLES, 4)), ALU.subtract).then_inc(dif_set, 1)
                    dve.wait_ge(wt_set, b.count(1))
                    for q in range(SM_TABLES):
                        part = r[:, q, 4:SMW].rearrange("p (h m) -> p h m", h=4)
                        ins = dve.tensor_tensor(part, part, bcast(wt[k][:, q, :].unsqueeze(2), (P, 4, HD)), ALU.mult)
                    link(ins)
                    link(dve.tensor_reduce(tot[k][:, :], r[:, :, 4:SMW].rearrange("p k m -> p m k"), AX.X, ALU.add))
                    heads = tot[k][:, :].rearrange("p (h m) -> p h m", h=4)
                    link(dve.tensor_scalar(heads[:, :, 0:1], heads[:, :, 0:1], 1e-16, None, ALU.add))
                    link(dve.reciprocal(heads[:, :, 0:1], heads[:, :, 0:1]))
                    if b.reuses(2):
                        dve.wait_ge(agg_t, b.count(-1))
                    inv = heads[:, :, 0:1]
                    dve.tensor_tensor(agg[k][:, 0:CS].rearrange("p (h m) -> p h m", h=4), heads[:, :, 1:17], bcast(inv, (P, 4, 16)), ALU.mult)
                    for c in range(3):
                        ins = dve.tensor_tensor(agg[k][:, CS + c * CV:CS + (c + 1) * CV].rearrange("p (h m) -> p h m", h=4),
                                                heads[:, :, 17 + 8 * c:25 + 8 * c], bcast(inv, (P, 4, 8)), ALU.mult)
                    ins.then_inc(agg_set, 1)
                    dve.wait_ge(o_set, b.count(1))
                    dve.wait_ge(row_in[k], b.dma())
                    dve.scalar_tensor_tensor(out=y[k][:, :], in0=row[k][:, :], scalar=2.0, in1=ps_o[:, 0:D], op0=ALU.mult, op1=ALU.add).then_inc(upd_set, 1)
                    dve.wait_ge(upd_set, b.count(1))
                    if b.reuses(2):
                        dve.wait_ge(new_t, b.count(-1))
                        dve.wait_ge(stored[k], b.value(32, 32 * b.off))
                    layernorm(dve, chain, y[k][:, :], stats[k], new[k][:, 0:D], squares, roots, b, 1, 1).then_inc(new_set, 1)
                    link(dve.memset(stats[k][:, 21:22], 0.0))
                    chain.end()
                node_steps(dve, step)


def scale_columns(act, W, scales, ready):
    for lo, hi, value in scales:
        ins = act.mul(W[:, :, lo:hi], W[:, :, lo:hi], value)
    ins.then_inc(ready, 1)


def message_rows(pe, g, b, new, newT, WT, ps_n, ps_c, ps_d, new_set, new_t, newT_set, c_set, tab_set):
    pe.wait_ge(new_set, b.count(1))
    if b.reuses(1):
        pe.wait_ge(newT_set, b.count(0))
    for c in range(2):
        ins = pe.transpose(ps_n[:, c * P:(c + 1) * P], new[:, c * P:(c + 1) * P], g.ident[:, :])
    ins.then_inc(new_t, 1)
    pe.wait_ge(newT_set, b.count(1))
    if b.reuses(1):
        pe.wait_ge(tab_set, b.count(0))
    for ps, lo, hi in ((ps_c, 0, 2 * D), (ps_d, 2 * D, CAT)):
        for c in range(2):
            ins = pe.matmul(ps[:, 0:hi - lo], newT[:, c * P:(c + 1) * P], WT[:, c, lo:hi], start=c == 0, stop=c == 1)
    ins.then_inc(c_set, 1)


def message_copies(act, b, newT, tab, ps_n, ps_c, ps_d, new_t, newT_set, c_set, tab_set, stored, puts):
    act.wait_ge(new_t, b.count(1))
    if b.reuses(2):
        act.wait_ge(c_set, b.count(-1))
    act.activation(newT[:, :], ps_n[:, 0:2 * P], ACT.Copy).then_inc(newT_set, 1)
    act.wait_ge(c_set, b.count(1))
    if b.reuses(2):
        act.wait_ge(stored, b.value(16 * puts, 16 * puts * b.off))
    act.activation(tab[:, 0:2 * D], ps_c[:, 0:2 * D], ACT.Copy)
    act.activation(tab[:, 2 * D:CAT], ps_d[:, 0:CAT - 2 * D], ACT.Copy).then_inc(tab_set, 1)


def edge_messages(nc, g, name, table, accs):
    with Phase(nc, name) as ph:
        two = range(2)
        keys = [ph.sb(f"keys{k}", [P, P]) for k in range(U)]
        take = [ph.sb(f"take{k}", [P, 1], I32) for k in range(U)]
        put = [ph.sb(f"put{k}", [P, 1], I32) for k in range(U)]
        row = [ph.sb(f"row{k}", [P, CAT]) for k in range(U)]
        same = [ph.sb(f"same{k}", [P, P]) for k in two]
        q = [ph.sb(f"q{k}", [P, D]) for k in two]
        total = [ph.sb(f"total{k}", [P, D]) for k in range(U)]
        ps_o = [ph.ps(f"ps_o{k}") for k in two]
        keys_in = ph.sems_of("keys_in", U)
        row_in, added = g.pool_dmas[name]
        take_set, put_set, same_set, base, term0, term1, feats, sums_ps, total_set, started = (ph.sem(n) for n in (
            "take_set", "put_set", "same_set", "base", "term0", "term1", "feats", "sums_ps", "total_set", "started"))
        AE, C0, DD = D, 2 * D, 2 * D + 3 * CS

        def attr(t, c):
            return g.attr4[:, bass.ds(t.t(), 1), c]

        with nc.Block() as block:
            @block.sync
            def _(sp):
                def step(t):
                    if t.reuses(U):
                        sp.wait_ge(same_set, t.count(1 - U))
                    sp.dma_start(keys[t.j][:, :], g.key_rows[0][bass.ds(t.t() * P, P)].partition_broadcast(P)).then_inc(keys_in[t.j], 16)
                edge_steps(sp, step, 0)

            @block.gpsimd
            def _(pool):
                def step(s):
                    if s.exists():
                        t = s
                        pool.wait_ge(started, 1)
                        pool.wait_ge(take_set, t.count(1))
                        if t.reuses(U):
                            pool.wait_ge(feats, t.count(1 - U))
                        pool.indirect_dma_start(out=row[t.j][:, :], out_offset=None, in_=table,
                                                in_offset=bass.IndirectOffsetOnAxis(ap=take[t.j][:, :], axis=0)).then_inc(row_in[t.j], 16)
                    t = s.back(3)
                    if t.exists():
                        pool.wait_ge(started, 1)
                        pool.wait_ge(total_set, t.count(1))
                        pool.wait_ge(put_set, t.count(1))
                        if t.reuses(ADD_TABLES):
                            pool.wait_ge(added[(t.j - ADD_TABLES) % U], t.back(ADD_TABLES).dma())
                        pool.indirect_dma_start(out=accs[t.j % ADD_TABLES], out_offset=bass.IndirectOffsetOnAxis(ap=put[t.j][:, :], axis=0),
                                                in_=total[t.j][:, :], in_offset=None, compute_op=ALU.add).then_inc(added[t.j], 16)
                edge_steps(pool, step, 3, [(U, c) for c in range(-6, 5)] + [(16, 16 * c) for c in (-1, 0, 1)])
                for k in range(U):
                    pool.wait_ge(added[k], 16 * (NT // U))

            @block.tensor
            def _(pe):
                def step(s):
                    t = s.back(2)
                    if t.exists():
                        b = t.j % 2
                        pe.wait_ge(feats, t.count(1))
                        if t.reuses(2):
                            pe.wait_ge(total_set, t.count(-1))
                        pe.matmul(ps_o[b][:, 0:D], same[b][:, :], q[b][:, :], start=True, stop=True).then_inc(sums_ps, 1)
                edge_steps(pe, step, 2)

            @block.scalar
            def _(act):
                def step(s):
                    t = s.back(2)
                    if t.exists():
                        b = t.j % 2
                        act.wait_ge(sums_ps, t.count(1))
                        if t.reuses(U):
                            act.wait_ge(added[t.j], t.dma(1))
                        act.activation(total[t.j][:, :], ps_o[b][:, 0:D], ACT.Copy).then_inc(total_set, 1)
                edge_steps(act, step, 2)

            @block.vector
            def _(dve):
                dve.memset(q[0][:, :], 0.0).then_inc(started, 1)

                def step(s):
                    if s.exists():
                        t = s
                        if t.reuses(U):
                            dve.wait_ge(row_in[t.j], t.dma(1))
                        dve.tensor_copy(take[t.j][:, :], g.key_i[1][:, bass.ds(t.t(), 1)]).then_inc(take_set, 1)
                    t = s.back(2)
                    if not t.exists():
                        return
                    b = t.j % 2
                    qb, r = q[b], row[t.j]
                    if t.reuses(U):
                        dve.wait_ge(added[t.j], t.dma(1))
                    dve.tensor_copy(put[t.j][:, :], g.put_i[0][:, bass.ds(t.t(), 1)]).then_inc(put_set, 1)
                    dve.wait_ge(row_in[t.j], t.dma())
                    if t.reuses(2):
                        dve.wait_ge(sums_ps, t.count(-1))
                    dve.scalar_tensor_tensor(out=qb[:, :], in0=r[:, AE:AE + D], scalar=attr(t, 3), in1=r[:, 0:D],
                                             op0=ALU.mult, op1=ALU.add).then_inc(base, 1)
                    dve.wait_ge(keys_in[t.j], t.dma())
                    dve.tensor_scalar(same[b][:, :], keys[t.j][:, :], g.key_f[0][:, bass.ds(t.t(), 1)], None, ALU.is_equal).then_inc(same_set, 1)
                    dve.wait_ge(base, t.count(1))

                    def scalars(c):
                        return dve.scalar_tensor_tensor(out=qb[:, 0:CS], in0=r[:, C0 + c * CS:C0 + (c + 1) * CS], scalar=attr(t, c),
                                                        in1=qb[:, 0:CS], op0=ALU.mult, op1=ALU.add)

                    def vectors(c):
                        at = CS + c * CV
                        return dve.scalar_tensor_tensor(out=qb[:, at:at + CV], in0=r[:, DD:DD + CV], scalar=attr(t, c),
                                                        in1=qb[:, at:at + CV], op0=ALU.mult, op1=ALU.add)
                    scalars(0).then_inc(term0, 1)
                    vectors(0)
                    vectors(1)
                    dve.wait_ge(term0, t.count(1))
                    scalars(1).then_inc(term1, 1)
                    vectors(2)
                    dve.wait_ge(term1, t.count(1))
                    scalars(2).then_inc(feats, 1)
                edge_steps(dve, step, 2)


def nodes_update(nc, g, A, name, mats, x, accs, x_out, table, next_tab, scales, next_scales):
    W0, W1 = 5 * 1024, 4 * 1024
    CH = 512
    with Phase(nc, name) as ph:
        two = range(2)

        def pair(name, shape):
            return [ph.sb(f"{name}{k}", shape) for k in two]
        WA0, WA1, WL = ph.sb("WA0", [CS, W0]), ph.sb("WA1", [CV, W1]), ph.sb("WL", [P, 2, D])
        WT = ph.sb("WT", [P, 2, CAT]) if table is not None else None
        row, agg, part = pair("row", [P, 2 * P]), pair("agg", [P, D]), [pair(f"acc{a}_", [P, D]) for a in range(ADD_TABLES)]
        a0T, a1T, rowT = pair("a0T", [CS, P]), pair("a1T", [CV, 3 * P]), pair("rowT", [P, 2 * P])
        prod = [ph.sb(f"prod{k}", [P, CH]) for k in range(4)]
        r0, r1 = pair("r0", [P, 4, CS]), pair("r1", [P, 2, 3 * CV])
        y, stats, new, newT = pair("y", [P, D]), pair("stats", [P, 24]), pair("new", [P, 2 * P]), pair("newT", [P, 2 * P])
        tab = pair("tab", [P, CAT]) if table is not None else None
        ps_z = [ph.ps(f"ps_z{k}") for k in range(4)]
        ps_t, ps_l, ps_c, ps_d = (ph.ps(n) for n in ("ps_t", "ps_l", "ps_c", "ps_d"))
        (wl, ready, blank, agg_set, turned, turned_sb, z_ps, multiplied, reduced, l_ps, upd_set, squares, roots, new_set, new_t,
         newT_set, c_set, tab_set, chained, linked) = (ph.sem(n) for n in (
             "weights", "ready", "blank", "agg_set", "turned", "turned_sb", "z_ps", "multiplied", "reduced", "l_ps", "upd_set",
             "squares", "roots", "new_set", "new_t", "newT_set", "c_set", "tab_set", "chained", "linked"))
        row_in, acc_in, stored = (ph.sems_of(n, 2) for n in ("row_in", "acc_in", "stored"))
        puts = 1 if table is None else 2

        chunks = []
        for c in range(8):
            chunks.append((None, c * CH, [((0, CS), ("r0", 0, 8 * c))], 8, CS))
        for c in two:
            chunks.append((None, 4096 + c * CH, [((CS + k * CV, CS + (k + 1) * CV), ("r1", 1, k * CV + 16 * c)) for k in range(3)], 16, CV))
        for k in range(3):
            for c in range(4):
                chunks.append((k, c * CH, [((CS + k * CV, CS + (k + 1) * CV), ("r0", 1 + k, 16 * c))], 16, CV))
            for c in range(4):
                chunks.append((k, 2048 + c * CH, [((0, CS), ("r1", 0, k * CV + 8 * c))], 8, CS))
        NCH = len(chunks)
        last_mult = []
        for ch in chunks:
            last_mult.append((last_mult[-1] if last_mult else 0) + len(ch[2]))
        NM = last_mult[-1]

        def bank(b, n):
            return (NCH * b.j + n) % 4
        assert 2 * NCH % 4 == 0

        with nc.Block() as block:
            @block.sync
            def _(sp):
                sp.dma_start(WA0[:, :], A[mats + "_a0"]).then_inc(wl, 16)
                sp.dma_start(WA1[:, :], A[mats + "_a1"]).then_inc(wl, 16)
                load_matrix(sp, WL, A[mats + "_lin"], wl)
                if table is not None:
                    load_matrix(sp, WT, A[next_tab], wl)

                def store(p):
                    where = bass.ds(p.t() * P, P)
                    sp.wait_ge(new_set, p.count(1))
                    sp.dma_start(x_out[where, :], new[p.j][:, 0:D]).then_inc(stored[p.j], 16)
                    if table is not None:
                        sp.wait_ge(tab_set, p.count(1))
                        sp.dma_start(table[where, :], tab[p.j][:, :]).then_inc(stored[p.j], 16)

                def step(b):
                    where = bass.ds(b.t() * P, P)
                    if b.reuses(2):
                        sp.wait_ge(agg_set, b.count(-1))
                    for a in range(ADD_TABLES):
                        sp.dma_start(part[a][b.j][:, :], accs[a][where, :]).then_inc(acc_in[b.j], 16)
                    if b.reuses(2):
                        sp.wait_ge(upd_set, b.count(-1))
                    sp.dma_start(row[b.j][:, 0:D], x[where, :]).then_inc(row_in[b.j], 16)
                    p = b.back(1)
                    if p.exists():
                        store(p)
                node_steps(sp, step)
                store(Tile(NB // 2 - 1, 1, 2, NB))
                for k in two:
                    sp.wait_ge(stored[k], 16 * puts * (NB // 2))

            @block.tensor
            def _(pe):
                pe.wait_ge(ready, 1)
                pe.wait_ge(blank, 1)

                def step(b):
                    k = b.j
                    pe.wait_ge(agg_set, b.count(1))
                    pe.wait_ge(row_in[k], b.dma())
                    if b.reuses(1):
                        pe.wait_ge(turned_sb, b.count(0))
                        pe.wait_ge(upd_set, b.count(0))
                    for c in two:
                        pe.transpose(ps_l[:, 256 + c * P:256 + (c + 1) * P], row[k][:, c * P:(c + 1) * P], g.ident[:, :])
                    pe.transpose(ps_t[0:CS, 0:P], agg[k][:, 0:CS], g.ident[:, :])
                    for c in range(3):
                        ins = pe.transpose(ps_t[0:CV, (c + 1) * P:(c + 2) * P], agg[k][:, CS + c * CV:CS + (c + 1) * CV], g.ident[:, :])
                    ins.then_inc(turned, 1)
                    pe.wait_ge(turned_sb, b.count(1))
                    for n, (comp, col, _, _, _) in enumerate(chunks):
                        if n >= 4:
                            pe.wait_ge(multiplied, b.count(last_mult[n - 4], NM))
                        elif b.reuses(1):
                            pe.wait_ge(multiplied, b.count(last_mult[NCH + n - 4] - NM, NM))
                        if comp is None:
                            lhs, rhs = a0T[k][:, :], WA0[:, col:col + CH]
                        else:
                            lhs, rhs = a1T[k][:, comp * P:(comp + 1) * P], WA1[:, col:col + CH]
                        pe.matmul(ps_z[bank(b, n)][:, :], lhs, rhs, start=True, stop=True).then_inc(z_ps, 1)
                    for c in two:
                        ins = pe.matmul(ps_l[:, 0:D], rowT[k][:, c * P:(c + 1) * P], WL[:, c, :], start=c == 0, stop=c == 1)
                    ins.then_inc(l_ps, 1)
                    if table is not None:
                        message_rows(pe, g, b, new[k], newT[k], WT, ps_t, ps_c, ps_d, new_set, new_t, newT_set, c_set, tab_set)
                node_steps(pe, step)

            @block.scalar
            def _(act):
                act.wait_ge(wl, 64 if table is not None else 48)
                s_ss, s_vv, s_sv, s_vs, l_s, l_v = scales
                act.mul(WA0[:, 0:4096], WA0[:, 0:4096], s_ss)
                act.mul(WA0[:, 4096:W0], WA0[:, 4096:W0], s_vs)
                act.mul(WA1[:, 0:2048], WA1[:, 0:2048], s_vv)
                act.mul(WA1[:, 2048:W1], WA1[:, 2048:W1], s_sv)
                if table is not None:
                    scale_columns(act, WT, next_scales, chained)
                act.mul(WL[:, :, 0:CS], WL[:, :, 0:CS], l_s)
                act.mul(WL[:, :, CS:D], WL[:, :, CS:D], l_v).then_inc(ready, 1)

                def step(b):
                    k = b.j
                    act.wait_ge(turned, b.count(1))
                    if b.reuses(2):
                        act.wait_ge(l_ps, b.count(-1))
                    act.activation(a0T[k][:, :], ps_t[0:CS, 0:P], ACT.Copy)
                    act.activation(a1T[k][:, :], ps_t[0:CV, P:4 * P], ACT.Copy)
                    act.activation(rowT[k][:, :], ps_l[:, 256:512], ACT.Copy).then_inc(turned_sb, 1)
                    root(act, stats[k][:, 8:9], squares, roots, b, 1, 1)
                    if table is not None:
                        message_copies(act, b, newT[k], tab[k], ps_t, ps_c, ps_d, new_t, newT_set, c_set, tab_set, stored[k], puts)
                node_steps(act, step)

            @block.vector
            def _(dve):
                for k in two:
                    dve.memset(row[k][:, D:2 * P], 0.0)
                    ins = dve.memset(new[k][:, D:2 * P], 0.0)
                ins.then_inc(blank, 1)
                links = Linked(dve, linked, 6)

                def step(b):
                    k = b.j
                    links.start(b)
                    dve.wait_ge(acc_in[k], b.value(32, 32 * (b.off + 1)))
                    if b.reuses(2):
                        dve.wait_ge(turned, b.count(-1))
                    dve.tensor_tensor(agg[k][:, :], part[0][k][:, :], part[1][k][:, :], ALU.add).then_inc(agg_set, 1)
                    dve.wait_ge(row_in[k], b.dma())
                    todo = []

                    def reduce(m, dst, w, u):
                        dve.wait_ge(multiplied, b.count(m, NM))
                        which, slot, at = dst
                        out = (r0 if which == "r0" else r1)[k][:, slot, at:at + w]
                        dve.tensor_reduce(out, prod[(m - 1) % 4][:, :].rearrange("p (w u) -> p w u", w=w), AX.X, ALU.add).then_inc(reduced, 1)
                    m = 0
                    for n, (comp, col, uses, w, u) in enumerate(chunks):
                        dve.wait_ge(z_ps, b.count(n + 1, NCH))
                        for (lo, hi), dst in uses:
                            m += 1
                            if m > 4:
                                dve.wait_ge(reduced, b.count(m - 4, NM))
                            elif b.reuses(1):
                                dve.wait_ge(reduced, b.count(0, NM))
                            z = ps_z[bank(b, n)][:, :].rearrange("p (w u) -> p w u", w=w)
                            dve.tensor_tensor(prod[(m - 1) % 4][:, :].rearrange("p (w u) -> p w u", w=w), z,
                                              bcast(row[k][:, lo:hi].unsqueeze(1), (P, w, u)), ALU.mult).then_inc(multiplied, 1)
                            todo.append((m, dst, w, u))
                            if len(todo) > 1:
                                reduce(*todo.pop(0))
                    reduce(*todo.pop(0))
                    dve.wait_ge(reduced, b.count(NM, NM))
                    dve.tensor_reduce(y[k][:, 0:CS], r0[k][:, :, :].rearrange("p a w -> p w a"), AX.X, ALU.add)
                    links.link(dve.tensor_tensor(y[k][:, CS:D], r1[k][:, 0, :], r1[k][:, 1, :], ALU.add))
                    links.link(dve.scalar_tensor_tensor(out=y[k][:, :], in0=row[k][:, 0:D], scalar=2.0, in1=y[k][:, :], op0=ALU.mult, op1=ALU.add))
                    dve.wait_ge(l_ps, b.count(1))
                    dve.tensor_tensor(y[k][:, :], y[k][:, :], ps_l[:, 0:D], ALU.add).then_inc(upd_set, 1)
                    dve.wait_ge(upd_set, b.count(1))
                    if b.reuses(2):
                        if table is not None:
                            dve.wait_ge(new_t, b.count(-1))
                        dve.wait_ge(stored[k], b.value(16 * puts, 16 * puts * b.off))
                    layernorm(dve, links, y[k][:, :], stats[k], new[k][:, 0:D], squares, roots, b, 1, 1).then_inc(new_set, 1)
                    links.link(dve.memset(stats[k][:, 21:22], 0.0))
                    links.end()
                node_steps(dve, step)


class Globals:
    pass


def build(nc, A, out):
    def dram(name, shape):
        return nc.dram_tensor(name, shape, F32).ap()
    with ExitStack() as ctx:
        def sb(name, shape, dtype=F32):
            return ctx.enter_context(nc.sbuf_tensor(name, shape, dtype))
        g = Globals()
        g.key_i = [sb(f"key_i{k}", [P, NT], I32) for k in range(2)]
        g.key_f = [sb(f"key_f{k}", [P, NT]) for k in range(2)]
        g.put_i = [sb(f"put_i{k}", [P, NT], I32) for k in range(2)]
        g.attr4 = sb("attr4", [P, NT, 4])
        g.attr3 = sb("attr3", [P, NT, 3])
        g.ident, g.before, g.waste = sb("ident", [P, P]), sb("before", [P, P]), sb("waste", [P, 1])
        g.pool_dmas = {phase: [[ctx.enter_context(nc.semaphore(f"{phase}_{stream}{k}")) for k in range(U)] for stream in streams]
                       for phase, streams in (("e0", ("row_in", "added")), ("e1", ("srow_in", "crow_in", "written")),
                                              ("e2", ("row_in", "added")), ("e3", ("row_in", "added")))}
        g.key_rows = [dram(f"key_rows{k}", [EP]) for k in range(2)]
        table0, src_table = dram("table0", [NP, D]), dram("src_table", [NP, D])
        accs0 = [dram(f"accs0{k}", [ACC_ROWS, AGG0]) for k in range(ADD_TABLES)]
        combs = [dram(f"comb{k}", [ACC_ROWS, COMB]) for k in range(SM_TABLES)]
        accs2, accs3 = ([dram(f"{n}{k}", [ACC_ROWS, D]) for k in range(ADD_TABLES)] for n in ("accs2", "accs3"))
        x1, x2, x3 = (dram(n, [NP, D]) for n in ("x1", "x2", "x3"))
        table2, table3 = dram("table2", [NP, CAT]), dram("table3", [NP, CAT])
        prepare(nc, g, A, accs0 + accs2 + accs3)
        first_table(nc, g, A, A["x"], table0)
        edge_layer0(nc, g, A, table0, accs0)
        nodes_after_0(nc, g, A, A["x"], accs0, x1, src_table, combs)
        edge_layer1(nc, g, A, src_table, combs)
        c = 96.0 ** -0.5
        l_s, l_v = 64.0 ** -0.5, 32.0 ** -0.5
        nodes_after_1(nc, g, A, x1, combs, x2, table2,
                      [(0, 64, l_s), (64, 160, l_v), (160, 320, c), (320, 512, c / S3), (512, 544, c)])
        edge_messages(nc, g, "e2", table2, accs2)
        f0, f1 = 5120.0 ** -0.5, 4096.0 ** -0.5
        nodes_update(nc, g, A, "n3", "w2", x2, accs2, x3, table3, "w3_tab", (f0, f0 / S3, f1, f1, l_s, l_v),
                     [(0, 64, l_s), (64, 160, l_v), (160, 224, l_s), (224, 320, l_v), (320, 512, l_v / S3), (512, 544, l_s)])
        edge_messages(nc, g, "e3", table3, accs3)
        h = 2048.0 ** -0.5
        nodes_update(nc, g, A, "n4", "w3", x3, accs3, out, None, None, (1.0 / 64, 1.0 / 32 / S3, h, h, l_s, l_v), None)


def layout_rest(a, f, g):
    import numpy as np
    a["w1_rbf"], a["w1_g"], a["w1_v1"], a["w1_v2"] = g["W_rbf"], g["Wg"], g["Wv_val"], g["Wv_vlin"]
    a["w1_s1"] = _blocks(P, 128, [(0, 0, g["W_alpha"]), (0, 64, g["Ws_val"])])
    a["w1_s2"] = _blocks(P, CS, [(0, 0, g["Ws_vlin"])])
    a["w1_valT"] = _blocks(64, P, [(0, 0, g["Ws_val"].T)])
    w2 = np.zeros((P, 2), np.float32)
    w2[:96, 0] = np.concatenate([g["w2_ss"], g["w2_vv0"]])
    w2[:, 1] = np.concatenate([g["w2_sv"], g["w2_vs"], g["w2_vv1"]])
    a["w1_w2"] = w2
    a["w1_adot"] = g["alpha_dot"].reshape(-1)
    a["w1_out"] = _blocks(256, D, [(0, 0, g["Wps"])] + _per_component(64, 64, g["Wpv"]))

    def messages(lin_s, lin_v, ss, sv, vs, vv):
        return _blocks(256, CAT, [(0, 0, lin_s), (0, 160, ss), (0, 512, sv)] + _per_component(64, 64, lin_v)
                       + _per_component(64, 224, vs) + _per_component(64, 320, vv))

    def update(name, ss, sv, vs, vv, lin_s, lin_v):
        def behind(w):
            return w.transpose(1, 2, 0).reshape(w.shape[1], -1)
        a[name + "_a0"] = np.concatenate([behind(ss), behind(vs)], axis=1)
        a[name + "_a1"] = np.concatenate([behind(vv), behind(sv)], axis=1)
        a[name + "_lin"] = _blocks(256, D, [(0, 0, lin_s)] + _per_component(64, 64, lin_v))
    m = {k[7:]: v for k, v in f.items() if k.startswith("L2_gnn_")}
    a["w2_tab"] = messages(m["lm0"], m["lm1"], m["wm000"][:, 0], m["wm011"][:, 0], m["wm101"][:, 0], m["wm110"][:, 0])
    update("w2", m["wu000"], m["wu011"], m["wu101"], m["wu110"], m["lu0"], m["lu1"])
    m = {k[7:]: v for k, v in f.items() if k.startswith("L3_gnn_")}
    a["w3_tab"] = messages(m["Lm_s"], m["Lm_v"], m["Wm_ss"], m["Wm_sv"], m["Wm_vs"], m["Wm_vv"])
    update("w3", m["Wu_ss"], m["Wu_sv"], m["Wu_vs"], m["Wu_vv"], m["Lu_s"], m["Lu_v"])



def _blocks(rows, cols, blocks):
    import numpy as np
    m = np.zeros((rows, cols), np.float32)
    for r, c, b in blocks:
        m[r:r + b.shape[0], c:c + b.shape[1]] = b
    return m


def _per_component(r, c, b, dr=None, dc=None):
    return [(r + k * (dr or b.shape[0]), c + k * (dc or b.shape[1]), b) for k in range(3)]


def layout(inputs):
    import numpy as np
    f = {k: np.asarray(v) for k, v in inputs.items()}

    def rows(a, n):
        out = np.zeros((n,) + a.shape[1:], a.dtype)
        out[:a.shape[0]] = a
        return out

    x = f["x"]
    node = np.zeros((NP, D), np.float32)
    node[:N, :CS] = x[:, :CS]
    node[:N, CS:] = x[:, CS:].reshape(N, CV, 3).transpose(0, 2, 1).reshape(N, 3 * CV)
    a = {"x": node}
    for key in ("src", "dst"):
        k = np.full((EP,), N, np.int32)
        k[:E] = f[key]
        a[key + "_row"] = k.reshape(P, NT)
        a[key + "_col"] = k.reshape(NT, P).T

    def edges(name, width):
        e = np.ones((EP, width), np.float32)
        e[:E] = f[name]
        return e
    a["attr3"] = edges("edge_attr_3", 3).reshape(NT, P, 3).transpose(1, 0, 2)
    a["attr4"] = edges("edge_attr_4", 4).reshape(NT, P, 4).transpose(1, 0, 2)
    a["attr64_T"] = edges("edge_attr_64", 64).T
    a["attr16_T"] = edges("edge_attr_16", 16).T
    g = {k[7:]: v for k, v in f.items() if k.startswith("L0_gnn_")}
    a["w0_nl"] = _blocks(256, D, [(0, 0, g["W_nl0"])] + _per_component(64, 64, g["W_nl1"]))
    a["w0_fc1"], a["w0_fc2"] = _blocks(64, P, [(0, 0, g["W_fc1"])]), g["W_fc2"]
    wv, ws = g["W_out_v"], g["W_out_s"]
    a["w0_agg"] = _blocks(512, 192, _per_component(0, 96, wv[:64]) + _per_component(192, 96, wv[96:])
                          + [(288, 0, ws[64:]), (320, 0, ws[:64])] + _per_component(384, 96, wv[64:96]))
    a["w0_skip"] = _blocks(256, 192, [(0, 0, g["W_skip0"])] + _per_component(64, 96, g["W_skip1"]))
    g = {k[7:]: v for k, v in f.items() if k.startswith("L1_gnn_")}
    a["w1_tab"] = _blocks(256, 2 * D, [(0, 0, g["Ws_src"]), (0, D, g["Ws_dst"])]
                          + _per_component(64, 64, g["Wv_src"]) + _per_component(64, D + 64, g["Wv_dst"]))
    a["gamma1"] = np.concatenate([g["gamma_s"]] + 3 * [g["gamma_v"]])
    a["beta1"] = g["beta_s"]
    layout_rest(a, f, g)
    return {k: np.ascontiguousarray(v) for k, v in a.items()}


def kernel(**inputs):
    import numpy as np
    import concourse.bacc as bacc
    from concourse.bass_utils import run_bass_kernel_spmd as run

    arrays = layout(inputs)
    nc = bacc.Bacc("TRN2", target_bir_lowering=False, num_devices=1)
    A = {k: nc.dram_tensor(f"in_{k}", a.shape, mybir.dt.from_np(a.dtype), kind="ExternalInput").ap() for k, a in arrays.items()}
    out = nc.dram_tensor("out_x", (NP, D), F32, kind="ExternalOutput").ap()
    build(nc, A, out)
    r = run(nc, [{f"in_{k}": a for k, a in arrays.items()}], core_ids=[0])
    got = np.asarray(r.results[0]["out_x"])[:N]
    return np.concatenate([got[:, :CS], got[:, CS:].reshape(N, 3, CV).transpose(0, 2, 1).reshape(N, 3 * CV)], axis=1)
```

```python
from contextlib import ExitStack

import concourse.bass as bass
from concourse import mybir

F32 = mybir.dt.float32
I32 = mybir.dt.int32
BF16 = mybir.dt.bfloat16
ALU = mybir.AluOpType
ACT = mybir.ActivationFunctionType
AX = mybir.AxisListType

P = 128
N, E = 6250, 206250
NB = 2 * -(-N // (2 * P))
NP = NB * P
NT = 12 * -(-E // (12 * P))
EP = NT * P
U = 4
TURNS = NT // U
assert TURNS * U == NT
CS, CV = 64, 32
D = CS + 3 * CV
ACC_ROWS = NP + P
ADD_TABLES = 2
SM_TABLES = 6
AGG0 = 480
CAT = 2 * D + 3 * CS + CV
HD = 41
SMW = 4 + 4 * HD
COMB = D + SMW
LOW = -1.0e30
EPS = 1e-5
S3 = 3.0 ** 0.5
S2 = 2.0 ** 0.5


class Tile:

    def __init__(self, i, j, unroll, number, off=0, held=None):
        self.i, self.j, self.unroll, self.number, self.off, self.held = i, j, unroll, number, off, held

    def back(self, k):
        off, j = divmod(self.j - k, self.unroll)
        return Tile(self.i, j, self.unroll, self.number, self.off + off, self.held)

    def value(self, a, c):
        if self.held is not None:
            return self.held[(a, c)]
        return self.i * a + c

    def first_turns(self):
        return isinstance(self.i, int)

    def exists(self):
        return not self.first_turns() or 0 <= self.unroll * (self.i + self.off) + self.j < self.number

    def t(self):
        return self.i * self.unroll + (self.unroll * self.off + self.j)

    def count(self, more=0, each=1):
        return self.value(each * self.unroll, each * (self.unroll * self.off + self.j) + more)

    def dma(self, before=0):
        return self.value(16, 16 * (self.off + 1 - before))

    def reuses(self, slots):
        return not self.first_turns() or self.unroll * (self.i + self.off) + self.j >= slots


def run_steps(eng, step, lag, unroll, number, held=()):
    turns = number // unroll
    assert turns * unroll == number and lag <= unroll
    for j in range(unroll):
        step(Tile(0, j, unroll, number))
    with eng.Fori(1, turns) as i:
        registers = {(a, c): eng.snap(eng.to_reg(i * a + c)) for a, c in held} or None
        for j in range(unroll):
            step(Tile(i, j, unroll, number, 0, registers))
    for j in range(lag):
        step(Tile(turns, j, unroll, number))


def edge_steps(eng, step, lag, held=()):
    run_steps(eng, step, lag, U, NT, held)


def node_steps(eng, step):
    run_steps(eng, step, 0, 2, NB)


def bcast(ap, shape):
    return ap.to_broadcast(list(shape))


class Phase:

    def __init__(self, nc, name):
        self.nc, self.name, self.ctx, self.sems = nc, name, ExitStack(), []

    def __enter__(self):
        self.ctx.__enter__()
        return self

    def __exit__(self, *args):
        if args[0] is None:
            sems = self.sems
            with self.nc.Block() as block:
                @block.gpsimd
                def _(pool):
                    for s in sems:
                        pool.sem_clear(s)
        return self.ctx.__exit__(*args)

    def sb(self, name, shape, dtype=F32):
        return self.ctx.enter_context(self.nc.sbuf_tensor(f"{self.name}_{name}", shape, dtype))

    def ps(self, name, shape=(P, 512)):
        return self.ctx.enter_context(self.nc.psum_tensor(f"{self.name}_{name}", list(shape), F32))

    def sem(self, name):
        s = self.ctx.enter_context(self.nc.semaphore(f"{self.name}_{name}"))
        self.sems.append(s)
        return s

    def sems_of(self, name, n):
        return [self.sem(f"{name}{k}") for k in range(n)]


def prepare(nc, g, A, tables):
    with Phase(nc, "prep") as ph:
        rows = [ph.sb(f"row_i{k}", [P, NT], I32) for k in range(2)]
        rows_f = [ph.sb(f"row_f{k}", [P, NT]) for k in range(2)]
        square = ph.sb("square", [P, NT, 3])
        norm = ph.sb("norm", [P, NT])
        waste_i = ph.sb("waste_i", [P, 1], I32)
        ones = ph.sb("ones", [P, P])
        zeros = ph.sb("zeros", [P, AGG0])
        loaded, made, unit, stored, consts = (ph.sem(n) for n in ("loaded", "cast", "unit", "stored", "consts"))
        rooted, zeroed, cleared = (ph.sem(n) for n in ("rooted", "zeroed", "cleared"))
        with nc.Block() as block:
            @block.sync
            def _(sp):
                for dst, src in ((g.key_i[0], A["src_col"]), (g.key_i[1], A["dst_col"]),
                                 (rows[0], A["src_row"]), (rows[1], A["dst_row"])):
                    sp.dma_start(dst[:, :], src).then_inc(loaded, 16)
                sp.dma_start(g.attr3[:, :, :], A["attr3"]).then_inc(loaded, 16)
                sp.dma_start(g.attr4[:, :, :], A["attr4"]).then_inc(loaded, 16)
                sp.wait_ge(zeroed, 1)
                for table in tables:
                    width = table.shape[1]
                    sp.dma_start(table.rearrange("(b p) w -> p b w", p=P),
                                 bcast(zeros[:, 0:width].unsqueeze(1), (P, ACC_ROWS // P, width))).then_inc(cleared, 16)
                sp.wait_ge(cleared, 16 * len(tables))
                for k in range(2):
                    sp.wait_ge(made, k + 1)
                    sp.dma_start(g.key_rows[k].rearrange("(p t) -> p t", p=P), rows_f[k][:, :]).then_inc(stored, 16)
                sp.wait_ge(stored, 32)

            @block.gpsimd
            def _(pool):
                pool.memset(ones[:, :], 1.0).then_inc(consts, 1)
                pool.iota(waste_i[:, :], pattern=[[0, 1]], base=NP, channel_multiplier=1).then_inc(consts, 1)
                pool.wait_ge(consts, 1)
                pool.affine_select(out=g.ident[:, :], in_=ones[:, :], compare_op=ALU.is_equal, fill=0.0, base=0,
                                   pattern=[[-1, P]], channel_multiplier=1).then_inc(consts, 1)
                pool.affine_select(out=g.before[:, :], in_=ones[:, :], compare_op=ALU.is_gt, fill=0.0, base=0,
                                   pattern=[[-1, P]], channel_multiplier=1).then_inc(consts, 1)

            @block.vector
            def _(dve):
                dve.memset(zeros[:, :], 0.0).then_inc(zeroed, 1)
                dve.wait_ge(loaded, 96)
                for k in range(2):
                    dve.tensor_copy(rows_f[k][:, :], rows[k][:, :]).then_inc(made, 1)
                for k in range(2):
                    dve.tensor_copy(g.key_f[k][:, :], g.key_i[k][:, :])
                dve.wait_ge(consts, 2)
                dve.tensor_copy(g.waste[:, :], waste_i[:, :])
                dve.tensor_tensor(square[:, :, :], g.attr3[:, :, :], g.attr3[:, :, :], ALU.mult).then_inc(unit, 1)
                dve.wait_ge(unit, 1)
                dve.tensor_reduce(norm[:, :], square[:, :, :], AX.X, ALU.add).then_inc(unit, 1)
                dve.wait_ge(rooted, 1)
                dve.reciprocal(norm[:, :], norm[:, :]).then_inc(unit, 1)
                dve.wait_ge(unit, 3)
                dve.scalar_tensor_tensor(out=g.attr3[:, :, :], in0=g.attr3[:, :, :], scalar=S3,
                                         in1=bcast(norm[:, :].unsqueeze(2), (P, NT, 3)),
                                         op0=ALU.mult, op1=ALU.mult).then_inc(unit, 1)
                dve.wait_ge(unit, 4)

            @block.scalar
            def _(act):
                act.wait_ge(unit, 2)
                act.activation(norm[:, :], norm[:, :], ACT.Sqrt).then_inc(rooted, 1)

    with Phase(nc, "firsts") as ph:
        W = 6
        keys = [[ph.sb(f"keys{k}{q}", [P, W * P]) for q in range(2)] for k in range(2)]
        earlier = [ph.sb(f"earlier{k}", [P, NT]) for k in range(2)]
        hit = [ph.sb(f"hit{q}", [P, 2 * W * P]) for q in range(2)]
        work = [ph.sb(f"work{k}", [P, NT]) for k in range(2)]
        landed = [ph.sems_of(f"landed{k}", 2) for k in range(2)]
        counted, final = ph.sem("counted"), ph.sem("final")
        with nc.Block() as block:
            @block.sync
            def _(sp):
                def load(s):
                    if s.reuses(2):
                        sp.wait_ge(counted, s.count(-1))
                    for k in range(2):
                        src = g.key_rows[k][bass.ds(s.t() * (W * P), W * P)].partition_broadcast(P)
                        sp.dma_start(keys[k][s.j][:, :], src).then_inc(landed[k][s.j], 16)
                run_steps(sp, load, 0, 2, NT // W)

            @block.vector
            def _(dve):
                def count(s):
                    if s.reuses(2):
                        dve.wait_ge(counted, s.count(-1))
                    for k in range(2):
                        dve.wait_ge(landed[k][s.j], s.dma())
                        for w in range(W):
                            t = s.t() * W + w
                            place = (W * k + w) * P
                            ins = dve.scalar_tensor_tensor(
                                out=hit[s.j][:, place:place + P], in0=keys[k][s.j][:, w * P:(w + 1) * P],
                                scalar=g.key_f[k][:, bass.ds(t, 1)], in1=g.before[:, :],
                                op0=ALU.is_equal, op1=ALU.mult, accum_out=earlier[k][:, bass.ds(t, 1)])
                    ins.then_inc(counted, 1)
                run_steps(dve, count, 0, 2, NT // W)
                dve.wait_ge(counted, NT // W)
                n = 0

                def then(ins):
                    nonlocal n
                    n += 1
                    ins.then_inc(final, 1)
                    dve.wait_ge(final, n)
                for k in range(2):
                    then(dve.tensor_scalar(earlier[k][:, :], earlier[k][:, :], 1.0, None, ALU.min))
                    then(dve.tensor_scalar(work[k][:, :], g.key_f[k][:, :], -1.0, g.waste[:, 0:1], ALU.mult, ALU.add))
                    then(dve.tensor_tensor(work[k][:, :], work[k][:, :], earlier[k][:, :], ALU.mult))
                    then(dve.tensor_tensor(g.put_i[k][:, :], work[k][:, :], g.key_f[k][:, :], ALU.add))



def edge_layer0(nc, g, A, table, accs):
    with Phase(nc, "e0") as ph:
        W1, W2 = ph.sb("W1", [64, P]), ph.sb("W2", [64, 224])
        feat = [ph.sb(f"feat{k}", [64, P]) for k in range(U)]
        keys = [ph.sb(f"keys{k}", [P, P]) for k in range(U)]
        take = [ph.sb(f"take{k}", [P, 1], I32) for k in range(U)]
        put = [ph.sb(f"put{k}", [P, 1], I32) for k in range(U)]
        row = [ph.sb(f"row{k}", [P, D]) for k in range(U)]
        hid = [ph.sb(f"hid{k}", [64, P]) for k in range(2)]
        same = [ph.sb(f"same{k}", [P, P]) for k in range(2)]
        QW = 1024
        q = [ph.sb(f"q{k}", [P, QW]) for k in range(2)]
        part = ph.sb("part", [P, 3 * CV])
        total = [ph.sb(f"total{k}", [P, AGG0]) for k in range(U)]
        ps_h, ps_w, ps_o = ([ph.ps(f"{n}{k}") for k in range(2)] for n in ("ps_h", "ps_w", "ps_o"))
        wl = ph.sem("weights")
        keys_in, feat_in = ph.sems_of("keys_in", U), ph.sems_of("feat_in", U)
        row_in, added = g.pool_dmas["e0"]
        (take_set, put_set, same_set, prods, dot0, dot1, halves, feats, hid_ps, hid_set, w_ps, sv_set,
         sums_ps, total_set) = (ph.sem(n) for n in (
             "take_set", "put_set", "same_set", "prods", "dot0", "dot1", "halves", "feats", "hid_ps",
             "hid_set", "w_ps", "sv_set", "sums_ps", "total_set"))
        SV, CR, DOT, S0, V2, T1 = 0, 192, 288, 320, 384, 672

        with nc.Block() as block:
            @block.sync
            def _(sp):
                sp.dma_start(W1[:, :], A["w0_fc1"]).then_inc(wl, 16)
                sp.dma_start(W2[:, :], A["w0_fc2"]).then_inc(wl, 16)

                def step(t):
                    if not t.exists():
                        return
                    if t.reuses(U):
                        sp.wait_ge(same_set, t.count(1 - U))
                    sp.dma_start(keys[t.j][:, :], g.key_rows[0][bass.ds(t.t() * P, P)].partition_broadcast(P)).then_inc(keys_in[t.j], 16)
                    if t.reuses(U):
                        sp.wait_ge(hid_ps, t.count(1 - U))
                    sp.dma_start(feat[t.j][:, :], A["attr64_T"][:, bass.ds(t.t() * P, P)]).then_inc(feat_in[t.j], 16)
                edge_steps(sp, step, 0)

            @block.gpsimd
            def _(pool):
                def step(s):
                    if s.exists():
                        t = s
                        pool.wait_ge(wl, 32)
                        pool.wait_ge(take_set, t.count(1))
                        if t.reuses(U):
                            pool.wait_ge(prods, t.count(1 - U))
                        pool.indirect_dma_start(out=row[t.j][:, :], out_offset=None, in_=table,
                                                in_offset=bass.IndirectOffsetOnAxis(ap=take[t.j][:, :], axis=0)).then_inc(row_in[t.j], 16)
                    t = s.back(4)
                    if t.exists():
                        pool.wait_ge(wl, 32)
                        pool.wait_ge(total_set, t.count(1))
                        pool.wait_ge(put_set, t.count(1))
                        if t.reuses(ADD_TABLES):
                            pool.wait_ge(added[(t.j - ADD_TABLES) % U], t.back(ADD_TABLES).dma())
                        pool.indirect_dma_start(out=accs[t.j % ADD_TABLES], out_offset=bass.IndirectOffsetOnAxis(ap=put[t.j][:, :], axis=0),
                                                in_=total[t.j][:, :], in_offset=None, compute_op=ALU.add).then_inc(added[t.j], 16)
                edge_steps(pool, step, 4, [(U, c) for c in range(-6, 5)] + [(16, 16 * c) for c in (-1, 0, 1)])
                for k in range(U):
                    pool.wait_ge(added[k], 16 * TURNS)

            @block.tensor
            def _(pe):
                pe.wait_ge(wl, 32)

                def step(s):
                    t = s.back(1)
                    if t.exists():
                        b = t.j % 2
                        pe.wait_ge(feat_in[t.j], t.dma())
                        if t.reuses(2):
                            pe.wait_ge(hid_set, t.count(-1))
                        pe.matmul(ps_h[b][:, 0:P], W1[:, :], feat[t.j][:, :], start=True, stop=True).then_inc(hid_ps, 1)
                    t = s.back(3)
                    if t.exists():
                        b = t.j % 2
                        pe.wait_ge(feats, t.count(1))
                        pe.wait_ge(sv_set, t.count(1))
                        if t.reuses(2):
                            pe.wait_ge(total_set, t.count(-1))
                        pe.matmul(ps_o[b][:, 0:AGG0], same[b][:, :], q[b][:, 0:AGG0], start=True, stop=True).then_inc(sums_ps, 1)
                    t = s.back(1)
                    if t.exists():
                        b = t.j % 2
                        pe.wait_ge(hid_set, t.count(1))
                        if t.reuses(2):
                            pe.wait_ge(prods, t.count(-1))
                        pe.matmul(ps_w[b][:, 0:224], hid[b][:, :], W2[:, :], start=True, stop=True).then_inc(w_ps, 1)
                edge_steps(pe, step, 3)

            @block.scalar
            def _(act):
                def step(s):
                    t = s.back(1)
                    if t.exists():
                        b = t.j % 2
                        act.wait_ge(hid_ps, t.count(1))
                        if t.reuses(2):
                            act.wait_ge(w_ps, t.count(-1))
                        act.activation(hid[b][:, :], ps_h[b][0:64, 0:P], ACT.Relu).then_inc(hid_set, 1)
                    t = s.back(2)
                    if t.exists():
                        b = t.j % 2
                        act.wait_ge(prods, t.count(1))
                        if t.reuses(2):
                            act.wait_ge(sums_ps, t.count(-1))
                        for c in range(3):
                            ins = act.activation(q[b][:, SV + CS * c:SV + CS * (c + 1)], q[b][:, T1:T1 + CS], ACT.Copy,
                                                 scale=g.attr3[:, bass.ds(t.t(), 1), c])
                        ins.then_inc(sv_set, 1)
                    t = s.back(3)
                    if t.exists():
                        b = t.j % 2
                        act.wait_ge(sums_ps, t.count(1))
                        if t.reuses(U):
                            act.wait_ge(added[t.j], t.dma(1))
                        act.activation(total[t.j][:, :], ps_o[b][:, 0:AGG0], ACT.Copy).then_inc(total_set, 1)
                edge_steps(act, step, 3)

            @block.vector
            def _(dve):
                def step(s):
                    if s.exists():
                        t = s
                        if t.reuses(U):
                            dve.wait_ge(row_in[t.j], t.dma(1))
                        dve.tensor_copy(take[t.j][:, :], g.key_i[1][:, bass.ds(t.t(), 1)]).then_inc(take_set, 1)
                    t = s.back(2)
                    if not t.exists():
                        return
                    b = t.j % 2
                    qb, w = q[b], ps_w[b]
                    sh = [g.attr3[:, bass.ds(t.t(), 1), c] for c in range(3)]
                    if t.reuses(U):
                        dve.wait_ge(added[t.j], t.dma(1))
                    dve.tensor_copy(put[t.j][:, :], g.put_i[0][:, bass.ds(t.t(), 1)]).then_inc(put_set, 1)
                    dve.wait_ge(row_in[t.j], t.dma())
                    dve.wait_ge(w_ps, t.count(1))
                    if t.reuses(2):
                        dve.wait_ge(sums_ps, t.count(-1))
                        dve.wait_ge(sv_set, t.count(-1))
                    dve.tensor_tensor(qb[:, S0:S0 + 2 * (T1 - S0)].rearrange("p (a c) -> p a c", a=2)[:, :, 0:CS],
                                      w[:, 0:2 * CS].rearrange("p (a c) -> p a c", a=2),
                                      bcast(row[t.j][:, 0:CS].unsqueeze(1), (P, 2, CS)), ALU.mult)
                    dve.tensor_tensor(qb[:, V2:V2 + 9 * CV].rearrange("p (g c m) -> p g c m", g=3, c=3),
                                      bcast(w[:, 2 * CS:2 * CS + 3 * CV].rearrange("p (g m) -> p g m", g=3).unsqueeze(2), (P, 3, 3, CV)),
                                      bcast(row[t.j][:, CS:D].rearrange("p (c m) -> p c m", c=3).unsqueeze(1), (P, 3, 3, CV)),
                                      ALU.mult).then_inc(prods, 1)
                    dve.wait_ge(keys_in[t.j], t.dma())
                    dve.tensor_scalar(same[b][:, :], keys[t.j][:, :], g.key_f[0][:, bass.ds(t.t(), 1)], None, ALU.is_equal).then_inc(same_set, 1)
                    q3 = [qb[:, V2 + (3 + c) * CV:V2 + (4 + c) * CV] for c in range(3)]
                    q4 = [qb[:, V2 + (6 + c) * CV:V2 + (7 + c) * CV] for c in range(3)]
                    dot = qb[:, DOT:DOT + CV]
                    dve.wait_ge(prods, t.count(1))
                    dve.tensor_scalar(dot, q3[0], sh[0], None, ALU.mult).then_inc(dot0, 1)
                    for c in range(3):
                        ins = dve.tensor_scalar(part[:, c * CV:(c + 1) * CV], q4[(c + 2) % 3], sh[(c + 1) % 3], None, ALU.mult)
                    ins.then_inc(halves, 1)
                    dve.wait_ge(dot0, t.count(1))
                    dve.scalar_tensor_tensor(out=dot, in0=q3[1], scalar=sh[1], in1=dot, op0=ALU.mult, op1=ALU.add).then_inc(dot1, 1)
                    dve.wait_ge(halves, t.count(1))
                    for c in range(3):
                        dve.scalar_tensor_tensor(out=qb[:, CR + c * CV:CR + (c + 1) * CV], in0=q4[(c + 1) % 3], scalar=sh[(c + 2) % 3],
                                                 in1=part[:, c * CV:(c + 1) * CV], op0=ALU.mult, op1=ALU.subtract)
                    dve.wait_ge(dot1, t.count(1))
                    dve.scalar_tensor_tensor(out=dot, in0=q3[2], scalar=sh[2], in1=dot, op0=ALU.mult, op1=ALU.add).then_inc(feats, 1)
                edge_steps(dve, step, 2)


class Linked:

    def __init__(self, eng, sem, each):
        self.eng, self.sem, self.each, self.k = eng, sem, each, 0

    def start(self, item):
        self.item, self.k = item, 0

    def link(self, ins):
        self.k += 1
        ins.then_inc(self.sem, 1)
        self.eng.wait_ge(self.sem, self.item.count(self.k, self.each))

    def end(self):
        assert self.k == self.each, self.k


def layernorm(dve, chain, y, stats, out, squares, roots, item, nth, each):
    chain.link(dve.bn_stats(stats[:, 0:6], y))
    dve.memset(stats[:, 22:23], 0.0)
    chain.link(dve.bn_aggr(stats[:, 6:8], stats[:, 0:6]))
    dve.tensor_scalar(stats[:, 8:9], stats[:, 7:8], EPS, None, ALU.add).then_inc(squares, 1)
    dve.wait_ge(roots, item.count(nth, each))
    chain.link(dve.reciprocal(stats[:, 8:9], stats[:, 8:9]))
    return dve.tensor_scalar(out, y, stats[:, 6:7], stats[:, 8:9], ALU.subtract, ALU.mult)


def root(act, at, squares, roots, item, nth, each):
    act.wait_ge(squares, item.count(nth, each))
    act.activation(at, at, ACT.Sqrt).then_inc(roots, 1)


def load_matrix(eng, dst, src, sem):
    eng.dma_start(dst[:, :, :], src.rearrange("(k p) n -> p k n", p=P)).then_inc(sem, 16)


def first_table(nc, g, A, x, table):
    with Phase(nc, "n0") as ph:
        W = ph.sb("W", [P, 2, D])
        row = [ph.sb(f"row{k}", [P, 2 * P]) for k in range(2)]
        rowT = [ph.sb(f"rowT{k}", [P, 2 * P]) for k in range(2)]
        out = [ph.sb(f"out{k}", [P, D]) for k in range(2)]
        ps_t, ps_o = [ph.ps(f"ps_t{k}") for k in range(2)], [ph.ps(f"ps_o{k}") for k in range(2)]
        wl, blank, turned, turned_sb, ps_set, out_set = (ph.sem(n) for n in (
            "weights", "blank", "turned", "turned_sb", "ps_set", "out_set"))
        row_in, stored = ph.sems_of("row_in", 2), ph.sems_of("stored", 2)
        with nc.Block() as block:
            @block.sync
            def _(sp):
                load_matrix(sp, W, A["w0_nl"], wl)

                def step(b):
                    if b.reuses(2):
                        sp.wait_ge(turned, b.count(-1))
                    sp.dma_start(row[b.j][:, 0:D], x[bass.ds(b.t() * P, P), :]).then_inc(row_in[b.j], 16)
                    p = b.back(1)
                    if p.exists():
                        sp.wait_ge(out_set, p.count(1))
                        sp.dma_start(table[bass.ds(p.t() * P, P), :], out[p.j][:, :]).then_inc(stored[p.j], 16)
                run_steps(sp, step, 0, 2, NB)
                last = Tile(NB // 2 - 1, 1, 2, NB)
                sp.wait_ge(out_set, last.count(1))
                sp.dma_start(table[(NB - 1) * P:NB * P, :], out[1][:, :]).then_inc(stored[1], 16)
                for k in range(2):
                    sp.wait_ge(stored[k], 16 * (NB // 2))

            @block.tensor
            def _(pe):
                pe.wait_ge(wl, 16)
                pe.wait_ge(blank, 1)

                def step(b):
                    pe.wait_ge(row_in[b.j], b.dma())
                    if b.reuses(2):
                        pe.wait_ge(turned_sb, b.count(-1))
                    pe.transpose(ps_t[b.j][:, 0:P], row[b.j][:, 0:P], g.ident[:, :])
                    pe.transpose(ps_t[b.j][:, P:2 * P], row[b.j][:, P:2 * P], g.ident[:, :]).then_inc(turned, 1)
                    pe.wait_ge(turned_sb, b.count(1))
                    if b.reuses(2):
                        pe.wait_ge(out_set, b.count(-1))
                    for c in range(2):
                        ins = pe.matmul(ps_o[b.j][:, 0:D], rowT[b.j][:, c * P:(c + 1) * P], W[:, c, :], start=c == 0, stop=c == 1)
                    ins.then_inc(ps_set, 1)
                node_steps(pe, step)

            @block.scalar
            def _(act):
                def step(b):
                    act.wait_ge(turned, b.count(1))
                    if b.reuses(2):
                        act.wait_ge(ps_set, b.count(-1))
                    act.activation(rowT[b.j][:, :], ps_t[b.j][:, 0:2 * P], ACT.Copy).then_inc(turned_sb, 1)
                node_steps(act, step)

            @block.vector
            def _(dve):
                dve.memset(row[0][:, D:2 * P], 0.0)
                dve.memset(row[1][:, D:2 * P], 0.0).then_inc(blank, 1)

                def step(b):
                    dve.wait_ge(ps_set, b.count(1))
                    if b.reuses(2):
                        dve.wait_ge(stored[b.j], b.dma(1))
                    dve.tensor_copy(out[b.j][:, :], ps_o[b.j][:, 0:D]).then_inc(out_set, 1)
                node_steps(dve, step)


def nodes_after_0(nc, g, A, x, accs, x_out, src_table, combs):
    with Phase(nc, "n1") as ph:
        WA, WX, WT = ph.sb("WA", [P, 4, 192]), ph.sb("WX", [P, 2, 192]), ph.sb("WT", [P, 2, 2 * D])
        gam, bet = ph.sb("gam", [P, D]), ph.sb("bet", [P, CS])
        two = range(2)
        acc = [[ph.sb(f"acc{k}{a}", [P, AGG0]) for a in range(ADD_TABLES)] for k in two]
        row = [ph.sb(f"row{k}", [P, 2 * P]) for k in two]
        agg = [ph.sb(f"agg{k}", [P, 4 * P]) for k in two]
        aggT = [ph.sb(f"aggT{k}", [P, 4 * P]) for k in two]
        rowT = [ph.sb(f"rowT{k}", [P, 2 * P]) for k in two]
        sig = [ph.sb(f"sig{k}", [P, 96]) for k in two]
        y = [ph.sb(f"y{k}", [P, D]) for k in two]
        new = [ph.sb(f"new{k}", [P, D]) for k in two]
        nrm = [ph.sb(f"nrm{k}", [P, 2 * P]) for k in two]
        nrmT = [ph.sb(f"nrmT{k}", [P, 2 * P]) for k in two]
        stats = [ph.sb(f"stats{k}", [P, 24]) for k in two]
        ts = [ph.sb(f"ts{k}", [P, D]) for k in two]
        comb = [ph.sb(f"comb{k}", [P, COMB]) for k in two]
        sq = ph.sb("sq", [P, 3 * CV])
        ps_a, ps_x, ps_o, ps_n, ps_c = (ph.ps(n) for n in ("ps_a", "ps_x", "ps_o", "ps_n", "ps_c"))
        names = ("weights", "scaled", "blank", "agg_set", "agg_t", "aggT_set", "rowT_set", "o_set", "sig_set",
                 "chain", "new_set", "nrm_set", "nrm_t", "nrmT_set", "c_set", "out_set", "upd_set", "squares", "roots")
        (wl, scaled, blank, agg_set, agg_t, aggT_set, rowT_set, o_set, sig_set, chained, new_set, nrm_set,
         nrm_t, nrmT_set, c_set, out_set, upd_set, squares, roots) = (ph.sem(n) for n in names)
        row_in, acc_in, stored = ph.sems_of("row_in", 2), ph.sems_of("acc_in", 2), ph.sems_of("stored", 2)
        PUTS = 2 + SM_TABLES
        with nc.Block() as block:
            @block.sync
            def _(sp):
                load_matrix(sp, WA, A["w0_agg"], wl)
                load_matrix(sp, WX, A["w0_skip"], wl)
                load_matrix(sp, WT, A["w1_tab"], wl)
                sp.dma_start(gam[:, :], A["gamma1"].partition_broadcast(P)).then_inc(wl, 16)
                sp.dma_start(bet[:, :], A["beta1"].partition_broadcast(P)).then_inc(wl, 16)

                def store(p):
                    where = bass.ds(p.t() * P, P)
                    sp.wait_ge(new_set, p.count(1))
                    sp.dma_start(x_out[where, :], new[p.j][:, :]).then_inc(stored[p.j], 16)
                    sp.wait_ge(out_set, p.count(1))
                    sp.dma_start(src_table[where, :], ts[p.j][:, :]).then_inc(stored[p.j], 16)
                    for k in range(SM_TABLES):
                        sp.dma_start(combs[k][where, :], comb[p.j][:, :]).then_inc(stored[p.j], 16)

                def step(b):
                    where = bass.ds(b.t() * P, P)
                    if b.reuses(2):
                        sp.wait_ge(agg_set, b.count(-1))
                    for a in range(ADD_TABLES):
                        sp.dma_start(acc[b.j][a][:, :], accs[a][where, :]).then_inc(acc_in[b.j], 16)
                    if b.reuses(2):
                        sp.wait_ge(upd_set, b.count(-1))
                    sp.dma_start(row[b.j][:, 0:D], x[where, :]).then_inc(row_in[b.j], 16)
                    p = b.back(1)
                    if p.exists():
                        store(p)
                node_steps(sp, step)
                store(Tile(NB // 2 - 1, 1, 2, NB))
                for k in two:
                    sp.wait_ge(stored[k], 16 * PUTS * (NB // 2))

            @block.tensor
            def _(pe):
                pe.wait_ge(scaled, 1)
                pe.wait_ge(blank, 1)

                def step(b):
                    pe.wait_ge(agg_set, b.count(1))
                    pe.wait_ge(row_in[b.j], b.dma())
                    if b.reuses(2):
                        pe.wait_ge(rowT_set, b.count(0))
                    for c in range(4):
                        pe.transpose(ps_a[:, c * P:(c + 1) * P], agg[b.j][:, c * P:(c + 1) * P], g.ident[:, :])
                    for c in range(2):
                        ins = pe.transpose(ps_x[:, c * P:(c + 1) * P], row[b.j][:, c * P:(c + 1) * P], g.ident[:, :])
                    ins.then_inc(agg_t, 1)
                    pe.wait_ge(rowT_set, b.count(1))
                    if b.reuses(2):
                        pe.wait_ge(upd_set, b.count(0))
                    for c in range(4):
                        pe.matmul(ps_o[:, 0:192], aggT[b.j][:, c * P:(c + 1) * P], WA[:, c, :], start=c == 0, stop=False)
                    for c in range(2):
                        ins = pe.matmul(ps_o[:, 0:192], rowT[b.j][:, c * P:(c + 1) * P], WX[:, c, :], start=False, stop=c == 1)
                    ins.then_inc(o_set, 1)
                    pe.wait_ge(nrm_set, b.count(1))
                    if b.reuses(2):
                        pe.wait_ge(nrmT_set, b.count(0))
                    for c in range(2):
                        ins = pe.transpose(ps_n[:, c * P:(c + 1) * P], nrm[b.j][:, c * P:(c + 1) * P], g.ident[:, :])
                    ins.then_inc(nrm_t, 1)
                    pe.wait_ge(nrmT_set, b.count(1))
                    if b.reuses(2):
                        pe.wait_ge(out_set, b.count(0))
                    for c in range(2):
                        ins = pe.matmul(ps_c[:, 0:2 * D], nrmT[b.j][:, c * P:(c + 1) * P], WT[:, c, :], start=c == 0, stop=c == 1)
                    ins.then_inc(c_set, 1)
                node_steps(pe, step)

            @block.scalar
            def _(act):
                act.wait_ge(wl, 16 * 5)
                act.mul(WA[:, :, :], WA[:, :, :], 1.0 / 32.0).then_inc(scaled, 1)
                act.wait_ge(scaled, 1)
                act.mul(WA[64:128, 1, :], WA[64:128, 1, :], 1.0 / S2)
                act.mul(WA[0:32, 2, :], WA[0:32, 2, :], 1.0 / S2)
                act.mul(WA[32:64, 2, :], WA[32:64, 2, :], 1.0 / S3).then_inc(scaled, 1)

                def step(b):
                    act.wait_ge(agg_t, b.count(1))
                    if b.reuses(2):
                        act.wait_ge(o_set, b.count(-1))
                    act.activation(aggT[b.j][:, :], ps_a[:, :], ACT.Copy)
                    act.activation(rowT[b.j][:, :], ps_x[:, 0:2 * P], ACT.Copy).then_inc(rowT_set, 1)
                    act.wait_ge(o_set, b.count(1))
                    if b.reuses(2):
                        act.wait_ge(upd_set, b.count(-1))
                    act.activation(sig[b.j][:, :], ps_o[:, 0:96], ACT.Sigmoid).then_inc(sig_set, 1)
                    root(act, stats[b.j][:, 8:9], squares, roots, b, 1, 2)
                    root(act, stats[b.j][:, 18:20], squares, roots, b, 2, 2)
                    act.wait_ge(nrm_t, b.count(1))
                    if b.reuses(2):
                        act.wait_ge(c_set, b.count(-1))
                    act.activation(nrmT[b.j][:, :], ps_n[:, 0:2 * P], ACT.Copy).then_inc(nrmT_set, 1)
                    act.wait_ge(c_set, b.count(1))
                    if b.reuses(2):
                        act.wait_ge(stored[b.j], b.value(16 * PUTS, 16 * PUTS * b.off))
                    act.activation(ts[b.j][:, :], ps_c[:, 0:D], ACT.Copy)
                    act.activation(comb[b.j][:, 0:D], ps_c[:, D:2 * D], ACT.Copy).then_inc(out_set, 1)
                node_steps(act, step)

            @block.vector
            def _(dve):
                for k in two:
                    dve.memset(row[k][:, D:2 * P], 0.0)
                    dve.memset(nrm[k][:, D:2 * P], 0.0)
                    dve.memset(agg[k][:, AGG0:4 * P], 0.0)
                    dve.memset(comb[k][:, D:D + 4], LOW)
                    ins = dve.memset(comb[k][:, D + 4:COMB], 0.0)
                ins.then_inc(blank, 1)
                chain = Linked(dve, chained, 11)

                def step(b):
                    chain.start(b)
                    s, link = stats[b.j], chain.link
                    dve.wait_ge(acc_in[b.j], b.value(32, 32 * (b.off + 1)))
                    if b.reuses(2):
                        dve.wait_ge(agg_t, b.count(-1))
                    dve.tensor_tensor(agg[b.j][:, 0:AGG0], acc[b.j][0][:, :], acc[b.j][1][:, :], ALU.add).then_inc(agg_set, 1)
                    dve.wait_ge(sig_set, b.count(1))
                    yb = y[b.j]
                    dve.tensor_tensor(yb[:, 0:CS], ps_o[:, 0:CS], sig[b.j][:, 0:CS], ALU.mult)
                    link(dve.tensor_tensor(yb[:, CS:D].rearrange("p (c m) -> p c m", c=3),
                                           ps_o[:, 96:192].rearrange("p (c m) -> p c m", c=3),
                                           bcast(sig[b.j][:, CS:96].unsqueeze(1), (P, 3, CV)), ALU.mult))
                    dve.tensor_tensor(yb[:, :], yb[:, :], row[b.j][:, 0:D], ALU.add).then_inc(upd_set, 1)
                    dve.wait_ge(upd_set, b.count(1))
                    if b.reuses(2):
                        dve.wait_ge(stored[b.j], b.value(16 * PUTS, 16 * PUTS * b.off))
                    layernorm(dve, chain, yb[:, :], s, new[b.j][:, :], squares, roots, b, 1, 2).then_inc(new_set, 1)
                    dve.wait_ge(new_set, b.count(1))
                    nb, nv = new[b.j], nrm[b.j]
                    link(dve.bn_stats(s[:, 9:15], nb[:, 0:CS]))
                    link(dve.tensor_tensor(sq[:, :], nb[:, CS:D], nb[:, CS:D], ALU.mult))
                    dve.memset(s[:, 22:23], 0.0)
                    link(dve.bn_aggr(s[:, 15:17], s[:, 9:15]))
                    link(dve.tensor_reduce(s[:, 17:18], sq[:, :], AX.X, ALU.add))
                    dve.tensor_scalar(s[:, 18:19], s[:, 16:17], EPS, None, ALU.add)
                    dve.tensor_scalar(s[:, 19:20], s[:, 17:18], 1.0 / CV, EPS, ALU.mult, ALU.add).then_inc(squares, 1)
                    dve.wait_ge(roots, b.count(2, 2))
                    link(dve.reciprocal(s[:, 18:20], s[:, 18:20]))
                    if b.reuses(2):
                        dve.wait_ge(nrm_t, b.count(-1))
                    dve.tensor_scalar(nv[:, 0:CS], nb[:, 0:CS], s[:, 15:16], s[:, 18:19], ALU.subtract, ALU.mult)
                    link(dve.tensor_scalar(nv[:, CS:D], nb[:, CS:D], s[:, 19:20], None, ALU.mult))
                    link(dve.tensor_tensor(nv[:, 0:D], nv[:, 0:D], gam[:, :], ALU.mult))
                    dve.tensor_tensor(nv[:, 0:CS], nv[:, 0:CS], bet[:, :], ALU.add).then_inc(nrm_set, 1)
                    chain.end()
                node_steps(dve, step)


def edge_layer1(nc, g, A, src_table, combs):
    SLOTS = SM_TABLES
    COUNTS = [(SLOTS, c) for c in range(-SLOTS, SLOTS + 1)] + [(16, 16 * c) for c in (-1, 0, 1)]
    with Phase(nc, "e1") as ph:
        two = range(2)

        def pair(name, shape):
            return [ph.sb(f"{name}{k}", shape) for k in two]
        WR, WG = ph.sb("WR", [16, 224]), ph.sb("WG", [64, CV])
        WS1, WV1, WS2, WV2 = ph.sb("WS1", [P, 160]), ph.sb("WV1", [P, CV]), ph.sb("WS2", [P, CS]), ph.sb("WV2", [P, CV])
        WvT, w2, adot = ph.sb("WvT", [64, P]), ph.sb("w2", [P, 2]), ph.sb("adot", [P, CS])
        rbf = [ph.sb(f"rbf{k}", [16, P]) for k in range(SLOTS)]
        keys = [ph.sb(f"keys{k}", [P, P]) for k in range(SLOTS)]
        takes = [[ph.sb(f"take{k}{q}", [P, 1], I32) for k in range(SLOTS)] for q in two]
        put = [ph.sb(f"put{k}", [P, 1], I32) for k in range(SLOTS)]
        yt = [ph.sb(f"yt{k}", [P, 10]) for k in range(SLOTS)]
        srow = [ph.sb(f"srow{k}", [P, D]) for k in range(SLOTS)]
        crow = [ph.sb(f"crow{k}", [P, COMB]) for k in range(SLOTS)]
        mv, qs, qv = pair("mv", [P, CS + 5 * CV]), pair("qs", [P, 2 * CS]), pair("qv", [P, 3 * CV])
        by_y1, by_y2, pairs = pair("by_y1", [P, 9 * CV]), pair("by_y2", [P, 9 * CV]), pair("pairs", [P, 4 * CV])
        m1, m2, m1T, m2T = (pair(n, [P, 4 * P]) for n in ("m1", "m2", "m1T", "m2T"))
        th, sg, vv = pair("th", [P, 96]), pair("sg", [P, 96]), pair("vv", [P, 5 * CV])
        ra, lr, lw = pair("ra", [P, CS]), pair("lr", [P, CS]), pair("lw", [P, CS])
        lg, mx, dif, ex = pair("lg", [P, 4]), pair("mx", [P, 8]), pair("dif", [P, 8]), pair("ex", [P, 8])
        same, hw = pair("same", [P, P]), pair("hw", [P, 4 * HD])
        apart = [ph.sb(f"apart{k}", [P, P], BF16) for k in two]
        ident16 = ph.sb("ident16", [P, P], BF16)
        ps_w = [ph.ps(f"ps_w{k}") for k in two]
        ps_m1, ps_m2, ps_a, ps_h, ps_x, ps_g = (ph.ps(n) for n in ("ps_m1", "ps_m2", "ps_a", "ps_h", "ps_x", "ps_g"))
        wl, made, wready, blank = (ph.sem(n) for n in ("weights", "made", "wready", "blank"))
        keys_in, rbf_in, yt_in = ph.sems_of("keys_in", SLOTS), ph.sems_of("rbf_in", SLOTS), ph.sems_of("yt_in", SLOTS)
        srow_in, crow_in, written = g.pool_dmas["e1"]
        (take_set, put_set, w_ps, mv_set, prods, sv1_set, by_y1_set, pairs_set, feats1, m1_t, m1T_set, a_ps, th_set, ra_set, sg_set,
         vv_set, lr_set, sv2_set, by_y2_set, feats2, m2_t, m2T_set, h_ps, masks, lw_set, lg_set, x_ps, mx_set, mn_set,
         dif_set, ex_set, kept, hw_set, scaled, g_ps, row_set, den_set) = (ph.sem(n) for n in (
             "take_set", "put_set", "w_ps", "mv_set", "prods", "sv1_set", "by_y1_set", "pairs_set", "feats1", "m1_t", "m1T_set",
             "a_ps", "th_set", "ra_set", "sg_set", "vv_set", "lr_set", "sv2_set", "by_y2_set", "feats2", "m2_t",
             "m2T_set", "h_ps", "masks", "lw_set", "lg_set", "x_ps", "mx_set", "mn_set", "dif_set", "ex_set", "kept",
             "hw_set", "scaled", "g_ps", "row_set", "den_set"))
        Y0, Y1 = 0, 1

        def y(t, c):
            return yt[t.j][:, c:c + 1]

        with nc.Block() as block:
            @block.sync
            def _(sp):
                for dst, src in ((WR, "w1_rbf"), (WG, "w1_g"), (WS2, "w1_s2"), (WV1, "w1_v1"), (WV2, "w1_v2"), (WvT, "w1_valT"), (w2, "w1_w2")):
                    sp.dma_start(dst[:, :], A[src]).then_inc(wl, 16)
                sp.dma_start(WS1[:, 0:128], A["w1_s1"]).then_inc(wl, 16)
                sp.dma_start(adot[:, :], A["w1_adot"].partition_broadcast(P)).then_inc(wl, 16)

                def step(t):
                    if t.reuses(SLOTS):
                        sp.wait_ge(masks, t.count(1 - SLOTS))
                    sp.dma_start(keys[t.j][:, :], g.key_rows[1][bass.ds(t.t() * P, P)].partition_broadcast(P)).then_inc(keys_in[t.j], 16)
                    if t.reuses(SLOTS):
                        sp.wait_ge(w_ps, t.count(1 - SLOTS))
                    sp.dma_start(rbf[t.j][:, :], A["attr16_T"][:, bass.ds(t.t() * P, P)]).then_inc(rbf_in[t.j], 16)
                    if t.reuses(SLOTS):
                        sp.wait_ge(sv2_set, t.count(1 - SLOTS))
                        sp.wait_ge(feats2, t.count(1 - SLOTS))
                    sp.dma_start(yt[t.j][:, :], A["attr4_10"][bass.ds(t.t() * P, P), :]).then_inc(yt_in[t.j], 16)
                run_steps(sp, step, 0, SLOTS, NT, COUNTS)

            @block.gpsimd
            def _(pool):
                def step(s):
                    t = s
                    if t.exists():
                        pool.wait_ge(wl, 16 * 9)
                        pool.wait_ge(take_set, t.count(1))
                        if t.reuses(SLOTS):
                            pool.wait_ge(mv_set, t.count(1 - SLOTS))
                        pool.indirect_dma_start(out=srow[t.j][:, :], out_offset=None, in_=src_table,
                                                in_offset=bass.IndirectOffsetOnAxis(ap=takes[0][t.j][:, :], axis=0)).then_inc(srow_in[t.j], 16)
                    t = s
                    if t.exists():
                        pool.wait_ge(wl, 16 * 9)
                        if t.reuses(SLOTS):
                            pool.wait_ge(written[t.j], t.dma(1))
                        pool.indirect_dma_start(out=crow[t.j][:, :], out_offset=None, in_=combs[t.j][0:NP, :],
                                                in_offset=bass.IndirectOffsetOnAxis(ap=takes[1][t.j][:, :], axis=0)).then_inc(crow_in[t.j], 16)
                    t = s.back(5)
                    if t.exists():
                        pool.wait_ge(wl, 16 * 9)
                        pool.wait_ge(put_set, t.count(1))
                        pool.wait_ge(row_set, t.count(1))
                        pool.indirect_dma_start(out=combs[t.j], out_offset=bass.IndirectOffsetOnAxis(ap=put[t.j][:, :], axis=0),
                                                in_=crow[t.j][:, :], in_offset=None).then_inc(written[t.j], 16)
                run_steps(pool, step, 5, SLOTS, NT, COUNTS)
                for k in range(SLOTS):
                    pool.wait_ge(written[k], 16 * (NT // SLOTS))

            @block.tensor
            def _(pe):
                pe.wait_ge(wl, 16 * 9)
                pe.matmul(ps_g[:, 0:CV], WvT[:, :], WG[:, :], start=True, stop=True).then_inc(made, 1)
                pe.wait_ge(wready, 1)
                pe.wait_ge(blank, 1)

                def turn(t, m, ps, ready, half, free, out):
                    pe.wait_ge(ready, t.count(1))
                    pe.wait_ge(half, t.count(1))
                    if t.reuses(1):
                        pe.wait_ge(free, t.count(0))
                    for c in range(4):
                        ins = pe.transpose(ps[:, c * P:(c + 1) * P], m[t.j % 2][:, c * P:(c + 1) * P], g.ident[:, :])
                    ins.then_inc(out, 1)

                def step(s):
                    a, b, c = s.back(2), s.back(3), s.back(4)
                    if c.exists():
                        k = c.j % 2
                        pe.wait_ge(lg_set, c.count(1))
                        if c.reuses(1):
                            pe.wait_ge(mx_set, c.count(0))
                        pe.matmul(ps_x[:, :].rearrange("p (h e) -> p h e", h=4), ident16[:, :],
                                  bcast(apart[k][:, :].unsqueeze(1), (P, 4, P)), start=True, stop=False)
                        for h in range(4):
                            ins = pe.matmul(ps_x[:, h * P:(h + 1) * P], bcast(lg[k][:, h:h + 1], (P, P)), g.ident[:, :],
                                            start=False, stop=h == 3)
                        ins.then_inc(x_ps, 1)
                    n = s.back(1)
                    if n.exists():
                        k = n.j % 2
                        pe.wait_ge(rbf_in[n.j], n.dma())
                        if n.reuses(2):
                            pe.wait_ge(feats1, n.count(-1))
                        pe.matmul(ps_w[k][:, 0:224], rbf[n.j][:, :], WR[:, :], start=True, stop=True).then_inc(w_ps, 1)
                    if a.exists():
                        turn(a, m1, ps_m1, feats1, sv1_set, m1T_set, m1_t)
                    if c.exists():
                        k = c.j % 2
                        pe.wait_ge(m2T_set, c.count(1))
                        if c.reuses(1):
                            pe.wait_ge(hw_set, c.count(0))
                        heads = ps_h[:, 0:4 * (HD - 1)].rearrange("p (h m) -> p h m", h=4)
                        pe.matmul(heads[:, :, 0:16], m2T[k][:, 0:P], WS2[:, :], start=True, stop=True)
                        for q in range(3):
                            ins = pe.matmul(heads[:, :, 16 + 8 * q:24 + 8 * q], m2T[k][:, (q + 1) * P:(q + 2) * P], WV2[:, :],
                                            start=True, stop=True)
                        ins.then_inc(h_ps, 1)
                    if b.exists():
                        turn(b, m2, ps_m2, feats2, sv2_set, m2T_set, m2_t)
                    if c.exists():
                        k = c.j % 2
                        pe.wait_ge(hw_set, c.count(1))
                        pe.wait_ge(den_set, c.count(1))
                        if c.reuses(1):
                            pe.wait_ge(row_set, c.count(0))
                        pe.matmul(ps_g[:, 0:4 * HD], same[k][:, :], hw[k][:, :], start=True, stop=True).then_inc(g_ps, 1)
                    if a.exists():
                        k = a.j % 2
                        pe.wait_ge(m1T_set, a.count(1))
                        if a.reuses(1):
                            pe.wait_ge(lr_set, a.count(0))
                        pe.matmul(ps_a[:, 0:160], m1T[k][:, 0:P], WS1[:, :], start=True, stop=True)
                        values = ps_a[:, 160:160 + 6 * CV].rearrange("p (r q m) -> p q r m", r=2, q=3)
                        for q in range(3):
                            ins = pe.matmul(values[:, q], m1T[k][:, (q + 1) * P:(q + 2) * P], bcast(WV1[:, :].unsqueeze(1), (P, 2, CV)),
                                            start=True, stop=True)
                        ins.then_inc(a_ps, 1)
                run_steps(pe, step, 4, SLOTS, NT, COUNTS)

            @block.scalar
            def _(act):
                def products(t, m, p0, pv, qvs, out):
                    act.activation(m[:, 0:CS], p0, ACT.Copy, scale=y(t, Y0))
                    for c in range(3):
                        act.activation(m[:, (c + 1) * P:(c + 1) * P + CS], pv, ACT.Copy, scale=y(t, Y1 + c))
                    act.activation(m[:, P:4 * P].rearrange("p (c m) -> p c m", c=3)[:, :, CS:CS + CV],
                                   qvs.rearrange("p (c m) -> p c m", c=3), ACT.Copy, scale=y(t, Y0)).then_inc(out, 1)

                def step(s):
                    a, b, c = s.back(2), s.back(3), s.back(4)
                    if b.exists():
                        k = b.j % 2
                        act.wait_ge(a_ps, b.count(1))
                        if b.reuses(2):
                            act.wait_ge(lr_set, b.count(-1))
                        act.activation(th[k][:, :], ps_a[:, CS:160], ACT.Tanh, scale=0.5).then_inc(th_set, 1)
                        act.activation(ra[k][:, :], ps_a[:, 0:CS], ACT.Relu, scale=0.8).then_inc(ra_set, 1)
                    if a.exists():
                        k = a.j % 2
                        act.wait_ge(yt_in[a.j], a.dma())
                        act.wait_ge(prods, a.count(1))
                        if a.reuses(2):
                            act.wait_ge(m1_t, a.count(-1))
                        products(a, m1[k], qs[k][:, 0:CS], qs[k][:, CS:2 * CS], qv[k][:, :], sv1_set)
                    if b.exists():
                        k = b.j % 2
                        act.wait_ge(sg_set, b.count(1))
                        act.wait_ge(vv_set, b.count(1))
                        if b.reuses(2):
                            act.wait_ge(m2_t, b.count(-1))
                        products(b, m2[k], sg[k][:, 0:CS], sg[k][:, 0:CS], vv[k][:, 0:3 * CV], sv2_set)
                    if c.exists():
                        k = c.j % 2
                        act.wait_ge(dif_set, c.count(1))
                        if c.reuses(2):
                            act.wait_ge(scaled, c.count(-1))
                        act.activation(ex[k][:, :], dif[k][:, :], ACT.Exp).then_inc(ex_set, 1)
                        if c.reuses(2):
                            act.wait_ge(g_ps, c.count(-1))
                        act.activation(hw[k][:, :].rearrange("p (h m) -> p h m", h=4)[:, :, 0:1], dif[k][:, 0:4].unsqueeze(2), ACT.Exp).then_inc(den_set, 1)
                    if a.exists():
                        k = a.j % 2
                        act.wait_ge(m1_t, a.count(1))
                        if a.reuses(2):
                            act.wait_ge(a_ps, a.count(-1))
                        act.activation(m1T[k][:, :], ps_m1[:, :], ACT.Copy).then_inc(m1T_set, 1)
                    if b.exists():
                        k = b.j % 2
                        act.wait_ge(m2_t, b.count(1))
                        if b.reuses(2):
                            act.wait_ge(h_ps, b.count(-1))
                        act.activation(m2T[k][:, :], ps_m2[:, :], ACT.Copy).then_inc(m2T_set, 1)
                run_steps(act, step, 4, SLOTS, NT, COUNTS)

            @block.vector
            def _(dve):
                for k in two:
                    dve.memset(m1[k][:, 96:P], 0.0)
                    ins = dve.memset(m2[k][:, 96:P], 0.0)
                ins.then_inc(blank, 1)
                dve.wait_ge(wl, 16 * 9)
                dve.tensor_copy(ident16[:, :], g.ident[:, :])
                dve.wait_ge(made, 1)
                dve.tensor_copy(WS1[:, 128:160], ps_g[:, 0:CV])
                dve.tensor_scalar(WV1[96:128, :], WV1[96:128, :], 1.0 / S2, None, ALU.mult)
                dve.tensor_scalar(WS2[:, :], WS2[:, :], w2[:, 0:1], None, ALU.mult)
                dve.tensor_scalar(WV2[:, :], WV2[:, :], w2[:, 1:2], None, ALU.mult).then_inc(blank, 1)
                dve.wait_ge(blank, 2)
                dve.tensor_scalar(WS1[64:96, :], WS1[64:96, :], 1.0 / S3, None, ALU.mult)
                dve.tensor_scalar(WS2[64:96, :], WS2[64:96, :], 1.0 / S3, None, ALU.mult)
                dve.tensor_scalar(WV2[96:128, :], WV2[96:128, :], 1.0 / S2, None, ALU.mult).then_inc(wready, 1)

                def by_y(t, out, v, done):
                    windows = bass.AP(v.tensor, v.offset, [v.ap[0], [CV, 3], [CV, 3], [1, CV]])
                    dve.tensor_tensor(out[:, :].rearrange("p (g c m) -> p g c m", g=3, c=3), windows,
                                      bcast(yt[t.j][:, 1:10].rearrange("p (g c) -> p g c", g=3).unsqueeze(3), (P, 3, 3, CV)),
                                      ALU.mult).then_inc(done, 1)

                def vectors(m):
                    return m[:, P:4 * P].rearrange("p (c m) -> p c m", c=3)

                def dot_and_cross(dot, cross, terms):
                    dve.tensor_reduce(dot, terms[:, 0:3 * CV].rearrange("p (c m) -> p m c", c=3), AX.X, ALU.add)
                    return dve.tensor_tensor(cross, terms[:, 3 * CV:6 * CV].rearrange("p (c m) -> p c m", c=3),
                                             terms[:, 6 * CV:9 * CV].rearrange("p (c m) -> p c m", c=3), ALU.subtract)

                def step(s):
                    a, b, c = s.back(2), s.back(3), s.back(4)
                    ka, kb, kc = a.j % 2, b.j % 2, c.j % 2
                    row = crow[c.j]
                    if s.exists():
                        t = s
                        if t.reuses(SLOTS):
                            dve.wait_ge(srow_in[t.j], t.dma(1))
                            dve.wait_ge(crow_in[t.j], t.dma(1))
                        dve.tensor_copy(takes[0][t.j][:, :], g.key_i[0][:, bass.ds(t.t(), 1)])
                        dve.tensor_copy(takes[1][t.j][:, :], g.key_i[1][:, bass.ds(t.t(), 1)]).then_inc(take_set, 1)
                    if a.exists():
                        dve.wait_ge(srow_in[a.j], a.dma())
                        dve.wait_ge(crow_in[a.j], a.dma())
                        dve.tensor_tensor(mv[ka][:, 0:D], srow[a.j][:, :], crow[a.j][:, 0:D], ALU.add)
                        dve.tensor_tensor(mv[ka][:, D:D + 2 * CV], srow[a.j][:, CS:CS + 2 * CV], crow[a.j][:, CS:CS + 2 * CV], ALU.add).then_inc(mv_set, 1)
                        if a.reuses(SLOTS):
                            dve.wait_ge(written[a.j], a.dma(1))
                        dve.tensor_copy(put[a.j][:, :], g.put_i[1][:, bass.ds(a.t(), 1)]).then_inc(put_set, 1)
                    if a.exists():
                        dve.wait_ge(w_ps, a.count(1))
                        dve.wait_ge(mv_set, a.count(1))
                        if a.reuses(2):
                            dve.wait_ge(sv1_set, a.count(-1))
                        dve.tensor_tensor(qs[ka][:, :].rearrange("p (g m) -> p g m", g=2), ps_w[ka][:, 0:2 * CS].rearrange("p (g m) -> p g m", g=2),
                                          bcast(mv[ka][:, 0:CS].unsqueeze(1), (P, 2, CS)), ALU.mult)
                        dve.tensor_tensor(qv[ka][:, :].rearrange("p (c m) -> p c m", c=3), mv[ka][:, CS:D].rearrange("p (c m) -> p c m", c=3),
                                          bcast(ps_w[ka][:, 2 * CS:2 * CS + CV].unsqueeze(1), (P, 3, CV)), ALU.mult).then_inc(prods, 1)
                        dve.wait_ge(yt_in[a.j], a.dma())
                        by_y(a, by_y1[ka], mv[ka][:, CS:D], by_y1_set)
                    if a.exists():
                        dve.wait_ge(by_y1_set, a.count(1))
                        dot_and_cross(pairs[ka][:, 0:CV], pairs[ka][:, CV:4 * CV].rearrange("p (c m) -> p c m", c=3), by_y1[ka]).then_inc(pairs_set, 1)
                    if b.exists():
                        dve.wait_ge(th_set, b.count(1))
                        if b.reuses(2):
                            dve.wait_ge(sv2_set, b.count(-1))
                        dve.tensor_scalar(sg[kb][:, :], th[kb][:, :], 0.5, 0.5, ALU.mult, ALU.add).then_inc(sg_set, 1)
                    if a.exists():
                        dve.wait_ge(pairs_set, a.count(1))
                        if a.reuses(2):
                            dve.wait_ge(m1_t, a.count(-1))
                        dve.tensor_tensor(m1[ka][:, CS:CS + CV], ps_w[ka][:, 2 * CS + CV:2 * CS + 2 * CV], pairs[ka][:, 0:CV], ALU.mult)
                        dve.tensor_tensor(vectors(m1[ka])[:, :, CS + CV:P], pairs[ka][:, CV:4 * CV].rearrange("p (c m) -> p c m", c=3),
                                          bcast(ps_w[ka][:, 2 * CS + 2 * CV:224].unsqueeze(1), (P, 3, CV)), ALU.mult).then_inc(feats1, 1)
                    if b.exists():
                        dve.wait_ge(ra_set, b.count(1))
                        dve.wait_ge(sg_set, b.count(1))
                        dve.tensor_tensor(vv[kb][:, :].rearrange("p (c m) -> p c m", c=5), ps_a[:, 160:320].rearrange("p (c m) -> p c m", c=5),
                                          bcast(sg[kb][:, CS:96].unsqueeze(1), (P, 5, CV)), ALU.mult).then_inc(vv_set, 1)
                        dve.scalar_tensor_tensor(out=lr[kb][:, :], in0=ps_a[:, 0:CS], scalar=0.2, in1=ra[kb][:, :], op0=ALU.mult, op1=ALU.add).then_inc(lr_set, 1)
                    if b.exists():
                        dve.wait_ge(vv_set, b.count(1))
                        if b.reuses(2):
                            dve.wait_ge(m2_t, b.count(-1))
                        by_y(b, by_y2[kb], vv[kb][:, 0:3 * CV], by_y2_set)
                    if c.exists():
                        dve.wait_ge(x_ps, c.count(1))
                        dve.tensor_reduce(mx[kc][:, 0:4], ps_x[:, :].rearrange("p (h e) -> p h e", h=4), AX.X, ALU.max).then_inc(mx_set, 1)
                    if b.exists():
                        dve.wait_ge(lr_set, b.count(1))
                        dve.tensor_tensor(lw[kb][:, :], lr[kb][:, :], adot[:, :], ALU.mult).then_inc(lw_set, 1)
                        dve.wait_ge(by_y2_set, b.count(1))
                        dot_and_cross(m2[kb][:, CS:CS + CV], vectors(m2[kb])[:, :, CS + CV:P], by_y2[kb]).then_inc(feats2, 1)
                    if c.exists():
                        dve.wait_ge(mx_set, c.count(1))
                        dve.tensor_tensor(mx[kc][:, 4:8], row[:, D:D + 4], mx[kc][:, 0:4], ALU.max).then_inc(mn_set, 1)
                    if c.exists():
                        dve.wait_ge(mn_set, c.count(1))
                        if c.reuses(2):
                            dve.wait_ge(ex_set, c.count(-1))
                        dve.tensor_tensor(dif[kc][:, 0:4], lg[kc][:, :], mx[kc][:, 4:8], ALU.subtract)
                        dve.tensor_tensor(dif[kc][:, 4:8], row[:, D:D + 4], mx[kc][:, 4:8], ALU.subtract).then_inc(dif_set, 1)
                    if c.exists():
                        dve.wait_ge(ex_set, c.count(1))
                        acc = row[:, D + 4:COMB].rearrange("p (h m) -> p h m", h=4)
                        dve.tensor_tensor(acc, acc, bcast(ex[kc][:, 4:8].unsqueeze(2), (P, 4, HD)), ALU.mult).then_inc(scaled, 1)
                        dve.wait_ge(h_ps, c.count(1))
                        heads = hw[kc][:, :].rearrange("p (h m) -> p h m", h=4)
                        e4 = ex[kc][:, 0:4]
                        dve.tensor_tensor(heads[:, :, 1:HD], ps_h[:, 0:4 * (HD - 1)].rearrange("p (h m) -> p h m", h=4),
                                          bcast(e4.unsqueeze(2), (P, 4, HD - 1)), ALU.mult).then_inc(hw_set, 1)
                    if b.exists():
                        dve.wait_ge(keys_in[b.j], b.dma())
                        key = g.key_f[1][:, bass.ds(b.t(), 1)]
                        dve.tensor_scalar(same[kb][:, :], keys[b.j][:, :], key, None, ALU.is_equal)
                        dve.tensor_scalar(apart[kb][:, :], keys[b.j][:, :], key, LOW, ALU.not_equal, ALU.mult).then_inc(masks, 1)
                        dve.wait_ge(lw_set, b.count(1))
                        dve.tensor_reduce(lg[kb][:, :], lw[kb][:, :].rearrange("p (h m) -> p h m", h=4), AX.X, ALU.add).then_inc(lg_set, 1)
                    if c.exists():
                        dve.wait_ge(dif_set, c.count(1))
                        dve.tensor_copy(row[:, D:D + 4], mx[kc][:, 4:8]).then_inc(kept, 1)
                        dve.wait_ge(g_ps, c.count(1))
                        dve.wait_ge(scaled, c.count(1))
                        dve.tensor_tensor(row[:, D + 4:COMB], row[:, D + 4:COMB], ps_g[:, 0:4 * HD], ALU.add).then_inc(row_set, 1)
                run_steps(dve, step, 4, SLOTS, NT, COUNTS)


def nodes_after_1(nc, g, A, x, combs, x_out, table, scales):
    with Phase(nc, "n2") as ph:
        two = range(2)

        def pair(name, shape):
            return [ph.sb(f"{name}{k}", shape) for k in two]
        WP, WT = ph.sb("WP", [P, 2, D]), ph.sb("WT", [P, 2, CAT])
        runs, row, agg, aggT, new, newT = pair("runs", [P, SM_TABLES, SMW]), pair("row", [P, D]), pair("agg", [P, 2 * P]), pair("aggT", [P, 2 * P]), pair("new", [P, 2 * P]), pair("newT", [P, 2 * P])
        mx, wt, tot, y, stats, tab = pair("mx", [P, 4]), pair("wt", [P, SM_TABLES, 4]), pair("tot", [P, 4 * HD]), pair("y", [P, D]), pair("stats", [P, 24]), pair("tab", [P, CAT])
        ps_a, ps_o, ps_n, ps_c, ps_d = (ph.ps(n) for n in ("ps_a", "ps_o", "ps_n", "ps_c", "ps_d"))
        (wl, ready, blank, dif_set, wt_set, agg_set, agg_t, aggT_set, o_set, upd_set, squares, roots, new_set, new_t, newT_set,
         c_set, tab_set, chained) = (ph.sem(n) for n in (
             "weights", "ready", "blank", "dif_set", "wt_set", "agg_set", "agg_t", "aggT_set", "o_set", "upd_set", "squares",
             "roots", "new_set", "new_t", "newT_set", "c_set", "tab_set", "chained"))
        row_in, runs_in, stored = (ph.sems_of(n, 2) for n in ("row_in", "runs_in", "stored"))
        with nc.Block() as block:
            @block.sync
            def _(sp):
                load_matrix(sp, WP, A["w1_out"], wl)
                load_matrix(sp, WT, A["w2_tab"], wl)

                def store(p):
                    where = bass.ds(p.t() * P, P)
                    sp.wait_ge(new_set, p.count(1))
                    sp.dma_start(x_out[where, :], new[p.j][:, 0:D]).then_inc(stored[p.j], 16)
                    sp.wait_ge(tab_set, p.count(1))
                    sp.dma_start(table[where, :], tab[p.j][:, :]).then_inc(stored[p.j], 16)

                def step(b):
                    where = bass.ds(b.t() * P, P)
                    if b.reuses(2):
                        sp.wait_ge(agg_set, b.count(-1))
                    for k in range(SM_TABLES):
                        sp.dma_start(runs[b.j][:, k, :], combs[k][where, D:COMB]).then_inc(runs_in[b.j], 16)
                    if b.reuses(2):
                        sp.wait_ge(upd_set, b.count(-1))
                    sp.dma_start(row[b.j][:, :], x[where, :]).then_inc(row_in[b.j], 16)
                    p = b.back(1)
                    if p.exists():
                        store(p)
                node_steps(sp, step)
                store(Tile(NB // 2 - 1, 1, 2, NB))
                for k in two:
                    sp.wait_ge(stored[k], 32 * (NB // 2))

            @block.tensor
            def _(pe):
                pe.wait_ge(ready, 1)
                pe.wait_ge(blank, 1)

                def step(b):
                    pe.wait_ge(agg_set, b.count(1))
                    if b.reuses(1):
                        pe.wait_ge(aggT_set, b.count(0))
                    for c in range(2):
                        ins = pe.transpose(ps_a[:, c * P:(c + 1) * P], agg[b.j][:, c * P:(c + 1) * P], g.ident[:, :])
                    ins.then_inc(agg_t, 1)
                    pe.wait_ge(aggT_set, b.count(1))
                    if b.reuses(1):
                        pe.wait_ge(upd_set, b.count(0))
                    for c in range(2):
                        ins = pe.matmul(ps_o[:, 0:D], aggT[b.j][:, c * P:(c + 1) * P], WP[:, c, :], start=c == 0, stop=c == 1)
                    ins.then_inc(o_set, 1)
                    message_rows(pe, g, b, new[b.j], newT[b.j], WT, ps_n, ps_c, ps_d, new_set, new_t, newT_set, c_set, tab_set)
                node_steps(pe, step)

            @block.scalar
            def _(act):
                act.wait_ge(wl, 32)
                scale_columns(act, WT, scales, ready)

                def step(b):
                    act.wait_ge(dif_set, b.count(1))
                    if b.reuses(2):
                        act.wait_ge(agg_set, b.count(-1))
                    act.activation(wt[b.j][:, :, :], wt[b.j][:, :, :], ACT.Exp).then_inc(wt_set, 1)
                    act.wait_ge(agg_t, b.count(1))
                    if b.reuses(2):
                        act.wait_ge(o_set, b.count(-1))
                    act.activation(aggT[b.j][:, :], ps_a[:, 0:2 * P], ACT.Copy).then_inc(aggT_set, 1)
                    root(act, stats[b.j][:, 8:9], squares, roots, b, 1, 1)
                    message_copies(act, b, newT[b.j], tab[b.j], ps_n, ps_c, ps_d, new_t, newT_set, c_set, tab_set, stored[b.j], 2)
                node_steps(act, step)

            @block.vector
            def _(dve):
                for k in two:
                    dve.memset(agg[k][:, D:2 * P], 0.0)
                    ins = dve.memset(new[k][:, D:2 * P], 0.0)
                ins.then_inc(blank, 1)
                chain = Linked(dve, chained, 9)

                def step(b):
                    chain.start(b)
                    link, r, k = chain.link, runs[b.j], b.j
                    dve.wait_ge(runs_in[k], b.value(16 * SM_TABLES, 16 * SM_TABLES * (b.off + 1)))
                    link(dve.tensor_reduce(mx[k][:, :], r[:, :, 0:4].rearrange("p k h -> p h k"), AX.X, ALU.max))
                    dve.tensor_tensor(wt[k][:, :, :], r[:, :, 0:4], bcast(mx[k][:, :].unsqueeze(1), (P, SM_TABLES, 4)), ALU.subtract).then_inc(dif_set, 1)
                    dve.wait_ge(wt_set, b.count(1))
                    for q in range(SM_TABLES):
                        part = r[:, q, 4:SMW].rearrange("p (h m) -> p h m", h=4)
                        ins = dve.tensor_tensor(part, part, bcast(wt[k][:, q, :].unsqueeze(2), (P, 4, HD)), ALU.mult)
                    link(ins)
                    link(dve.tensor_reduce(tot[k][:, :], r[:, :, 4:SMW].rearrange("p k m -> p m k"), AX.X, ALU.add))
                    heads = tot[k][:, :].rearrange("p (h m) -> p h m", h=4)
                    link(dve.tensor_scalar(heads[:, :, 0:1], heads[:, :, 0:1], 1e-16, None, ALU.add))
                    link(dve.reciprocal(heads[:, :, 0:1], heads[:, :, 0:1]))
                    if b.reuses(2):
                        dve.wait_ge(agg_t, b.count(-1))
                    inv = heads[:, :, 0:1]
                    dve.tensor_tensor(agg[k][:, 0:CS].rearrange("p (h m) -> p h m", h=4), heads[:, :, 1:17], bcast(inv, (P, 4, 16)), ALU.mult)
                    for c in range(3):
                        ins = dve.tensor_tensor(agg[k][:, CS + c * CV:CS + (c + 1) * CV].rearrange("p (h m) -> p h m", h=4),
                                                heads[:, :, 17 + 8 * c:25 + 8 * c], bcast(inv, (P, 4, 8)), ALU.mult)
                    ins.then_inc(agg_set, 1)
                    dve.wait_ge(o_set, b.count(1))
                    dve.wait_ge(row_in[k], b.dma())
                    dve.scalar_tensor_tensor(out=y[k][:, :], in0=row[k][:, :], scalar=2.0, in1=ps_o[:, 0:D], op0=ALU.mult, op1=ALU.add).then_inc(upd_set, 1)
                    dve.wait_ge(upd_set, b.count(1))
                    if b.reuses(2):
                        dve.wait_ge(new_t, b.count(-1))
                        dve.wait_ge(stored[k], b.value(32, 32 * b.off))
                    layernorm(dve, chain, y[k][:, :], stats[k], new[k][:, 0:D], squares, roots, b, 1, 1).then_inc(new_set, 1)
                    link(dve.memset(stats[k][:, 21:22], 0.0))
                    chain.end()
                node_steps(dve, step)


def scale_columns(act, W, scales, ready):
    for lo, hi, value in scales:
        ins = act.mul(W[:, :, lo:hi], W[:, :, lo:hi], value)
    ins.then_inc(ready, 1)


def message_rows(pe, g, b, new, newT, WT, ps_n, ps_c, ps_d, new_set, new_t, newT_set, c_set, tab_set):
    pe.wait_ge(new_set, b.count(1))
    if b.reuses(1):
        pe.wait_ge(newT_set, b.count(0))
    for c in range(2):
        ins = pe.transpose(ps_n[:, c * P:(c + 1) * P], new[:, c * P:(c + 1) * P], g.ident[:, :])
    ins.then_inc(new_t, 1)
    pe.wait_ge(newT_set, b.count(1))
    if b.reuses(1):
        pe.wait_ge(tab_set, b.count(0))
    for ps, lo, hi in ((ps_c, 0, 2 * D), (ps_d, 2 * D, CAT)):
        for c in range(2):
            ins = pe.matmul(ps[:, 0:hi - lo], newT[:, c * P:(c + 1) * P], WT[:, c, lo:hi], start=c == 0, stop=c == 1)
    ins.then_inc(c_set, 1)


def message_copies(act, b, newT, tab, ps_n, ps_c, ps_d, new_t, newT_set, c_set, tab_set, stored, puts):
    act.wait_ge(new_t, b.count(1))
    if b.reuses(2):
        act.wait_ge(c_set, b.count(-1))
    act.activation(newT[:, :], ps_n[:, 0:2 * P], ACT.Copy).then_inc(newT_set, 1)
    act.wait_ge(c_set, b.count(1))
    if b.reuses(2):
        act.wait_ge(stored, b.value(16 * puts, 16 * puts * b.off))
    act.activation(tab[:, 0:2 * D], ps_c[:, 0:2 * D], ACT.Copy)
    act.activation(tab[:, 2 * D:CAT], ps_d[:, 0:CAT - 2 * D], ACT.Copy).then_inc(tab_set, 1)


def edge_messages(nc, g, name, table, accs):
    with Phase(nc, name) as ph:
        two = range(2)
        keys = [ph.sb(f"keys{k}", [P, P]) for k in range(U)]
        take = [ph.sb(f"take{k}", [P, 1], I32) for k in range(U)]
        put = [ph.sb(f"put{k}", [P, 1], I32) for k in range(U)]
        row = [ph.sb(f"row{k}", [P, CAT]) for k in range(U)]
        same = [ph.sb(f"same{k}", [P, P]) for k in two]
        q = [ph.sb(f"q{k}", [P, D]) for k in two]
        total = [ph.sb(f"total{k}", [P, D]) for k in range(U)]
        ps_o = [ph.ps(f"ps_o{k}") for k in two]
        keys_in = ph.sems_of("keys_in", U)
        row_in, added = g.pool_dmas[name]
        take_set, put_set, same_set, base, term0, term1, feats, sums_ps, total_set, started = (ph.sem(n) for n in (
            "take_set", "put_set", "same_set", "base", "term0", "term1", "feats", "sums_ps", "total_set", "started"))
        AE, C0, DD = D, 2 * D, 2 * D + 3 * CS

        def attr(t, c):
            return g.attr4[:, bass.ds(t.t(), 1), c]

        with nc.Block() as block:
            @block.sync
            def _(sp):
                def step(t):
                    if t.reuses(U):
                        sp.wait_ge(same_set, t.count(1 - U))
                    sp.dma_start(keys[t.j][:, :], g.key_rows[0][bass.ds(t.t() * P, P)].partition_broadcast(P)).then_inc(keys_in[t.j], 16)
                edge_steps(sp, step, 0)

            @block.gpsimd
            def _(pool):
                def step(s):
                    if s.exists():
                        t = s
                        pool.wait_ge(started, 1)
                        pool.wait_ge(take_set, t.count(1))
                        if t.reuses(U):
                            pool.wait_ge(feats, t.count(1 - U))
                        pool.indirect_dma_start(out=row[t.j][:, :], out_offset=None, in_=table,
                                                in_offset=bass.IndirectOffsetOnAxis(ap=take[t.j][:, :], axis=0)).then_inc(row_in[t.j], 16)
                    t = s.back(3)
                    if t.exists():
                        pool.wait_ge(started, 1)
                        pool.wait_ge(total_set, t.count(1))
                        pool.wait_ge(put_set, t.count(1))
                        if t.reuses(ADD_TABLES):
                            pool.wait_ge(added[(t.j - ADD_TABLES) % U], t.back(ADD_TABLES).dma())
                        pool.indirect_dma_start(out=accs[t.j % ADD_TABLES], out_offset=bass.IndirectOffsetOnAxis(ap=put[t.j][:, :], axis=0),
                                                in_=total[t.j][:, :], in_offset=None, compute_op=ALU.add).then_inc(added[t.j], 16)
                edge_steps(pool, step, 3, [(U, c) for c in range(-6, 5)] + [(16, 16 * c) for c in (-1, 0, 1)])
                for k in range(U):
                    pool.wait_ge(added[k], 16 * (NT // U))

            @block.tensor
            def _(pe):
                def step(s):
                    t = s.back(2)
                    if t.exists():
                        b = t.j % 2
                        pe.wait_ge(feats, t.count(1))
                        if t.reuses(2):
                            pe.wait_ge(total_set, t.count(-1))
                        pe.matmul(ps_o[b][:, 0:D], same[b][:, :], q[b][:, :], start=True, stop=True).then_inc(sums_ps, 1)
                edge_steps(pe, step, 2)

            @block.scalar
            def _(act):
                def step(s):
                    t = s.back(2)
                    if t.exists():
                        b = t.j % 2
                        act.wait_ge(sums_ps, t.count(1))
                        if t.reuses(U):
                            act.wait_ge(added[t.j], t.dma(1))
                        act.activation(total[t.j][:, :], ps_o[b][:, 0:D], ACT.Copy).then_inc(total_set, 1)
                edge_steps(act, step, 2)

            @block.vector
            def _(dve):
                dve.memset(q[0][:, :], 0.0).then_inc(started, 1)

                def step(s):
                    if s.exists():
                        t = s
                        if t.reuses(U):
                            dve.wait_ge(row_in[t.j], t.dma(1))
                        dve.tensor_copy(take[t.j][:, :], g.key_i[1][:, bass.ds(t.t(), 1)]).then_inc(take_set, 1)
                    t = s.back(2)
                    if not t.exists():
                        return
                    b = t.j % 2
                    qb, r = q[b], row[t.j]
                    if t.reuses(U):
                        dve.wait_ge(added[t.j], t.dma(1))
                    dve.tensor_copy(put[t.j][:, :], g.put_i[0][:, bass.ds(t.t(), 1)]).then_inc(put_set, 1)
                    dve.wait_ge(row_in[t.j], t.dma())
                    if t.reuses(2):
                        dve.wait_ge(sums_ps, t.count(-1))
                    dve.scalar_tensor_tensor(out=qb[:, :], in0=r[:, AE:AE + D], scalar=attr(t, 3), in1=r[:, 0:D],
                                             op0=ALU.mult, op1=ALU.add).then_inc(base, 1)
                    dve.wait_ge(keys_in[t.j], t.dma())
                    dve.tensor_scalar(same[b][:, :], keys[t.j][:, :], g.key_f[0][:, bass.ds(t.t(), 1)], None, ALU.is_equal).then_inc(same_set, 1)
                    dve.wait_ge(base, t.count(1))

                    def scalars(c):
                        return dve.scalar_tensor_tensor(out=qb[:, 0:CS], in0=r[:, C0 + c * CS:C0 + (c + 1) * CS], scalar=attr(t, c),
                                                        in1=qb[:, 0:CS], op0=ALU.mult, op1=ALU.add)

                    def vectors(c):
                        at = CS + c * CV
                        return dve.scalar_tensor_tensor(out=qb[:, at:at + CV], in0=r[:, DD:DD + CV], scalar=attr(t, c),
                                                        in1=qb[:, at:at + CV], op0=ALU.mult, op1=ALU.add)
                    scalars(0).then_inc(term0, 1)
                    vectors(0)
                    vectors(1)
                    dve.wait_ge(term0, t.count(1))
                    scalars(1).then_inc(term1, 1)
                    vectors(2)
                    dve.wait_ge(term1, t.count(1))
                    scalars(2).then_inc(feats, 1)
                edge_steps(dve, step, 2)


def nodes_update(nc, g, A, name, mats, x, accs, x_out, table, next_tab, scales, next_scales):
    W0, W1 = 5 * 1024, 4 * 1024
    CH = 512
    with Phase(nc, name) as ph:
        two = range(2)

        def pair(name, shape):
            return [ph.sb(f"{name}{k}", shape) for k in two]
        WA0, WA1, WL = ph.sb("WA0", [CS, W0]), ph.sb("WA1", [CV, W1]), ph.sb("WL", [P, 2, D])
        WT = ph.sb("WT", [P, 2, CAT]) if table is not None else None
        row, agg, part = pair("row", [P, 2 * P]), pair("agg", [P, D]), [pair(f"acc{a}_", [P, D]) for a in range(ADD_TABLES)]
        a0T, a1T, rowT = pair("a0T", [CS, P]), pair("a1T", [CV, 3 * P]), pair("rowT", [P, 2 * P])
        prod = [ph.sb(f"prod{k}", [P, CH]) for k in range(4)]
        r0, r1 = pair("r0", [P, 4, CS]), pair("r1", [P, 2, 3 * CV])
        y, stats, new, newT = pair("y", [P, D]), pair("stats", [P, 24]), pair("new", [P, 2 * P]), pair("newT", [P, 2 * P])
        tab = pair("tab", [P, CAT]) if table is not None else None
        ps_z = [ph.ps(f"ps_z{k}") for k in range(4)]
        ps_t, ps_l, ps_c, ps_d = (ph.ps(n) for n in ("ps_t", "ps_l", "ps_c", "ps_d"))
        (wl, ready, blank, agg_set, turned, turned_sb, z_ps, multiplied, reduced, l_ps, upd_set, squares, roots, new_set, new_t,
         newT_set, c_set, tab_set, chained, linked) = (ph.sem(n) for n in (
             "weights", "ready", "blank", "agg_set", "turned", "turned_sb", "z_ps", "multiplied", "reduced", "l_ps", "upd_set",
             "squares", "roots", "new_set", "new_t", "newT_set", "c_set", "tab_set", "chained", "linked"))
        row_in, acc_in, stored = (ph.sems_of(n, 2) for n in ("row_in", "acc_in", "stored"))
        puts = 1 if table is None else 2

        chunks = []
        for c in range(8):
            chunks.append((None, c * CH, [((0, CS), ("r0", 0, 8 * c))], 8, CS))
        for c in two:
            chunks.append((None, 4096 + c * CH, [((CS + k * CV, CS + (k + 1) * CV), ("r1", 1, k * CV + 16 * c)) for k in range(3)], 16, CV))
        for k in range(3):
            for c in range(4):
                chunks.append((k, c * CH, [((CS + k * CV, CS + (k + 1) * CV), ("r0", 1 + k, 16 * c))], 16, CV))
            for c in range(4):
                chunks.append((k, 2048 + c * CH, [((0, CS), ("r1", 0, k * CV + 8 * c))], 8, CS))
        NCH = len(chunks)
        last_mult = []
        for ch in chunks:
            last_mult.append((last_mult[-1] if last_mult else 0) + len(ch[2]))
        NM = last_mult[-1]

        def bank(b, n):
            return (NCH * b.j + n) % 4
        assert 2 * NCH % 4 == 0

        with nc.Block() as block:
            @block.sync
            def _(sp):
                sp.dma_start(WA0[:, :], A[mats + "_a0"]).then_inc(wl, 16)
                sp.dma_start(WA1[:, :], A[mats + "_a1"]).then_inc(wl, 16)
                load_matrix(sp, WL, A[mats + "_lin"], wl)
                if table is not None:
                    load_matrix(sp, WT, A[next_tab], wl)

                def store(p):
                    where = bass.ds(p.t() * P, P)
                    sp.wait_ge(new_set, p.count(1))
                    sp.dma_start(x_out[where, :], new[p.j][:, 0:D]).then_inc(stored[p.j], 16)
                    if table is not None:
                        sp.wait_ge(tab_set, p.count(1))
                        sp.dma_start(table[where, :], tab[p.j][:, :]).then_inc(stored[p.j], 16)

                def step(b):
                    where = bass.ds(b.t() * P, P)
                    if b.reuses(2):
                        sp.wait_ge(agg_set, b.count(-1))
                    for a in range(ADD_TABLES):
                        sp.dma_start(part[a][b.j][:, :], accs[a][where, :]).then_inc(acc_in[b.j], 16)
                    if b.reuses(2):
                        sp.wait_ge(upd_set, b.count(-1))
                    sp.dma_start(row[b.j][:, 0:D], x[where, :]).then_inc(row_in[b.j], 16)
                    p = b.back(1)
                    if p.exists():
                        store(p)
                node_steps(sp, step)
                store(Tile(NB // 2 - 1, 1, 2, NB))
                for k in two:
                    sp.wait_ge(stored[k], 16 * puts * (NB // 2))

            @block.tensor
            def _(pe):
                pe.wait_ge(ready, 1)
                pe.wait_ge(blank, 1)

                def step(b):
                    k = b.j
                    pe.wait_ge(agg_set, b.count(1))
                    pe.wait_ge(row_in[k], b.dma())
                    if b.reuses(1):
                        pe.wait_ge(turned_sb, b.count(0))
                        pe.wait_ge(upd_set, b.count(0))
                    for c in two:
                        pe.transpose(ps_l[:, 256 + c * P:256 + (c + 1) * P], row[k][:, c * P:(c + 1) * P], g.ident[:, :])
                    pe.transpose(ps_t[0:CS, 0:P], agg[k][:, 0:CS], g.ident[:, :])
                    for c in range(3):
                        ins = pe.transpose(ps_t[0:CV, (c + 1) * P:(c + 2) * P], agg[k][:, CS + c * CV:CS + (c + 1) * CV], g.ident[:, :])
                    ins.then_inc(turned, 1)
                    pe.wait_ge(turned_sb, b.count(1))
                    for n, (comp, col, _, _, _) in enumerate(chunks):
                        if n >= 4:
                            pe.wait_ge(multiplied, b.count(last_mult[n - 4], NM))
                        elif b.reuses(1):
                            pe.wait_ge(multiplied, b.count(last_mult[NCH + n - 4] - NM, NM))
                        if comp is None:
                            lhs, rhs = a0T[k][:, :], WA0[:, col:col + CH]
                        else:
                            lhs, rhs = a1T[k][:, comp * P:(comp + 1) * P], WA1[:, col:col + CH]
                        pe.matmul(ps_z[bank(b, n)][:, :], lhs, rhs, start=True, stop=True).then_inc(z_ps, 1)
                    for c in two:
                        ins = pe.matmul(ps_l[:, 0:D], rowT[k][:, c * P:(c + 1) * P], WL[:, c, :], start=c == 0, stop=c == 1)
                    ins.then_inc(l_ps, 1)
                    if table is not None:
                        message_rows(pe, g, b, new[k], newT[k], WT, ps_t, ps_c, ps_d, new_set, new_t, newT_set, c_set, tab_set)
                node_steps(pe, step)

            @block.scalar
            def _(act):
                act.wait_ge(wl, 64 if table is not None else 48)
                s_ss, s_vv, s_sv, s_vs, l_s, l_v = scales
                act.mul(WA0[:, 0:4096], WA0[:, 0:4096], s_ss)
                act.mul(WA0[:, 4096:W0], WA0[:, 4096:W0], s_vs)
                act.mul(WA1[:, 0:2048], WA1[:, 0:2048], s_vv)
                act.mul(WA1[:, 2048:W1], WA1[:, 2048:W1], s_sv)
                if table is not None:
                    scale_columns(act, WT, next_scales, chained)
                act.mul(WL[:, :, 0:CS], WL[:, :, 0:CS], l_s)
                act.mul(WL[:, :, CS:D], WL[:, :, CS:D], l_v).then_inc(ready, 1)

                def step(b):
                    k = b.j
                    act.wait_ge(turned, b.count(1))
                    if b.reuses(2):
                        act.wait_ge(l_ps, b.count(-1))
                    act.activation(a0T[k][:, :], ps_t[0:CS, 0:P], ACT.Copy)
                    act.activation(a1T[k][:, :], ps_t[0:CV, P:4 * P], ACT.Copy)
                    act.activation(rowT[k][:, :], ps_l[:, 256:512], ACT.Copy).then_inc(turned_sb, 1)
                    root(act, stats[k][:, 8:9], squares, roots, b, 1, 1)
                    if table is not None:
                        message_copies(act, b, newT[k], tab[k], ps_t, ps_c, ps_d, new_t, newT_set, c_set, tab_set, stored[k], puts)
                node_steps(act, step)

            @block.vector
            def _(dve):
                for k in two:
                    dve.memset(row[k][:, D:2 * P], 0.0)
                    ins = dve.memset(new[k][:, D:2 * P], 0.0)
                ins.then_inc(blank, 1)
                links = Linked(dve, linked, 6)

                def step(b):
                    k = b.j
                    links.start(b)
                    dve.wait_ge(acc_in[k], b.value(32, 32 * (b.off + 1)))
                    if b.reuses(2):
                        dve.wait_ge(turned, b.count(-1))
                    dve.tensor_tensor(agg[k][:, :], part[0][k][:, :], part[1][k][:, :], ALU.add).then_inc(agg_set, 1)
                    dve.wait_ge(row_in[k], b.dma())
                    todo = []

                    def reduce(m, dst, w, u):
                        dve.wait_ge(multiplied, b.count(m, NM))
                        which, slot, at = dst
                        out = (r0 if which == "r0" else r1)[k][:, slot, at:at + w]
                        dve.tensor_reduce(out, prod[(m - 1) % 4][:, :].rearrange("p (w u) -> p w u", w=w), AX.X, ALU.add).then_inc(reduced, 1)
                    m = 0
                    for n, (comp, col, uses, w, u) in enumerate(chunks):
                        dve.wait_ge(z_ps, b.count(n + 1, NCH))
                        for (lo, hi), dst in uses:
                            m += 1
                            if m > 4:
                                dve.wait_ge(reduced, b.count(m - 4, NM))
                            elif b.reuses(1):
                                dve.wait_ge(reduced, b.count(0, NM))
                            z = ps_z[bank(b, n)][:, :].rearrange("p (w u) -> p w u", w=w)
                            dve.tensor_tensor(prod[(m - 1) % 4][:, :].rearrange("p (w u) -> p w u", w=w), z,
                                              bcast(row[k][:, lo:hi].unsqueeze(1), (P, w, u)), ALU.mult).then_inc(multiplied, 1)
                            todo.append((m, dst, w, u))
                            if len(todo) > 1:
                                reduce(*todo.pop(0))
                    reduce(*todo.pop(0))
                    dve.wait_ge(reduced, b.count(NM, NM))
                    dve.tensor_reduce(y[k][:, 0:CS], r0[k][:, :, :].rearrange("p a w -> p w a"), AX.X, ALU.add)
                    links.link(dve.tensor_tensor(y[k][:, CS:D], r1[k][:, 0, :], r1[k][:, 1, :], ALU.add))
                    links.link(dve.scalar_tensor_tensor(out=y[k][:, :], in0=row[k][:, 0:D], scalar=2.0, in1=y[k][:, :], op0=ALU.mult, op1=ALU.add))
                    dve.wait_ge(l_ps, b.count(1))
                    dve.tensor_tensor(y[k][:, :], y[k][:, :], ps_l[:, 0:D], ALU.add).then_inc(upd_set, 1)
                    dve.wait_ge(upd_set, b.count(1))
                    if b.reuses(2):
                        if table is not None:
                            dve.wait_ge(new_t, b.count(-1))
                        dve.wait_ge(stored[k], b.value(16 * puts, 16 * puts * b.off))
                    layernorm(dve, links, y[k][:, :], stats[k], new[k][:, 0:D], squares, roots, b, 1, 1).then_inc(new_set, 1)
                    links.link(dve.memset(stats[k][:, 21:22], 0.0))
                    links.end()
                node_steps(dve, step)


class Globals:
    pass


def build(nc, A, out):
    def dram(name, shape):
        return nc.dram_tensor(name, shape, F32).ap()
    with ExitStack() as ctx:
        def sb(name, shape, dtype=F32):
            return ctx.enter_context(nc.sbuf_tensor(name, shape, dtype))
        g = Globals()
        g.key_i = [sb(f"key_i{k}", [P, NT], I32) for k in range(2)]
        g.key_f = [sb(f"key_f{k}", [P, NT]) for k in range(2)]
        g.put_i = [sb(f"put_i{k}", [P, NT], I32) for k in range(2)]
        g.attr4 = sb("attr4", [P, NT, 4])
        g.attr3 = sb("attr3", [P, NT, 3])
        g.ident, g.before, g.waste = sb("ident", [P, P]), sb("before", [P, P]), sb("waste", [P, 1])
        g.pool_dmas = {phase: [[ctx.enter_context(nc.semaphore(f"{phase}_{stream}{k}")) for k in range(SM_TABLES if phase == "e1" else U)] for stream in streams]
                       for phase, streams in (("e0", ("row_in", "added")), ("e1", ("srow_in", "crow_in", "written")),
                                              ("e2", ("row_in", "added")), ("e3", ("row_in", "added")))}
        g.key_rows = [dram(f"key_rows{k}", [EP]) for k in range(2)]
        table0, src_table = dram("table0", [NP, D]), dram("src_table", [NP, D])
        accs0 = [dram(f"accs0{k}", [ACC_ROWS, AGG0]) for k in range(ADD_TABLES)]
        combs = [dram(f"comb{k}", [ACC_ROWS, COMB]) for k in range(SM_TABLES)]
        accs2, accs3 = ([dram(f"{n}{k}", [ACC_ROWS, D]) for k in range(ADD_TABLES)] for n in ("accs2", "accs3"))
        x1, x2, x3 = (dram(n, [NP, D]) for n in ("x1", "x2", "x3"))
        table2, table3 = dram("table2", [NP, CAT]), dram("table3", [NP, CAT])
        prepare(nc, g, A, accs0 + accs2 + accs3)
        first_table(nc, g, A, A["x"], table0)
        edge_layer0(nc, g, A, table0, accs0)
        nodes_after_0(nc, g, A, A["x"], accs0, x1, src_table, combs)
        edge_layer1(nc, g, A, src_table, combs)
        c = 96.0 ** -0.5
        l_s, l_v = 64.0 ** -0.5, 32.0 ** -0.5
        nodes_after_1(nc, g, A, x1, combs, x2, table2,
                      [(0, 64, l_s), (64, 160, l_v), (160, 320, c), (320, 512, c / S3), (512, 544, c)])
        edge_messages(nc, g, "e2", table2, accs2)
        f0, f1 = 5120.0 ** -0.5, 4096.0 ** -0.5
        nodes_update(nc, g, A, "n3", "w2", x2, accs2, x3, table3, "w3_tab", (f0, f0 / S3, f1, f1, l_s, l_v),
                     [(0, 64, l_s), (64, 160, l_v), (160, 224, l_s), (224, 320, l_v), (320, 512, l_v / S3), (512, 544, l_s)])
        edge_messages(nc, g, "e3", table3, accs3)
        h = 2048.0 ** -0.5
        nodes_update(nc, g, A, "n4", "w3", x3, accs3, out, None, None, (1.0 / 64, 1.0 / 32 / S3, h, h, l_s, l_v), None)


def layout_rest(a, f, g):
    import numpy as np
    a["w1_rbf"], a["w1_g"], a["w1_v1"], a["w1_v2"] = g["W_rbf"], g["Wg"], g["Wv_val"], g["Wv_vlin"]
    a["w1_s1"] = _blocks(P, 128, [(0, 0, g["W_alpha"]), (0, 64, g["Ws_val"])])
    a["w1_s2"] = _blocks(P, CS, [(0, 0, g["Ws_vlin"])])
    a["w1_valT"] = _blocks(64, P, [(0, 0, g["Ws_val"].T)])
    w2 = np.zeros((P, 2), np.float32)
    w2[:96, 0] = np.concatenate([g["w2_ss"], g["w2_vv0"]])
    w2[:, 1] = np.concatenate([g["w2_sv"], g["w2_vs"], g["w2_vv1"]])
    a["w1_w2"] = w2
    a["w1_adot"] = g["alpha_dot"].reshape(-1)
    a["w1_out"] = _blocks(256, D, [(0, 0, g["Wps"])] + _per_component(64, 64, g["Wpv"]))

    def messages(lin_s, lin_v, ss, sv, vs, vv):
        return _blocks(256, CAT, [(0, 0, lin_s), (0, 160, ss), (0, 512, sv)] + _per_component(64, 64, lin_v)
                       + _per_component(64, 224, vs) + _per_component(64, 320, vv))

    def update(name, ss, sv, vs, vv, lin_s, lin_v):
        def behind(w):
            return w.transpose(1, 2, 0).reshape(w.shape[1], -1)
        a[name + "_a0"] = np.concatenate([behind(ss), behind(vs)], axis=1)
        a[name + "_a1"] = np.concatenate([behind(vv), behind(sv)], axis=1)
        a[name + "_lin"] = _blocks(256, D, [(0, 0, lin_s)] + _per_component(64, 64, lin_v))
    m = {k[7:]: v for k, v in f.items() if k.startswith("L2_gnn_")}
    a["w2_tab"] = messages(m["lm0"], m["lm1"], m["wm000"][:, 0], m["wm011"][:, 0], m["wm101"][:, 0], m["wm110"][:, 0])
    update("w2", m["wu000"], m["wu011"], m["wu101"], m["wu110"], m["lu0"], m["lu1"])
    m = {k[7:]: v for k, v in f.items() if k.startswith("L3_gnn_")}
    a["w3_tab"] = messages(m["Lm_s"], m["Lm_v"], m["Wm_ss"], m["Wm_sv"], m["Wm_vs"], m["Wm_vv"])
    update("w3", m["Wu_ss"], m["Wu_sv"], m["Wu_vs"], m["Wu_vv"], m["Lu_s"], m["Lu_v"])



def _blocks(rows, cols, blocks):
    import numpy as np
    m = np.zeros((rows, cols), np.float32)
    for r, c, b in blocks:
        m[r:r + b.shape[0], c:c + b.shape[1]] = b
    return m


def _per_component(r, c, b, dr=None, dc=None):
    return [(r + k * (dr or b.shape[0]), c + k * (dc or b.shape[1]), b) for k in range(3)]


def layout(inputs):
    import numpy as np
    f = {k: np.asarray(v) for k, v in inputs.items()}

    def rows(a, n):
        out = np.zeros((n,) + a.shape[1:], a.dtype)
        out[:a.shape[0]] = a
        return out

    x = f["x"]
    node = np.zeros((NP, D), np.float32)
    node[:N, :CS] = x[:, :CS]
    node[:N, CS:] = x[:, CS:].reshape(N, CV, 3).transpose(0, 2, 1).reshape(N, 3 * CV)
    a = {"x": node}
    for key in ("src", "dst"):
        k = np.full((EP,), N, np.int32)
        k[:E] = f[key]
        a[key + "_row"] = k.reshape(P, NT)
        a[key + "_col"] = k.reshape(NT, P).T

    def edges(name, width):
        e = np.ones((EP, width), np.float32)
        e[:E] = f[name]
        return e
    a["attr3"] = edges("edge_attr_3", 3).reshape(NT, P, 3).transpose(1, 0, 2)
    a["attr4"] = edges("edge_attr_4", 4).reshape(NT, P, 4).transpose(1, 0, 2)
    a["attr4_10"] = edges("edge_attr_4", 4)[:, [0, 1, 2, 3, 3, 1, 2, 2, 3, 1]]
    a["attr64_T"] = edges("edge_attr_64", 64).T
    a["attr16_T"] = edges("edge_attr_16", 16).T
    g = {k[7:]: v for k, v in f.items() if k.startswith("L0_gnn_")}
    a["w0_nl"] = _blocks(256, D, [(0, 0, g["W_nl0"])] + _per_component(64, 64, g["W_nl1"]))
    a["w0_fc1"], a["w0_fc2"] = _blocks(64, P, [(0, 0, g["W_fc1"])]), g["W_fc2"]
    wv, ws = g["W_out_v"], g["W_out_s"]
    a["w0_agg"] = _blocks(512, 192, _per_component(0, 96, wv[:64]) + _per_component(192, 96, wv[96:])
                          + [(288, 0, ws[64:]), (320, 0, ws[:64])] + _per_component(384, 96, wv[64:96]))
    a["w0_skip"] = _blocks(256, 192, [(0, 0, g["W_skip0"])] + _per_component(64, 96, g["W_skip1"]))
    g = {k[7:]: v for k, v in f.items() if k.startswith("L1_gnn_")}
    a["w1_tab"] = _blocks(256, 2 * D, [(0, 0, g["Ws_src"]), (0, D, g["Ws_dst"])]
                          + _per_component(64, 64, g["Wv_src"]) + _per_component(64, D + 64, g["Wv_dst"]))
    a["gamma1"] = np.concatenate([g["gamma_s"]] + 3 * [g["gamma_v"]])
    a["beta1"] = g["beta_s"]
    layout_rest(a, f, g)
    return {k: np.ascontiguousarray(v) for k, v in a.items()}


def kernel(**inputs):
    import numpy as np
    import concourse.bacc as bacc
    from concourse.bass_utils import run_bass_kernel_spmd as run

    arrays = layout(inputs)
    nc = bacc.Bacc("TRN2", target_bir_lowering=False, num_devices=1)
    A = {k: nc.dram_tensor(f"in_{k}", a.shape, mybir.dt.from_np(a.dtype), kind="ExternalInput").ap() for k, a in arrays.items()}
    out = nc.dram_tensor("out_x", (NP, D), F32, kind="ExternalOutput").ap()
    build(nc, A, out)
    r = run(nc, [{f"in_{k}": a for k, a in arrays.items()}], core_ids=[0])
    got = np.asarray(r.results[0]["out_x"])[:N]
    return np.concatenate([got[:, :CS], got[:, CS:].reshape(N, 3, CV).transpose(0, 2, 1).reshape(N, 3 * CV)], axis=1)
```
